# Optimizing a Trainium2 kernel written in Bass

```python
import numpy as np
import jax
import jax.numpy as jnp

def _softmax(x, axis=-1):
    return jax.nn.softmax(x, axis=axis)

def _gelu(x):
    return jax.nn.gelu(x, approximate=True)

def _silu(x):
    return jax.nn.silu(x)

def _sigmoid(x):
    return jax.nn.sigmoid(x)

def _layernorm(x, axis=-1, eps=1e-05):
    m = jnp.mean(x, axis=axis, keepdims=True)
    v = jnp.var(x, axis=axis, keepdims=True)
    return (x - m) / jnp.sqrt(v + eps)

def _scatter_add(tgt, idx, src, axis=0):
    return tgt.at[idx].add(src)

def _segment_sum(src, seg, n):
    return jax.ops.segment_sum(src, seg, n)
kernel_name = 'mk_recurrent_d2_jaxref_r4_94083c'

def setup_inputs(seed: int=0):
    np.random.seed(seed)
    _w = jnp.asarray

    def _L0_attn_setup():
        import jax, jax.numpy as jnp
        import numpy as np
        import math
        INPUT_WIDTH = 256
        KEY_WIDTH = 64
        VALUE_WIDTH = 64
        NUM_HEADS = 16
        NUM_GROUPS = 4
        HEADS_PER_GROUP = NUM_HEADS // NUM_GROUPS
        key = jax.random.key(seed)
        k_x, k_q, k_k, k_v, k_p = jax.random.split(key, 5)
        n, s = (2, 512)

        def lin(k, fan_in, fan_out):
            bound = 1.0 / math.sqrt(fan_in)
            return jax.random.uniform(k, (fan_in, fan_out), minval=-bound, maxval=bound, dtype=jnp.float32)
        return {'X': jax.random.normal(k_x, (n, s, INPUT_WIDTH), dtype=jnp.float32), 'Wq': lin(k_q, INPUT_WIDTH, NUM_HEADS * KEY_WIDTH), 'Wk': lin(k_k, INPUT_WIDTH, NUM_GROUPS * KEY_WIDTH), 'Wv': lin(k_v, INPUT_WIDTH, NUM_GROUPS * VALUE_WIDTH), 'Wpost': lin(k_p, NUM_HEADS * VALUE_WIDTH, INPUT_WIDTH)}
    _L0_attn_in = _L0_attn_setup()

    def _L0_ffn_setup():
        import jax, jax.numpy as jnp
        import numpy as np
        B, S, H, I = (2, 512, 256, 128)
        E, K, G, TG = (64, 8, 8, 4)
        SCALE = 2.5
        CAP = 256
        key = jax.random.key(seed)
        ks = jax.random.split(key, 6)
        hidden_states = jax.random.normal(ks[0], (B, S, H), jnp.float32)
        gate_w = jax.random.normal(ks[1], (E, H), jnp.float32) * 0.02
        gate_bias = jax.random.normal(ks[2], (E,), jnp.float32) * 0.02
        w_gate = jax.random.normal(ks[3], (E, H, I), jnp.float32) * (1.0 / np.sqrt(H))
        w_up = jax.random.normal(ks[4], (E, H, I), jnp.float32) * (1.0 / np.sqrt(H))
        w_down = jax.random.normal(ks[5], (E, I, H), jnp.float32) * (1.0 / np.sqrt(I))
        return {'hidden_states': hidden_states, 'gate_w': gate_w, 'gate_bias': gate_bias, 'w_gate': w_gate, 'w_up': w_up, 'w_down': w_down}
    _L0_ffn_in = _L0_ffn_setup()

    def _L1_attn_setup():
        import jax, jax.numpy as jnp
        import numpy as np
        from jax import lax
        D_MODEL = 256
        D_INNER = 512
        D_STATE = 16
        D_CONV = 4
        DT_RANK = 64
        B, L = (2, 512)
        LN_EPS = 1e-05

        def _layernorm(x, g, b):
            mu = jnp.mean(x, axis=-1, keepdims=True)
            var = jnp.mean(jnp.square(x - mu), axis=-1, keepdims=True)
            return (x - mu) * lax.rsqrt(var + LN_EPS) * g + b

        def _selective_scan(x_h, dt, Bm, Cm, A):
            b = x_h.shape[0]
            xs = (jnp.swapaxes(x_h, 0, 1), jnp.swapaxes(dt, 0, 1), jnp.swapaxes(Bm, 0, 1), jnp.swapaxes(Cm, 0, 1))
            h0 = jnp.zeros((b, D_INNER, D_STATE), x_h.dtype)

            def step(ht, inp):
                x_t, dt_t, B_t, C_t = inp
                dA = jnp.exp(dt_t[..., None] * A)
                dB = dt_t[..., None] * B_t[:, None, :]
                ht = dA * ht + dB * x_t[..., None]
                y_t = jnp.sum(ht * C_t[:, None, :], axis=-1)
                return (ht, y_t)
            _, ys = lax.scan(step, h0, xs)
            return jnp.swapaxes(ys, 0, 1)
        key = jax.random.key(seed)
        ks = jax.random.split(key, 10)
        s = 0.02
        x = jax.random.normal(ks[0], (B, L, D_MODEL), dtype=jnp.float32)
        ln_g = jnp.ones((D_MODEL,), jnp.float32)
        ln_b = jnp.zeros((D_MODEL,), jnp.float32)
        W_in = jax.random.normal(ks[1], (2 * D_INNER, D_MODEL)) * s
        W_x = jax.random.normal(ks[2], (DT_RANK + 2 * D_STATE, D_INNER)) * s
        W_dt = jax.random.normal(ks[3], (D_INNER, DT_RANK)) * s
        b_dt = jax.random.normal(ks[4], (D_INNER,)) * s
        W_out = jax.random.normal(ks[5], (D_MODEL, D_INNER)) * s
        conv_w = jax.random.normal(ks[6], (D_INNER, 1, D_CONV)) * s
        conv_b = jnp.zeros((D_INNER,), jnp.float32)
        A_log = jnp.log(jnp.tile(jnp.arange(1, D_STATE + 1, dtype=jnp.float32), (D_INNER, 1)))
        D_param = jnp.ones((D_INNER,), jnp.float32)
        alpha = jnp.full((1,), 0.5, jnp.float32)
        return dict(x=x, ln_g=ln_g, ln_b=ln_b, W_in=W_in, W_x=W_x, W_dt=W_dt, b_dt=b_dt, W_out=W_out, conv_w=conv_w, conv_b=conv_b, A_log=A_log, D_param=D_param, alpha=alpha)
    _L1_attn_in = _L1_attn_setup()

    def _L1_ffn_setup():
        import jax, jax.numpy as jnp
        import numpy as np
        DIM = 256
        DEPTH = 7
        PAR = 8
        N_NODES = 2 ** (DEPTH + 1) - 1
        WIDTH = PAR * N_NODES
        key = jax.random.key(seed)
        k1, k2, k3, k4 = jax.random.split(key, 4)
        init_k = float(np.sqrt(1.0 / DIM))
        init_k2 = float(np.sqrt(1.0 / ((DEPTH + 1) * PAR)))
        oldx = jax.random.normal(k1, (4, 512, DIM), dtype=jnp.float32)
        W_in = jax.random.uniform(k2, (WIDTH, DIM), jnp.float32, -init_k, init_k)
        b_in = jax.random.uniform(k3, (WIDTH,), jnp.float32, -init_k, init_k)
        W_out = jax.random.uniform(k4, (DIM, WIDTH), jnp.float32, -init_k2, init_k2)
        return {'oldx': oldx, 'W_in': W_in, 'b_in': b_in, 'W_out': W_out}
    _L1_ffn_in = _L1_ffn_setup()
    _d = {'L0_attn_X': _L0_attn_in['X'], 'L0_attn_Wq': _L0_attn_in['Wq'], 'L0_attn_Wk': _L0_attn_in['Wk'], 'L0_attn_Wv': _L0_attn_in['Wv'], 'L0_attn_Wpost': _L0_attn_in['Wpost'], 'L0_ffn_gate_w': _L0_ffn_in['gate_w'], 'L0_ffn_gate_bias': _L0_ffn_in['gate_bias'], 'L0_ffn_w_gate': _L0_ffn_in['w_gate'], 'L0_ffn_w_up': _L0_ffn_in['w_up'], 'L0_ffn_w_down': _L0_ffn_in['w_down'], 'L1_attn_ln_g': _L1_attn_in['ln_g'], 'L1_attn_ln_b': _L1_attn_in['ln_b'], 'L1_attn_W_in': _L1_attn_in['W_in'], 'L1_attn_W_x': _L1_attn_in['W_x'], 'L1_attn_W_dt': _L1_attn_in['W_dt'], 'L1_attn_b_dt': _L1_attn_in['b_dt'], 'L1_attn_W_out': _L1_attn_in['W_out'], 'L1_attn_conv_w': _L1_attn_in['conv_w'], 'L1_attn_conv_b': _L1_attn_in['conv_b'], 'L1_attn_A_log': _L1_attn_in['A_log'], 'L1_attn_D_param': _L1_attn_in['D_param'], 'L1_attn_alpha': _L1_attn_in['alpha'], 'L1_ffn_W_in': _L1_ffn_in['W_in'], 'L1_ffn_b_in': _L1_ffn_in['b_in'], 'L1_ffn_W_out': _L1_ffn_in['W_out']}
    _x0 = _d['L0_attn_X']
    _d['L0_attn_X'] = jax.random.normal(jax.random.fold_in(jax.random.key(seed), 1), (8, 512, 256), dtype=_x0.dtype)
    del _x0
    return _d

def reference(L0_attn_X, L0_attn_Wq, L0_attn_Wk, L0_attn_Wv, L0_attn_Wpost, L0_ffn_gate_w, L0_ffn_gate_bias, L0_ffn_w_gate, L0_ffn_w_up, L0_ffn_w_down, L1_attn_ln_g, L1_attn_ln_b, L1_attn_W_in, L1_attn_W_x, L1_attn_W_dt, L1_attn_b_dt, L1_attn_W_out, L1_attn_conv_w, L1_attn_conv_b, L1_attn_A_log, L1_attn_D_param, L1_attn_alpha, L1_ffn_W_in, L1_ffn_b_in, L1_ffn_W_out):

    def _L0_attn_ref(X, Wq, Wk, Wv, Wpost):
        import jax, jax.numpy as jnp
        import numpy as np
        import math
        INPUT_WIDTH = 256
        KEY_WIDTH = 64
        VALUE_WIDTH = 64
        NUM_HEADS = 16
        NUM_GROUPS = 4
        HEADS_PER_GROUP = NUM_HEADS // NUM_GROUPS
        n, s, _ = X.shape
        Q = (X @ Wq).reshape(n, s, NUM_GROUPS, HEADS_PER_GROUP, KEY_WIDTH)
        K = (X @ Wk).reshape(n, s, NUM_GROUPS, KEY_WIDTH)
        V = (X @ Wv).reshape(n, s, NUM_GROUPS, VALUE_WIDTH)
        scale = 1.0 / math.sqrt(KEY_WIDTH)
        raw = jnp.einsum('bsgwe,btge->bstgw', Q, K * scale)
        attn = jax.nn.softmax(raw, axis=2)
        A = jnp.einsum('bstgw,btge->bsgwe', attn, V).reshape(n, s, NUM_HEADS * VALUE_WIDTH)
        P = A @ Wpost
        return X + P

    def _L0_ffn_ref(hidden_states, gate_w, gate_bias, w_gate, w_up, w_down):
        import jax, jax.numpy as jnp
        import numpy as np
        B, S, H, I = (2, 512, 256, 128)
        E, K, G, TG = (64, 8, 8, 4)
        SCALE = 2.5
        CAP = 256
        b, s, h = hidden_states.shape
        x = hidden_states.reshape(-1, h)
        n = x.shape[0]
        logits = x.astype(jnp.float32) @ gate_w.astype(jnp.float32).T
        scores = jax.nn.sigmoid(logits)
        sfc = scores + gate_bias[None, :]
        group_scores = jax.lax.top_k(sfc.reshape(n, G, E // G), 2)[0].sum(-1)
        gidx = jax.lax.top_k(group_scores, TG)[1]
        gmask = jnp.zeros((n, G), bool).at[jnp.arange(n)[:, None], gidx].set(True)
        smask = jnp.repeat(gmask, E // G, axis=1)
        tmp = jnp.where(smask, sfc, -jnp.inf)
        topk_idx = jax.lax.top_k(tmp, K)[1]
        topk_w = jnp.take_along_axis(scores, topk_idx, axis=1)
        topk_w = topk_w / (topk_w.sum(-1, keepdims=True) + 1e-20)
        topk_w = topk_w * SCALE
        e = topk_idx.reshape(-1)
        token = jnp.repeat(jnp.arange(n), K)
        oh = jax.nn.one_hot(e, E, dtype=jnp.int32)
        pos = jnp.take_along_axis(jnp.cumsum(oh, 0) - 1, e[:, None], 1)[:, 0]
        valid = pos < CAP
        pos_c = jnp.where(valid, pos, CAP)
        buf = jnp.zeros((E, CAP + 1, h), x.dtype).at[e, pos_c].set(x[token])[:, :CAP]
        g = jnp.einsum('ech,ehi->eci', buf, w_gate)
        u = jnp.einsum('ech,ehi->eci', buf, w_up)
        y = jnp.einsum('eci,eih->ech', jax.nn.silu(g) * u, w_down)
        y_slots = y[e, jnp.minimum(pos, CAP - 1)]
        w_slot = topk_w.reshape(-1) * valid.astype(topk_w.dtype)
        out = jnp.zeros((n, h), jnp.float32).at[token].add(y_slots * w_slot[:, None])
        return out.reshape(b, s, h)

    def _L1_attn_ref(x, ln_g, ln_b, W_in, W_x, W_dt, b_dt, W_out, conv_w, conv_b, A_log, D_param, alpha):
        import jax, jax.numpy as jnp
        import numpy as np
        from jax import lax
        D_MODEL = 256
        D_INNER = 512
        D_STATE = 16
        D_CONV = 4
        DT_RANK = 64
        B, L = (2, 512)
        LN_EPS = 1e-05

        def _layernorm(x, g, b):
            mu = jnp.mean(x, axis=-1, keepdims=True)
            var = jnp.mean(jnp.square(x - mu), axis=-1, keepdims=True)
            return (x - mu) * lax.rsqrt(var + LN_EPS) * g + b

        def _selective_scan(x_h, dt, Bm, Cm, A):
            b = x_h.shape[0]
            xs = (jnp.swapaxes(x_h, 0, 1), jnp.swapaxes(dt, 0, 1), jnp.swapaxes(Bm, 0, 1), jnp.swapaxes(Cm, 0, 1))
            h0 = jnp.zeros((b, D_INNER, D_STATE), x_h.dtype)

            def step(ht, inp):
                x_t, dt_t, B_t, C_t = inp
                dA = jnp.exp(dt_t[..., None] * A)
                dB = dt_t[..., None] * B_t[:, None, :]
                ht = dA * ht + dB * x_t[..., None]
                y_t = jnp.sum(ht * C_t[:, None, :], axis=-1)
                return (ht, y_t)
            _, ys = lax.scan(step, h0, xs)
            return jnp.swapaxes(ys, 0, 1)
        residual = x
        h = _layernorm(x, ln_g, ln_b)
        x_and_res = h @ W_in.T
        x_h, res = jnp.split(x_and_res, [D_INNER], axis=-1)
        xc = jnp.swapaxes(x_h, 1, 2)
        xc = lax.conv_general_dilated(xc, conv_w, window_strides=(1,), padding=[(D_CONV - 1, 0)], dimension_numbers=('NCH', 'OIH', 'NCH'), feature_group_count=D_INNER)
        xc = xc + conv_b[None, :, None]
        x_h = jax.nn.silu(jnp.swapaxes(xc, 1, 2))
        x_dbl = x_h @ W_x.T
        dt, Bm, Cm = jnp.split(x_dbl, [DT_RANK, DT_RANK + D_STATE], axis=-1)
        dt = jax.nn.softplus(dt @ W_dt.T + b_dt)
        A = -jnp.exp(A_log)
        y = _selective_scan(x_h, dt, Bm, Cm, A) + x_h * D_param
        y = y * jax.nn.silu(res)
        out = y @ W_out.T
        return residual + alpha * out

    def _L1_ffn_ref(oldx, W_in, b_in, W_out):
        import jax, jax.numpy as jnp
        import numpy as np
        DIM = 256
        DEPTH = 7
        PAR = 8
        N_NODES = 2 ** (DEPTH + 1) - 1
        WIDTH = PAR * N_NODES
        x = oldx.reshape(-1, DIM)
        B = x.shape[0]
        logits = x @ W_in.T + b_in
        decisions = (logits > 0).astype(jnp.int32).reshape(B, PAR, N_NODES)
        acts = jax.nn.silu(logits).reshape(B, PAR, N_NODES)
        current = jnp.zeros((B, PAR), dtype=jnp.int32)
        dmap = jax.nn.one_hot(current, N_NODES, dtype=acts.dtype)
        for d in range(DEPTH):
            cur_platform = 2 ** d - 1
            next_platform = 2 ** (d + 1) - 1
            moves = jnp.take_along_axis(decisions, current[..., None], axis=2)[..., 0]
            current = (current - cur_platform) * 2 + moves + next_platform
            dmap = dmap + jax.nn.one_hot(current, N_NODES, dtype=acts.dtype)
        masked = acts * jax.lax.stop_gradient(dmap)
        out = masked.reshape(B, WIDTH) @ W_out.T
        return out.reshape(oldx.shape)
    x = L0_attn_X
    xn = _layernorm(x, axis=-1)
    s = _L0_attn_ref(xn, L0_attn_Wq, L0_attn_Wk, L0_attn_Wv, L0_attn_Wpost)
    g = _silu(_L0_ffn_ref(xn, L0_ffn_gate_w, L0_ffn_gate_bias, L0_ffn_w_gate, L0_ffn_w_up, L0_ffn_w_down))
    x = x + s * g
    xn = _layernorm(x, axis=-1)
    s = _L1_attn_ref(xn, L1_attn_ln_g, L1_attn_ln_b, L1_attn_W_in, L1_attn_W_x, L1_attn_W_dt, L1_attn_b_dt, L1_attn_W_out, L1_attn_conv_w, L1_attn_conv_b, L1_attn_A_log, L1_attn_D_param, L1_attn_alpha)
    g = _silu(_L1_ffn_ref(xn, L1_ffn_W_in, L1_ffn_b_in, L1_ffn_W_out))
    x = x + s * g
    return x

_drawn_inputs = setup_inputs


def setup_inputs(seed=0):
    import zlib

    import numpy as np

    out = dict(_drawn_inputs(seed))
    spreads = {'L1_attn_ln_g': (1.0, 0.6),
     'L1_attn_ln_b': (0.0, 0.8),
     'L1_attn_conv_b': (0.0, 0.8),
     'L1_attn_D_param': (1.0, 0.6)}
    factors = {'L0_attn_Wq': 8.0,
     'L0_attn_Wk': 8.0,
     'L0_attn_Wv': 8.0,
     'L0_attn_Wpost': 7.719,
     'L1_attn_W_in': 8.0,
     'L1_attn_W_x': 8.0,
     'L1_attn_W_dt': 8.0,
     'L1_attn_b_dt': 8.0,
     'L1_attn_W_out': 8.0,
     'L1_attn_conv_w': 8.0,
     'L1_attn_A_log': 8.0}
    for name, (base, spread) in spreads.items():
        noise = np.random.default_rng([zlib.crc32(name.encode()), seed]).standard_normal(out[name].shape)
        drawn = base * np.exp(spread * noise) if base else spread * noise
        out[name] = jnp.asarray(drawn.astype(out[name].dtype))
    for name, factor in factors.items():
        out[name] = (out[name] * factor).astype(out[name].dtype)
    return out
```

```python
import concourse.bass as bass
from concourse import mybir
from contextlib import ExitStack
import numpy as np

NB, SEQ, DM = 8, 512, 256
P = 128
TILES = SEQ // P
NT = NB * TILES
KC = DM // P
HEADS, GROUPS, HD = 16, 4, 64
HPG = HEADS // GROUPS
EXPERTS, EG, TOPG, TOPK, EI, CAP = 64, 8, 4, 8, 128, 256
EPG = EXPERTS // EG
SLOTS = EXPERTS * CAP
ROUTE_SCALE = 2.5
DI, DS, DTR, DCONV = 512, 16, 64, 4
CB = DI // P
TREES, DEPTH = 8, 7
NODES = 2 ** (DEPTH + 1) - 1
INNER = 2 ** DEPTH - 1
HALF_STATES = DS // 2
EPS = 1e-5
RING_Q = 3
RING_ROWS = 4
BIG = 3.0e38
GONE = 65536.0


def build_program(nc, X, Wq, Wk, Wv, Wpost, gateT, gate_bias, w_gate, w_up, w_down, ln_gb, WinT, WxT, WdtT,
                  WoutT, chan, A_log, alpha, ffn_WinT, ffn_b, ffn_WoutT, path, need, tri, glt, slot_base, out):
    fp32, f32r, bf16 = mybir.dt.float32, mybir.dt.float32r, mybir.dt.bfloat16
    i32 = mybir.dt.int32
    ALU, ACT, AX = mybir.AluOpType, mybir.ActivationFunctionType, mybir.AxisListType

    ctx = ExitStack()
    queues = {n: [] for n in ("pe", "act", "dve", "pool", "sp")}
    sems, counts = {}, {}

    def semaphore(name):
        if name not in sems:
            sems[name] = ctx.enter_context(nc.semaphore(name))
            counts[name] = 0
        return sems[name]

    def do(engine, emit, after=(), signal=None, by=1):
        target = semaphore(signal) if signal else None
        queues[engine].append((emit, [a for a in after if a is not None], target, by))
        if signal:
            counts[signal] += by
            return (signal, counts[signal])
        return None

    def pe(emit, after=(), signal=None):
        return do("pe", emit, after, signal)

    def act(emit, after=(), signal=None):
        return do("act", emit, after, signal)

    def dve(emit, after=(), signal=None):
        return do("dve", emit, after, signal)

    def pool(emit, after=(), signal=None):
        return do("pool", emit, after, signal)

    def load(dst, src, signal, after=(), queue="sp"):
        return do(queue, lambda e: e.dma_start(dst, src), after, signal, 16)

    def run_queue(name, engine):
        reached = {}
        for emit, after, target, by in queues[name]:
            for sem, value in after:
                if reached.get(sem, 0) < value:
                    engine.wait_ge(sems[sem], value)
                    reached[sem] = value
            ins = emit(engine)
            if target is not None:
                ins.then_inc(target, by)

    def sb(name, shape, dt=fp32):
        return ctx.enter_context(nc.sbuf_tensor(name, shape, dt))

    xbuf = nc.dram_tensor("xbuf", [SLOTS, DM], fp32, kind="Internal").ap()
    ybuf = nc.dram_tensor("ybuf", [SLOTS, DM], fp32, kind="Internal").ap()
    bc_dram = nc.dram_tensor("bc_dram", [NB, 2 * DS, SEQ], fp32, kind="Internal").ap()

    ident = sb("ident", [P, P])
    tri_sb, ones_sb = sb("tri_sb", [P, P], bf16), sb("ones_sb", [P, P], bf16)
    path_sb = sb("path_sb", [P, 2 * P], bf16)
    need_sb = sb("need_sb", [P, 2])
    ffn_b_sb = sb("ffn_b_sb", [P, 2 * TREES])
    ln_gb_sb = sb("ln_gb_sb", [P, 2, KC])
    chan_sb = sb("chan_sb", [P, CB, DCONV + 3])
    A_sb = sb("A_sb", [P, CB, DS])
    alpha_sb = sb("alpha_sb", [P, 1])
    mhalf = sb("mhalf", [P, 1])
    Wq_sb = sb("Wq_sb", [P, KC, HEADS * HD])
    Wk_sb = sb("Wk_sb", [P, KC, GROUPS * 2 * HD])
    Wv_sb = sb("Wv_sb", [P, KC, GROUPS * HD])
    Wpost_sb = sb("Wpost_sb", [P, HEADS // 2, DM])
    WinT_sb = sb("WinT_sb", [P, KC, 2 * DI])
    WxT_sb = sb("WxT_sb", [P, CB, DTR + 2 * DS])
    WdtT_sb = sb("WdtT_sb", [DTR, DI])
    WoutT_sb = sb("WoutT_sb", [P, CB, DM])
    stats0 = sb("stats0", [P, NT, 2])
    slot_idx = sb("slot_idx", [P, NT, TOPK], i32)
    slot_w = sb("slot_w", [P, NT, TOPK])
    xa = sb("xa", [P, TILES, DM])
    xaT = sb("xaT", [P, KC, SEQ])
    Kst = sb("Kst", [P, 2, 2, SEQ], f32r)
    Qst = sb("Qst", [P, RING_Q, SEQ], f32r)
    V_sb = sb("V_sb", [P, TILES, GROUPS * HD])
    Pr = sb("Pr", [P, 3, SEQ])
    PT = sb("PT", [P, 3, TILES, P])
    AT = sb("AT", [P, HEADS // 2, SEQ])
    negmax, rowsum, rowinv = sb("negmax", [P, 4]), sb("rowsum", [P, 4]), sb("rowinv", [P, 4])
    s_sb = sb("s_sb", [P, 2, TILES, DM])
    rows_sb = sb("rows_sb", [P, RING_ROWS, DM])
    acc_sb = sb("acc_sb", [P, DM])
    gate_sb = sb("gate_sb", [P, DM])
    x1 = sb("x1", [P, 2, TILES, DM])
    xn1 = sb("xn1", [P, TILES, DM])
    bst, bag = sb("bst", [P, TILES, 6]), sb("bag", [P, TILES, 2])
    rst = sb("rst", [P, TILES])
    g1 = sb("g1", [P, 2, TILES, DM])
    wr_in = V_sb[:, 0:2, :].rearrange("p a (b c) -> p a b c", c=P)
    wr_out = V_sb[:, 2:4, :]
    arena = sb("arena", [P, 18944])
    view = {}
    at = [0]

    def part(name, *dims, base=None):
        n = int(np.prod(dims))
        if base is not None:
            at[0] = base
        v = arena[:, at[0]:at[0] + n]
        if len(dims) == 2:
            v = v.rearrange("p (a b) -> p a b", b=dims[1])
        elif len(dims) == 3:
            v = v.rearrange("p (a b c) -> p a b c", b=dims[1], c=dims[2])
        at[0] += n
        view[name] = v
        assert at[0] <= 18944, (name, at[0])
        return v

    hT = part("hT", KC, SEQ, base=0)
    dt_sb, u_sb, y_sb = part("dt", CB, SEQ), part("u", CB, SEQ), part("y", CB, SEQ)
    res_sb = part("res", SEQ)
    BC = part("BC", HALF_STATES, 2, SEQ)
    dA, dBu, hst = part("dA", 2, SEQ), part("dBu", 2, SEQ), part("hst", 2, SEQ)
    xs = BC.rearrange("p a b s -> p (a b) s")[:, 0:CB, :]
    xd = BC.rearrange("p a b s -> p (a b) s")[:, CB, :]
    sp_a = dA[:, :, :]
    xn_all = part("xn_all", NT, DM, base=0)
    RT = [part(f"route{i}", NT, EXPERTS) for i in range(5)]
    xe = part("xe", 2, 2, DM * 1, base=NT * DM)
    xeT = part("xeT", 2, KC, CAP)
    we = part("we", 2, 3, 2 * P)
    sg = part("sg", 2, CAP)
    he = part("he", 2, CAP)
    ye = part("ye", 2, 2, DM)
    route0_end = NT * DM + 5 * NT * EXPERTS
    gw_sb = arena[:, route0_end:route0_end + KC * EXPERTS].rearrange("p (a b) -> p a b", b=EXPERTS)
    bias_sb = arena[:, route0_end + 128:route0_end + 192]
    base_sb = arena[:, route0_end + 192:route0_end + 256]
    glt_sb = arena[:, route0_end + 256:route0_end + 320].rearrange("p (a b) -> p a b", b=EG)
    assert route0_end + 320 <= 18944
    act_sb = Pr
    masked = PT.rearrange("p a b c -> p a (b c)")
    dec_sb = sb("dec_sb", [P, 2, SEQ], bf16)
    xT1 = AT[:, 0:KC, :]
    oT = AT[:, KC:2 * KC, :]
    zt = AT[:, 4:6, :].rearrange("p a (b c) -> p (a b) c", c=DM)

    bank = [ctx.enter_context(nc.psum_tensor(f"bank{i}", [P, SEQ], fp32)) for i in range(8)]
    bank_free = [None] * 8

    def broadcast(src, n):
        return bass.AP(src.tensor, src.offset, [[0, P], [1, n]])

    w_first = load(gw_sb, gateT.rearrange("(c p) e -> p c e", p=P), "w_first")
    for dst, src in ((bias_sb, broadcast(gate_bias, EXPERTS)), (base_sb, broadcast(slot_base, EXPERTS)),
                     (glt_sb.rearrange("p a b -> p (a b)"), broadcast(glt, EG * EG))):
        w_first = load(dst, src, "w_first")
    stage = AT.rearrange("p a b -> p (a b)")
    w_small = load(stage[:, 0:P], tri, "w_small")
    for dst, src in ((stage[0:INNER, P:3 * P], path), (need_sb[:, :], need), (ffn_b_sb[:, :], ffn_b),
                     (ln_gb_sb[:, :, :], ln_gb), (chan_sb[:, :, :], chan), (A_sb[:, :, :], A_log),
                     (alpha_sb[:, :], broadcast(alpha, 1))):
        w_small = load(dst, src, "w_small")
    w_att = None
    for c in range(KC):
        for half in range(2):
            dst = Wk_sb[:, c, :].rearrange("p (g t d) -> p g t d", t=2, d=HD)[:, :, half, :]
            w_att = load(dst, Wk[c * P:(c + 1) * P, :].rearrange("p (g d) -> p g d", d=HD), "w_att", queue="act")
    for dst, src in ((Wq_sb, Wq), (Wv_sb, Wv), (Wpost_sb, Wpost)):
        w_att = load(dst[:, :, :], src.rearrange("(c p) n -> p c n", p=P), "w_att", queue="act")

    k0 = pool(lambda e: e.memset(ident[:, :], 0.0), signal="pool_const")
    ident_ok = pool(lambda e: e.affine_select(out=ident[:, :], in_=ident[:, :], compare_op=ALU.not_equal, fill=1.0, base=0,
                                              pattern=[[-1, P]], channel_multiplier=1), [k0], "pool_const")
    k1 = pool(lambda e: e.memset(ones_sb[:, :], 1.0), signal="pool_const")
    const_ok = pool(lambda e: e.memset(mhalf[:, :], -0.5), signal="pool_const")
    tri_ok = dve(lambda e: e.tensor_copy(tri_sb[:, :], stage[:, 0:P]), [w_small], "dve_const")
    path_ok = dve(lambda e: e.tensor_copy(path_sb[0:INNER, :], stage[0:INNER, P:3 * P]), [w_small], "dve_const")
    a0 = act(lambda e: e.activation(A_sb[:, :, :], A_sb[:, :, :], ACT.Exp), [w_small], "act_const")
    A_ok = dve(lambda e: e.tensor_scalar(A_sb[:, :, :], A_sb[:, :, :], -1.0, None, ALU.mult), [a0], "dve_const")
    zero_ok = dve(lambda e: e.memset(RT[4][:, :, :], 0.0), signal="dve_const")
    zrows = RT[4].rearrange("p a b -> p (a b)")
    ROWS_Z = NT * EXPERTS // DM
    for i in range(SLOTS // (P * ROWS_Z)):
        zeroed = load(xbuf[i * P * ROWS_Z:(i + 1) * P * ROWS_Z, :].rearrange("(p r) d -> p (r d)", p=P), zrows, "zeroed", [zero_ok])

    def statistics(src, mean_of, inv_of, after, tag, last=[None]):
        t = None
        for i in range(TILES):
            t = dve(lambda e, i=i: e.bn_stats(bst[:, i, :], src[:, i, :]), list(after) + [last[0]], "dve_stats")
        for i in range(TILES):
            t = dve(lambda e, i=i: e.bn_aggr(bag[:, i, :], bst[:, i, :]), [t], "dve_stats")
        t = dve(lambda e: e.tensor_scalar(rst[:, :], bag[:, :, 1], EPS, None, ALU.add), [t], "dve_stats")
        m = dve(lambda e: e.tensor_copy(mean_of, bag[:, :, 0]), [t], "dve_stats")
        r = pool(lambda e: e.tensor_tensor(inv_of, rst[:, :], mhalf[:, 0:1].broadcast_to([P, TILES]), ALU.pow), [t, const_ok], "pool_rsqrt")
        last[0] = r
        return [m, r]

    def normalise(dst, src, mean_of, inv_of, after):
        for i in range(TILES):
            t = dve(lambda e, i=i: e.tensor_scalar(dst[:, i, :], src[:, i, :], mean_of[:, i:i + 1], inv_of[:, i:i + 1],
                                                   ALU.subtract, ALU.mult), after, "dve_norm")
        return t

    def transposed(src, after, banks):
        out_t = []
        for c in range(KC):
            for i in range(TILES):
                t = pe(lambda e, c=c, i=i: e.transpose(bank[banks[c]][:, i * P:(i + 1) * P], src[:, i, c * P:(c + 1) * P], ident[:, :]),
                       list(after) + [bank_free[banks[c]], ident_ok], "pe_transposed")
            out_t.append(t)
        return out_t

    scores, sfc = RT[0], RT[1]
    x_done = [None]
    xT_done = [None, None]
    xn_ready = []
    for b in range(NB):
        xin = xn_all[:, b * TILES:(b + 1) * TILES, :]
        xl = load(xin, X[b].rearrange("(t p) d -> p t d", p=P), f"x_in{b}")
        mean_v, inv_v = stats0[:, b * TILES:(b + 1) * TILES, 0], stats0[:, b * TILES:(b + 1) * TILES, 1]
        st = statistics(xin, mean_v, inv_v, [xl], "x")
        nrm = normalise(xin, xin, mean_v, inv_v, st)
        xn_ready.append(nrm)
        tr = transposed(xin, [nrm], (0 + 2 * (b % 2), 1 + 2 * (b % 2)))
        for c in range(KC):
            bk = c + 2 * (b % 2)
            cp = act(lambda e, c=c, bk=bk: e.copy(xaT[:, c, :], bank[bk][:, :]), [tr[c], xT_done[0]], "act_xT")
            bank_free[bk] = cp
        for i in range(TILES):
            for c in range(KC):
                t = pe(lambda e, i=i, c=c, b=b: e.matmul(bank[4 + b % 2][:, i * EXPERTS:(i + 1) * EXPERTS], xaT[:, c, i * P:(i + 1) * P],
                                                    gw_sb[:, c, :], start=(c == 0), stop=(c == KC - 1)),
                       [cp, w_first, bank_free[4 + b % 2]], "pe_logits")
        xT_done[0] = t
        sc_ok = act(lambda e, b=b: e.activation(scores[:, b * TILES:(b + 1) * TILES, :].rearrange("p a b -> p (a b)"),
                                                bank[4 + b % 2][:, 0:TILES * EXPERTS], ACT.Sigmoid), [t], "act_scores")
        bank_free[4 + b % 2] = sc_ok

    def wide(src, dims):
        return bass.AP(src.tensor, src.offset, [list(src.ap[0])] + [list(d) for d in dims])

    small = g1.rearrange("p a b c -> p (a b c)")[:, 0:6 * NT * EG].rearrange("p (a b) -> p a b", b=NT * EG)
    m1, m2, n1, gsum, gpen = (small[:, i, :] for i in range(5))
    G8 = "p a (g k) -> p (a g) k"
    R1, R2, R3 = RT[2], RT[3], RT[4]
    ch = [None]

    def step(emit, after=()):
        ch[0] = dve(emit, [ch[0]] + list(after), "dve_route")
        return ch[0]

    def routing():
        sfc4 = sfc.rearrange(G8, k=EPG)
        rs = sfc4.ap[0]
        es = 1
        step(lambda e: e.tensor_tensor(sfc[:, :, :], scores[:, :, :], wide(bias_sb, [[0, NT], [1, EXPERTS]]), ALU.add), [sc_ok, w_first])
        step(lambda e: e.tensor_reduce(m1, sfc4, AX.X, ALU.max))
        step(lambda e: e.tensor_tensor(R1.rearrange(G8, k=EPG), sfc4, wide(m1, [[1, NT * EG], [0, EPG]]), ALU.is_equal))
        step(lambda e: e.tensor_reduce(n1, R1.rearrange(G8, k=EPG), AX.X, ALU.add))
        step(lambda e: e.scalar_tensor_tensor(R1[:, :, :], R1[:, :, :], -BIG, sfc[:, :, :], ALU.mult, ALU.add))
        step(lambda e: e.tensor_reduce(m2, R1.rearrange(G8, k=EPG), AX.X, ALU.max))
        step(lambda e: e.tensor_scalar(n1, n1, 2.0, -BIG, ALU.is_lt, ALU.mult))
        step(lambda e: e.tensor_tensor(n1, n1, m1, ALU.add))
        step(lambda e: e.tensor_tensor(m2, m2, n1, ALU.max))
        step(lambda e: e.tensor_tensor(gsum, m1, m2, ALU.add))
        yield
        gj = wide(gsum, [[EG, NT], [0, EG], [1, EG]])
        gi = wide(gsum, [[EG, NT], [1, EG], [0, EG]])
        r4 = "p a (i j) -> p a i j"
        step(lambda e: e.tensor_tensor(R1.rearrange(r4, j=EG), gj, gi, ALU.is_equal))
        step(lambda e: e.tensor_tensor(R1[:, :, :], R1[:, :, :], wide(glt_sb, [[0, NT], [1, EG * EG]]), ALU.mult))
        step(lambda e: e.tensor_tensor(R2.rearrange(r4, j=EG), gj, gi, ALU.is_gt))
        step(lambda e: e.tensor_tensor(R1[:, :, :], R1[:, :, :], R2[:, :, :], ALU.add))
        step(lambda e: e.tensor_reduce(gpen, R1.rearrange("p a (i j) -> p (a i) j", j=EG), AX.X, ALU.add))
        step(lambda e: e.tensor_scalar(gpen, gpen, float(TOPG), -BIG, ALU.is_ge, ALU.mult))
        step(lambda e: e.tensor_tensor(sfc4, sfc4, wide(gpen, [[1, NT * EG], [0, EPG]]), ALU.add))
        yield
        K8 = small[:, 5, :].rearrange("p (a b) -> p a b", b=TOPK)
        for t in range(NT):
            step(lambda e, t=t: e.max(K8[:, t, :], sfc[:, t, :]))
        for t in range(NT):
            step(lambda e, t=t: e.match_replace(R1[:, t, :], K8[:, t, :], sfc[:, t, :], -3.4e38))
        sel_b = R3.rearrange("p a b -> p (a b)")[:, 0:NT * EXPERTS // 2].bitcast(bf16)
        sel3 = sel_b.rearrange("p (a b) -> p a b", b=EXPERTS)
        yield
        sel_ok = step(lambda e: e.tensor_tensor(sel3, R1[:, :, :], sfc[:, :, :], ALU.not_equal), [zeroed])
        step(lambda e: e.tensor_tensor(scores[:, :, :], scores[:, :, :], sel3, ALU.mult))
        den = small[:, 0, 0:NT]
        step(lambda e: e.tensor_reduce(den, scores[:, :, :], AX.X, ALU.add))
        step(lambda e: e.tensor_scalar(den, den, 1e-20, None, ALU.add))
        step(lambda e: e.reciprocal(den, den))
        step(lambda e: e.tensor_scalar(den, den, ROUTE_SCALE, None, ALU.mult))
        step(lambda e: e.tensor_tensor(scores[:, :, :], scores[:, :, :], wide(den, [[1, NT], [0, EXPERTS]]), ALU.mult))
        yield
        QT = SEQ // EXPERTS
        tot = sfc.rearrange("p a b -> p (a b)").rearrange("p (b a) -> p a b", a=NT)
        for q in range(NT // QT):
            for j, (w, ok) in enumerate(((tri_sb, tri_ok), (ones_sb, const_ok))):
                t = pe(lambda e, j=j, w=w, q=q: e.matmul(bank[6 + j][:, :], w[:, :], sel_b[:, q * SEQ:(q + 1) * SEQ], start=True, stop=True),
                       [sel_ok, ok, bank_free[6 + j]], "pe_positions")
                dst = (R1 if j == 0 else tot)[:, q * QT:(q + 1) * QT, :]
                bank_free[6 + j] = step(lambda e, j=j, dst=dst: e.tensor_copy(dst, bank[6 + j].rearrange("p (a b) -> p a b", b=EXPERTS)), [t])
        keep = R2.rearrange("p a b -> p (a b)")
        step(lambda e: e.memset(keep, 1.0))
        step(lambda e: e.memset(keep.rearrange("p (b a) -> p b a", a=NT)[:, :, 0:1], 0.0))
        run = RT[3]
        flat = "p a b -> p (a b)"
        pre = small_scan
        step(lambda e: e.tensor_tensor_scan(pre[:, :], keep, sfc.rearrange(flat), 0.0, ALU.mult, ALU.add))
        step(lambda e: e.tensor_tensor(pre[:, :], pre[:, :], sfc.rearrange(flat), ALU.subtract))
        step(lambda e: e.tensor_tensor(R1[:, :, :], R1[:, :, :], pre.rearrange("p (b a) -> p a b", a=NT), ALU.add))
        step(lambda e: e.scalar_tensor_tensor(R2[:, :, :], R1[:, :, :], float(CAP), sel3, ALU.is_lt, ALU.mult))
        step(lambda e: e.tensor_tensor(scores[:, :, :], scores[:, :, :], R2[:, :, :], ALU.mult))
        step(lambda e: e.tensor_tensor(R1[:, :, :], R1[:, :, :], wide(base_sb, [[0, NT], [1, EXPERTS]]), ALU.add))
        step(lambda e: e.tensor_tensor(R1[:, :, :], R1[:, :, :], R2[:, :, :], ALU.mult))
        for t in range(NT):
            step(lambda e, t=t: e.max(K8[:, t, :], R1[:, t, :]))
        yield
        idx = small[:, 0, :].rearrange("p (a b) -> p a b", b=TOPK)
        step(lambda e: e.tensor_scalar(idx, K8, 0.0, GONE, ALU.is_equal, ALU.mult))
        step(lambda e: e.scalar_tensor_tensor(idx, K8, -1.0, idx, ALU.add, ALU.add))
        idx_ok[0] = step(lambda e: e.tensor_copy(slot_idx[:, :, :], idx))
        yield
        for k in range(TOPK):
            step(lambda e, k=k: e.tensor_tensor(R2[:, :, :], R1[:, :, :], wide(K8[:, :, k:k + 1], [[TOPK, NT], [0, EXPERTS]]), ALU.is_equal))
            step(lambda e: e.tensor_tensor(R2[:, :, :], R2[:, :, :], scores[:, :, :], ALU.mult))
            w_ok[0] = step(lambda e, k=k: e.tensor_reduce(slot_w[:, :, k], R2[:, :, :], AX.X, ALU.add))
            yield

    small_scan = s_sb.rearrange("p a b c -> p (a b c)")[:, 0:NT * EXPERTS]
    idx_ok, w_ok = [None], [None]

    def scatter():
        for t in range(NT):
            for k in range(TOPK):
                scattered[0] = do("pool", lambda e, t=t, k=k: e.indirect_dma_start(
                    xbuf, bass.IndirectOffsetOnAxis(ap=slot_idx[:, t, k:k + 1], axis=0), xn_all[:, t, :], None,
                    bounds_check=SLOTS - 1, oob_is_err=False), [idx_ok[0], xn_ready[t // TILES], zeroed], "scattered", 16)
                if k % 4 == 3:
                    yield

    scattered = [None]

    s_ready, s_free = [None] * NB, [None] * 2
    att_free = [None]

    def attention(b):
        xl = load(xa[:, :, :], X[b].rearrange("(t p) d -> p t d", p=P), "x_att", [att_free[0], att_x[0]])
        mean_v, inv_v = stats0[:, b * TILES:(b + 1) * TILES, 0], stats0[:, b * TILES:(b + 1) * TILES, 1]
        nrm = normalise(xa, xa, mean_v, inv_v, [xl, xn_ready[b]])
        tr = transposed(xa, [nrm], (2, 3))
        for c in range(KC):
            xT = act(lambda e, c=c: e.copy(xaT[:, c, :], bank[2 + c][:, :]), [tr[c], xT_done[0], xT_done[1]], "act_xT")
            bank_free[2 + c] = xT
        yield
        for i in range(TILES):
            bk = 2 + i // 2
            for c in range(KC):
                t = pe(lambda e, i=i, c=c, bk=bk: e.matmul(bank[bk][:, (i % 2) * DM:(i % 2 + 1) * DM], xaT[:, c, i * P:(i + 1) * P],
                                                           Wv_sb[:, c, :], start=(c == 0), stop=(c == KC - 1)),
                       [xT, w_att, bank_free[bk]], "pe_proj")
            if i % 2:
                v_ok = act(lambda e, i=i, bk=bk: e.copy(V_sb[:, i - 1:i + 1, :].rearrange("p a b -> p (a b)"), bank[bk][:, :]),
                           [t, V_free[0]], "act_v")
                bank_free[bk] = v_ok
            yield
        q_ready, k_ready = {}, {}

        def project_k(g):
            bk = 2 + g % 2
            for c in range(KC):
                t = pe(lambda e, c=c: e.matmul(bank[bk][:, :], Wk_sb[:, c, g * P:(g + 1) * P], xaT[:, c, :], start=(c == 0), stop=(c == KC - 1)),
                       [xT, bank_free[bk]], "pe_proj")
            hi = act(lambda e: e.activation(Kst[:, g % 2, 0, :], bank[bk][:, :], ACT.Copy, scale=HD ** -0.5), [t, K_free[g % 2]], "act_k")
            lo = dve(lambda e: e.scalar_tensor_tensor(Kst[:, g % 2, 1, :], bank[bk][:, :], HD ** -0.5, Kst[:, g % 2, 0, :].bitcast(fp32),
                                                      ALU.mult, ALU.subtract), [hi, K_free[g % 2]], "dve_k")
            bank_free[bk] = lo
            k_ready[g] = lo

        def project_q(pair):
            bk = 2 + pair % 2
            for c in range(KC):
                t = pe(lambda e, c=c: e.matmul(bank[bk][:, :], Wq_sb[:, c, pair * P:(pair + 1) * P], xaT[:, c, :], start=(c == 0), stop=(c == KC - 1)),
                       [xT, bank_free[bk]], "pe_proj")
            for j in range(2):
                slot = (2 * pair + j) % RING_Q
                own, other = slice(j * HD, (j + 1) * HD), slice((1 - j) * HD, (2 - j) * HD)
                hi = act(lambda e, slot=slot, own=own: e.copy(Qst[own, slot, :], bank[bk][own, :]), [t, Q_free[slot]], "act_q")
                lo = dve(lambda e, slot=slot, own=own, other=other: e.tensor_tensor(
                    Qst[other, slot, :], bank[bk][own, :], Qst[own, slot, :].bitcast(fp32), ALU.subtract), [hi], "dve_q")
                q_ready[2 * pair + j] = lo
            bank_free[bk] = lo

        steps = [(h, i) for h in range(HEADS) for i in range(TILES)]
        p_ready, pt_ready = {}, {}
        av_last = {}
        project_k(0)
        yield
        project_q(0)
        yield
        LAG_T, LAG_AV = 2, 4
        for n in range(len(steps) + LAG_AV):
            if n < len(steps):
                h, i = steps[n]
                if i == 0 and h % 2 == 1 and h + 1 < HEADS:
                    if (h + 1) % HPG == 0:
                        project_k((h + 1) // HPG)
                    project_q((h + 1) // 2)
                g, slot, bk, r = h // HPG, h % RING_Q, n % 2, n % 3
                for part_ in range(2):
                    t = pe(lambda e, i=i, slot=slot, g=g, bk=bk, part_=part_: e.matmul(
                        bank[bk][:, :], Qst[:, slot, i * P:(i + 1) * P], Kst[:, g % 2, part_, :], start=(part_ == 0), stop=(part_ == 1)),
                        [q_ready[h], k_ready[g], bank_free[bk]], "pe_scores")
                if i == TILES - 1:
                    Q_free[slot] = t
                    if h % HPG == HPG - 1:
                        K_free[g % 2] = t
                q4 = n % 4
                mx = dve(lambda e, bk=bk, q4=q4: e.tensor_reduce(negmax[:, q4:q4 + 1], bank[bk][:, :], AX.X, ALU.max, negate=True), [t, stat_free[q4]], "dve_rowmax")
                ex = act(lambda e, bk=bk, q4=q4, r=r: e.activation(Pr[:, r, :], bank[bk][:, :], ACT.Exp, bias=negmax[:, q4:q4 + 1],
                                                                   accum_out=rowsum[:, q4:q4 + 1]), [mx, P_free[r], att_free[0]], "act_softmax")
                bank_free[bk] = ex
                rc = dve(lambda e, q4=q4: e.reciprocal(rowinv[:, q4:q4 + 1], rowsum[:, q4:q4 + 1]), [ex], "dve_softmax")
                nm = dve(lambda e, q4=q4, r=r: e.tensor_scalar(Pr[:, r, :], Pr[:, r, :], rowinv[:, q4:q4 + 1], None, ALU.mult), [rc], "dve_softmax")
                stat_free[q4] = nm
                p_ready[n] = nm
            m = n - LAG_T
            if 0 <= m < len(steps):
                r, bk = m % 3, 2 + m % 2
                for c in range(TILES):
                    t = pe(lambda e, r=r, bk=bk, c=c: e.transpose(bank[bk][:, c * P:(c + 1) * P], Pr[:, r, c * P:(c + 1) * P], ident[:, :]),
                           [p_ready[m], bank_free[bk], ident_ok], "pe_probT")
                P_free[r] = t
                pt_ready[m] = act(lambda e, r=r, bk=bk: e.copy(PT[:, r, :, :].rearrange("p a b -> p (a b)"), bank[bk][:, :]), [t, PT_free[r]], "act_probT")
                bank_free[bk] = pt_ready[m]
            m = n - LAG_AV
            if m >= 0:
                h, i = steps[m]
                r, g, j = m % 3, h // HPG, h % 2
                for c in range(TILES):
                    t = pe(lambda e, r=r, g=g, j=j, c=c, i=i: e.matmul(bank[4][j * HD:(j + 1) * HD, i * P:(i + 1) * P], V_sb[:, c, g * HD:(g + 1) * HD],
                                                                  PT[:, r, c, :], start=(c == 0), stop=(c == TILES - 1)),
                           [pt_ready[m], v_ok, bank_free[4]], "pe_av")
                PT_free[r] = t
                if j == 1 and i == TILES - 1:
                    a_ok = act(lambda e, h=h: e.copy(AT[:, h // 2, :], bank[4][:, :]), [t, AT_free[0], att_free[0]], "act_av")
                    bank_free[4] = a_ok
            yield
        V_free[0] = t
        xT_done[1] = t
        sl = b % 2
        for i in range(TILES):
            bk = 2 + i % 2
            for p in range(HEADS // 2):
                t = pe(lambda e, i=i, p=p, bk=bk: e.matmul(bank[bk][:, 0:DM], AT[:, p, i * P:(i + 1) * P], Wpost_sb[:, p, :],
                                                           start=(p == 0), stop=(p == HEADS // 2 - 1)), [a_ok, bank_free[bk]], "pe_post")
            sok = dve(lambda e, i=i, bk=bk: e.tensor_tensor(s_sb[:, sl, i, :], bank[bk][:, 0:DM], xa[:, i, :], ALU.add),
                      [t, s_free[sl], w_ok[0]], "dve_s")
            bank_free[bk] = sok
            yield
        AT_free[0] = t
        att_x[0] = sok
        s_ready[b] = sok

    att_x, V_free, AT_free = [None], [None], [None]
    Q_free, K_free, P_free, PT_free, stat_free = [None] * RING_Q, [None] * 2, [None] * 3, [None] * 3, [None] * 4

    ex_free = {}

    def experts():
        y_done = None
        F = lambda k: ex_free.get(k)
        for e_ in range(EXPERTS):
            r = e_ % 2
            xl = load(xe[:, r, :, :], xbuf[e_ * CAP:(e_ + 1) * CAP, :].rearrange("(c p) d -> p c d", p=P), f"xe{r}", [scattered[0], w_ok[0], F(("xe", r))])
            wg = we[:, r, 0, :].rearrange("p (c i) -> p c i", c=KC)
            wu = we[:, r, 1, :].rearrange("p (c i) -> p c i", c=KC)
            wd = we[:, r, 2, :]
            for dst, src in ((wg, w_gate[e_].rearrange("(c p) i -> p c i", p=P)), (wu, w_up[e_].rearrange("(c p) i -> p c i", p=P)),
                             (wd, w_down[e_])):
                wl = load(dst, src, f"we{r}", [w_ok[0], F(("we", r))])
            for c in range(KC):
                for s in range(2):
                    t = pe(lambda e, c=c, s=s, r=r: e.transpose(bank[5][:, c * CAP + s * P:c * CAP + (s + 1) * P], xe[:, r, s, c * P:(c + 1) * P], ident[:, :]),
                           [xl, bank_free[5]], "pe_expert")
            ex_free[("xe", r)] = t
            xt = dve(lambda e, r=r: e.tensor_copy(xeT[:, r, :, :].rearrange("p a b -> p (a b)"), bank[5][:, :]), [t, F(("xeT", r))], "dve_expert")
            bank_free[5] = xt
            for j, w in enumerate((wg, wu)):
                for c in range(KC):
                    t = pe(lambda e, c=c, j=j, w=w, r=r: e.matmul(bank[6][:, j * CAP:(j + 1) * CAP], w[:, c, :], xeT[:, r, c, :],
                                                                  start=(c == 0), stop=(c == KC - 1)), [xt, wl, bank_free[6]], "pe_expert")
            ex_free[("xeT", r)] = t
            sl = act(lambda e, r=r: e.activation(sg[:, r, :], bank[6][:, 0:CAP], ACT.Silu), [t, F(("sg", r))], "act_expert")
            hh = dve(lambda e, r=r: e.tensor_tensor(he[:, r, :], bank[6][:, CAP:2 * CAP], sg[:, r, :], ALU.mult), [sl, F(("he", r))], "dve_expert")
            bank_free[6] = hh
            ex_free[("sg", r)] = hh
            yield
            for s in range(2):
                t = pe(lambda e, s=s, r=r, wd=wd: e.matmul(bank[7][:, s * DM:(s + 1) * DM], he[:, r, s * P:(s + 1) * P], wd, start=True, stop=True),
                       [hh, bank_free[7]], "pe_expert")
            ex_free[("he", r)] = ex_free[("we", r)] = t
            yk = act(lambda e, r=r: e.copy(ye[:, r, :, :].rearrange("p a b -> p (a b)"), bank[7][:, :]), [t, F(("ye", r))], "act_expert")
            bank_free[7] = yk
            ex_free[("ye", r)] = load(ybuf[e_ * CAP:(e_ + 1) * CAP, :].rearrange("(c p) d -> p c d", p=P), ye[:, r, :, :], f"y_out{r}", [yk])
            yield
        y_stored[:] = [ex_free[("ye", 0)], ex_free[("ye", 1)]]

    y_stored = [None, None]
    x1_ready, xn1_ready, z_args = [None] * NB, [None] * NB, [None] * NB
    batch_free = [None] * 2
    row_free = [None] * RING_ROWS
    xc_free = [None]

    def combine(b):
        sl = b % 2
        z = dve(lambda e: e.memset(rows_sb[:, :, :], 0.0), [], "dve_combine") if b == 0 else None
        xl = load(x1[:, sl, :, :], X[b].rearrange("(t p) d -> p t d", p=P), f"x_comb{sl}", [batch_free[sl]])
        for i in range(TILES):
            t_ = b * TILES + i
            got = {}

            def gather(k, t_=t_, got=got):
                r = k % RING_ROWS
                got[k] = do("pool", lambda e: e.indirect_dma_start(
                    rows_sb[:, r, :], None, ybuf, bass.IndirectOffsetOnAxis(ap=slot_idx[:, t_, k:k + 1], axis=0),
                    bounds_check=SLOTS - 1, oob_is_err=False), y_stored + [row_free[r], z], f"gather{r}", 16)

            for k in range(RING_ROWS):
                gather(k)
            yield
            for k in range(TOPK):
                r = k % RING_ROWS
                if k == 0:
                    t = dve(lambda e, t_=t_, r=r, k=k: e.tensor_scalar(acc_sb[:, :], rows_sb[:, r, :], slot_w[:, t_, k:k + 1], None, ALU.mult),
                            [got[k], w_ok[0], xc_free[0]], "dve_combine")
                else:
                    t = dve(lambda e, t_=t_, r=r, k=k: e.scalar_tensor_tensor(acc_sb[:, :], rows_sb[:, r, :], slot_w[:, t_, k:k + 1], acc_sb[:, :],
                                                                         ALU.mult, ALU.add), [got[k], t], "dve_combine")
                row_free[r] = t
                if k + RING_ROWS < TOPK:
                    gather(k + RING_ROWS)
                    yield
            gk = act(lambda e: e.activation(gate_sb[:, :], acc_sb[:, :], ACT.Silu), [t], "act_combine")
            xc_free[0] = gk
            t = dve(lambda e, i=i: e.tensor_tensor(gate_sb[:, :], gate_sb[:, :], s_sb[:, sl, i, :], ALU.mult), [gk, s_ready[b]], "dve_combine")
            t = dve(lambda e, i=i: e.tensor_tensor(x1[:, sl, i, :], x1[:, sl, i, :], gate_sb[:, :], ALU.add), [t, xl], "dve_combine")
            xc_free[0] = t
            yield
        s_free[sl] = t
        x1_ready[b] = t
        st = statistics(x1[:, sl], lnm[:, sl, 0, :], lnm[:, sl, 1, :], [t], "x1")
        xn1_ready[b] = normalise(xn1, x1[:, sl], lnm[:, sl, 0, :], lnm[:, sl, 1, :], st + xn1_free)
        yield

    lnm = sb("lnm", [P, 2, 4, TILES])
    g1_ready = [None] * NB
    xn1_free = [None, None]
    wr_free = [None] * 2
    dec_free, msk_free, actb_free = [None] * 2, [None] * 3, [None] * 3

    def trees(b):
        sl = b % 2
        tr = transposed(xn1, [xn1_ready[b]], (2, 3))
        xn1_free[0] = tr[KC - 1]
        for c in range(KC):
            xT = act(lambda e, c=c: e.copy(xT1[:, c, :], bank[2 + c][:, :]), [tr[c], AT_free[0]], "act_tree")
            bank_free[2 + c] = xT
        yield
        pend = []
        n_units = 2 * TREES
        state = {}

        def front(w):
            r, half = w // 2, w % 2
            m = INNER if half == 0 else P
            lo = r * NODES + half * INNER
            k = w % 2
            load(wr_in[:, k, :, 0:m], ffn_WinT[:, lo:lo + m].rearrange("(c p) n -> p c n", p=P), f"wr{k}", [wr_free[k], V_free[0]])
            wl = load(wr_out[0:m, k, :], ffn_WoutT[lo:lo + m, :], f"wr{k}", [wr_free[k], V_free[0]])
            for c in range(KC):
                t = pe(lambda e, c=c, k=k, m=m: e.matmul(bank[k][0:m, :], wr_in[:, k, c, 0:m], xT1[:, c, :], start=(c == 0), stop=(c == KC - 1)),
                       [xT, wl, bank_free[k]], "pe_tree")
            a = act(lambda e, w=w, k=k, m=m: e.activation(act_sb[0:m, w % 3, :], bank[k][0:m, :], ACT.Silu, bias=ffn_b_sb[0:m, w:w + 1]),
                    [t, actb_free[w % 3], P_free[w % 3]], "act_tree")
            bank_free[k] = a
            if half == 0:
                state[r] = dve(lambda e, w=w, k=k, r=r: e.tensor_scalar(dec_sb[0:INNER, r % 2, :], bank[k][0:INNER, :], ffn_b_sb[0:INNER, w:w + 1], 0.0,
                                                                    ALU.add, ALU.is_gt), [a, dec_free[r % 2]], "dve_tree")
                bank_free[k] = state[r]
            return a

        def back(w, a):
            r, half = w // 2, w % 2
            m = INNER if half == 0 else P
            k = w % 2
            t = pe(lambda e, r=r, half=half, m=m: e.matmul(bank[2][0:m, :], path_sb[0:INNER, half * P:half * P + m], dec_sb[0:INNER, r % 2, :],
                                                           start=True, stop=True), [state[r], bank_free[2], path_ok], "pe_tree")
            if half == 1:
                dec_free[r % 2] = t
            mk = dve(lambda e, w=w, half=half, m=m: e.scalar_tensor_tensor(masked[0:m, w % 3, :], bank[2][0:m, :], need_sb[0:m, half:half + 1],
                                                                           act_sb[0:m, w % 3, :], ALU.is_ge, ALU.mult),
                     [t, a, msk_free[w % 3], PT_free[w % 3]], "dve_tree")
            bank_free[2] = actb_free[w % 3] = mk
            for c in range(KC):
                t = pe(lambda e, w=w, c=c, m=m, k=k: e.matmul(bank[3 + c][:, :], wr_out[0:m, k, c * P:(c + 1) * P], masked[0:m, w % 3, :],
                                                         start=(w == 0), stop=(w == n_units - 1)), [mk, bank_free[3 + c]], "pe_tree")
            msk_free[w % 3] = wr_free[k] = t
            return t

        prev = None
        for w in range(n_units):
            a = front(w)
            if prev is not None:
                t = back(w - 1, prev)
            prev = a
            yield
        t = back(n_units - 1, prev)
        for c in range(KC):
            o = act(lambda e, c=c: e.copy(oT[:, c, :], bank[3 + c][:, :]), [t, AT_free[0]], "act_tree")
            bank_free[3 + c] = o
        yield
        for i in range(TILES):
            bk = i // 2
            for c in range(KC):
                t = pe(lambda e, i=i, c=c, bk=bk: e.transpose(bank[bk][:, (i % 2) * DM + c * P:(i % 2) * DM + (c + 1) * P], oT[:, c, i * P:(i + 1) * P], ident[:, :]),
                       [o, bank_free[bk]], "pe_tree")
            if i % 2:
                gk = act(lambda e, i=i, bk=bk: e.activation(g1[:, sl, i - 1:i + 1, :].rearrange("p a b -> p (a b)"), bank[bk][:, :], ACT.Silu),
                         [t, batch_free[sl]], "act_tree")
                bank_free[bk] = gk
        AT_free[0] = t
        for k in range(3):
            P_free[k], PT_free[k] = actb_free[k], msk_free[k]
        V_free[0] = msk_free[(n_units - 1) % 3]
        g1_ready[b] = gk
        yield

    MA, MB, MY = 5, 6, 7
    arena_free = [None]
    mz_free = [None]

    def mamba(b):
        sl = b % 2
        first = arena_free[0] if arena_free[0] else [scattered[0], w_ok[0]] + y_stored
        zz = hT.rearrange("p a (b c) -> p (a b) c", c=DM)
        st = statistics(xn1, lnm[:, sl, 2, :], lnm[:, sl, 3, :], [xn1_ready[b]], "xn1")
        z_sb = BC.rearrange("p a b s -> p (a b s)")[:, 0:TILES * DM].rearrange("p (t d) -> p t d", d=DM)
        nrm = normalise(z_sb, xn1, lnm[:, sl, 2, :], lnm[:, sl, 3, :], st + first)
        xn1_free[1] = nrm
        tr = transposed(z_sb, [nrm], (MA, MB))
        for c in range(KC):
            h_ok = act(lambda e, c=c: e.activation(hT[:, c, :], bank[MA + c][:, :], ACT.Identity, scale=ln_gb_sb[:, 0, c:c + 1], bias=ln_gb_sb[:, 1, c:c + 1]),
                       [tr[c]] + first, "act_ssm")
            bank_free[MA + c] = h_ok
        yield
        for cb in range(CB):
            bk = (MA, MB)[cb % 2]
            for c in range(KC):
                t = pe(lambda e, c=c, cb=cb, bk=bk: e.matmul(bank[bk][:, :], WinT_sb[:, c, cb * P:(cb + 1) * P], hT[:, c, :], start=(c == 0), stop=(c == KC - 1)),
                       [h_ok, w_ssm, bank_free[bk]], "pe_ssm")
            d = dve(lambda e, cb=cb, bk=bk: e.tensor_scalar(y_sb[:, cb, :], bank[bk][:, :], chan_sb[:, cb, DCONV - 1:DCONV], chan_sb[:, cb, DCONV:DCONV + 1],
                                                            ALU.mult, ALU.add), [t] + first, "dve_ssm")
            for j in range(1, DCONV):
                d = dve(lambda e, cb=cb, bk=bk, j=j: e.scalar_tensor_tensor(y_sb[:, cb, j:], bank[bk][:, 0:SEQ - j], chan_sb[:, cb, DCONV - 1 - j:DCONV - j],
                                                                            y_sb[:, cb, j:], ALU.mult, ALU.add), [d], "dve_ssm")
            bank_free[bk] = d
            xs_ok = act(lambda e, cb=cb: e.activation(xs[:, cb, :], y_sb[:, cb, :], ACT.Silu), [d, tr[1]], "act_ssm")
            yield
        for cb in range(CB):
            t = pe(lambda e, cb=cb: e.matmul(bank[MA][0:DTR + 2 * DS, :], WxT_sb[:, cb, :], xs[:, cb, :], start=(cb == 0), stop=(cb == CB - 1)),
                   [xs_ok, bank_free[MA]], "pe_ssm")
        xd_ok = act(lambda e: e.copy(xd[0:DTR + 2 * DS, :], bank[MA][0:DTR + 2 * DS, :]), [t, tr[1]], "act_ssm")
        bank_free[MA] = xd_ok
        bc_out = load(bc_dram[b], xd[DTR:DTR + 2 * DS, :], "bc_out", [xd_ok])
        bc_stores[:] = [bc_out]
        yield
        dt_read = None
        for cb in range(CB):
            bk = (MA, MB)[cb % 2]
            t = pe(lambda e, cb=cb, bk=bk: e.matmul(bank[bk][:, :], WdtT_sb[:, cb * P:(cb + 1) * P], xd[0:DTR, :], start=True, stop=True),
                   [xd_ok, bank_free[bk]], "pe_ssm")
            bdt = chan_sb[:, cb, DCONV + 1:DCONV + 2]
            a = act(lambda e, bk=bk, bdt=bdt: e.activation(sp_a[:, 0, :], bank[bk][:, :], ACT.Abs, bias=bdt), [t, dt_read] + first, "act_ssm")
            a = act(lambda e: e.activation(sp_a[:, 0, :], sp_a[:, 0, :], ACT.Exp, scale=-1.0), [a], "act_ssm")
            a = act(lambda e: e.activation(sp_a[:, 0, :], sp_a[:, 0, :], ACT.Ln, bias=1.0), [a], "act_ssm")
            d = dve(lambda e, cb=cb, bk=bk, bdt=bdt: e.tensor_scalar(dt_sb[:, cb, :], bank[bk][:, :], bdt, 0.0, ALU.add, ALU.max), [a] + first, "dve_ssm")
            bank_free[bk] = d
            dt_read = d = dve(lambda e, cb=cb: e.tensor_tensor(dt_sb[:, cb, :], dt_sb[:, cb, :], sp_a[:, 0, :], ALU.add), [d], "dve_ssm")
            u_ok = dve(lambda e, cb=cb: e.tensor_tensor(u_sb[:, cb, :], dt_sb[:, cb, :], xs[:, cb, :], ALU.mult), [d], "dve_ssm")
            y_ok = dve(lambda e, cb=cb: e.tensor_scalar(y_sb[:, cb, :], xs[:, cb, :], chan_sb[:, cb, DCONV + 2:DCONV + 3], None, ALU.mult), [xs_ok], "dve_ssm")
            yield
        last_bc = []
        bc_free = [[u_ok, y_ok, t, bc_out]] * HALF_STATES
        dA_free, dB_free, h_free = [dt_read, dt_read], [None, None], [None, None]
        Y_free = None
        for rnd in range(2):
            bc_ok = []
            for n in range(HALF_STATES):
                src = bass.AP(bc_dram.tensor, bc_dram[b, rnd * HALF_STATES + n].offset, [[0, P], [DS * SEQ, 2], [1, SEQ]])
                bc_ok.append(load(BC[:, n, :, :], src, f"bc{n}", bc_free[n]))
            bc_free = [[]] * HALF_STATES
            todo = [(cb, n) for cb in range(CB) for n in range(HALF_STATES)]
            scanned = {}
            for k in range(len(todo) + 1):
                if k < len(todo):
                    cb, n = todo[k]
                    r = k % 2
                    s = rnd * HALF_STATES + n
                    ea = act(lambda e, cb=cb, s=s, r=r: e.activation(dA[:, r, :], dt_sb[:, cb, :], ACT.Exp, scale=A_sb[:, cb, s:s + 1]), [dt_read, A_ok, dA_free[r]], "act_decay")
                    eb = pool(lambda e, cb=cb, n=n, r=r: e.tensor_tensor(dBu[:, r, :], u_sb[:, cb, :], BC[:, n, 0, :], ALU.mult), [u_ok, bc_ok[n], dB_free[r]], "pool_input")
                    sc = dve(lambda e, r=r: e.tensor_tensor_scan(hst[:, r, :], dA[:, r, :], dBu[:, r, :], 0.0, ALU.mult, ALU.add), [ea, eb, h_free[r]], "dve_scan")
                    dA_free[r] = dB_free[r] = sc
                    scanned[k] = sc
                    inputs_read = eb
                if k >= 1:
                    cb, n = todo[k - 1]
                    r = (k - 1) % 2
                    eng = pool if n % 2 == 0 else dve
                    pr = eng(lambda e, r=r, n=n: e.tensor_tensor(hst[:, r, :], hst[:, r, :], BC[:, n, 1, :], ALU.mult), [scanned[k - 1], bc_ok[n]],
                             "pool_output" if n % 2 == 0 else "dve_output")
                    t = pe(lambda e, r=r, n=n: e.matmul(bank[MY][:, :], ident[:, :], hst[:, r, :], start=(n == 0), stop=(n == HALF_STATES - 1)),
                           [pr, bank_free[MY]], "pe_states")
                    h_free[r] = t
                    if cb == CB - 1:
                        bc_free[n] = [pr, inputs_read]
                        last_bc += [pr, inputs_read]
                    if n == HALF_STATES - 1:
                        y_ok = dve(lambda e, cb=cb: e.tensor_tensor(y_sb[:, cb, :], bank[MY][:, :], y_sb[:, cb, :], ALU.add), [t, y_ok], "dve_y")
                        bank_free[MY] = y_ok
                yield
        for cb in range(CB):
            bk = (MA, MB)[cb % 2]
            for c in range(KC):
                t = pe(lambda e, c=c, cb=cb, bk=bk: e.matmul(bank[bk][:, :], WinT_sb[:, c, DI + cb * P:DI + (cb + 1) * P], hT[:, c, :], start=(c == 0), stop=(c == KC - 1)),
                       [bank_free[bk]], "pe_ssm")
            a = act(lambda e, bk=bk: e.activation(res_sb[:, :], bank[bk][:, :], ACT.Silu), [t, mz_free[0]] + first, "act_ssm")
            bank_free[bk] = a
            y_ok = mz_free[0] = dve(lambda e, cb=cb: e.tensor_tensor(y_sb[:, cb, :], y_sb[:, cb, :], res_sb[:, :], ALU.mult), [a, y_ok], "dve_y")
            yield
        d = y_ok
        for i in range(TILES):
            bk = (MA, MB)[i % 2]
            for cb in range(CB):
                t = pe(lambda e, i=i, cb=cb, bk=bk: e.matmul(bank[bk][:, 0:DM], y_sb[:, cb, i * P:(i + 1) * P], WoutT_sb[:, cb, :], start=(cb == 0), stop=(cb == CB - 1)),
                       [y_ok, bank_free[bk]], "pe_ssm")
            fin = res_sb[:, (i % 2) * DM:(i % 2 + 1) * DM]
            d0 = dve(lambda e, i=i, fin=fin: e.tensor_scalar(fin, x1[:, sl, i, :], lnm[:, sl, 0, i:i + 1], lnm[:, sl, 1, i:i + 1],
                                                        ALU.subtract, ALU.mult), [y_ok, d], "dve_y")
            d = dve(lambda e, i=i, bk=bk, fin=fin: e.scalar_tensor_tensor(fin, bank[bk][:, 0:DM], alpha_sb[:, 0:1], fin, ALU.mult, ALU.add), [t, d0, w_small], "dve_y")
            bank_free[bk] = d
            d = dve(lambda e, i=i, fin=fin: e.tensor_tensor(fin, fin, g1[:, sl, i, :], ALU.mult), [d, g1_ready[b]], "dve_y")
            d = dve(lambda e, i=i, fin=fin: e.tensor_tensor(x1[:, sl, i, :], x1[:, sl, i, :], fin, ALU.add), [d], "dve_y")
            yield
        stored = load(out[b].rearrange("(t p) d -> p t d", p=P), x1[:, sl, :, :], f"stored{sl}", [d])
        batch_free[sl] = stored
        final[sl] = stored
        arena_free[0] = [d, t, y_ok] + last_bc[-4:]
        yield

    final, bc_stores = [None, None], []

    def run(g):
        for _ in g:
            pass

    def together(a, b, ratio):
        credit, alive = 0.0, True
        for _ in b:
            credit += ratio
            while alive and credit >= 1:
                credit -= 1
                alive = next(a, "end") != "end"
        run(a)

    def chain(*gens):
        for g in gens:
            yield from g

    w_ssm = None
    for dst, src in ((WinT_sb, WinT), (WxT_sb, WxT), (WoutT_sb, WoutT)):
        w_ssm = load(dst[:, :, :], src.rearrange("(c p) n -> p c n", p=P), "w_ssm", queue="act")
    w_ssm = load(WdtT_sb[:, :], WdtT, "w_ssm", queue="act")
    AT_free[0] = path_ok
    run(routing())
    run(scatter())
    run(attention(0))
    run(experts())
    for b in range(NB):
        run(combine(b))
        run(trees(b))
        run(mamba(b))
        if b + 1 < NB:
            run(attention(b + 1))

    block = ctx.enter_context(nc.Block())

    @block.sync
    def _(e):
        run_queue("sp", e)
        for sem, value in final + bc_stores:
            e.wait_ge(sems[sem], value)

    @block.scalar
    def _(e):
        run_queue("act", e)

    @block.vector
    def _(e):
        run_queue("dve", e)

    @block.gpsimd
    def _(e):
        run_queue("pool", e)

    @block.tensor
    def _(e):
        run_queue("pe", e)

    ctx.close()


def host_layout(d):
    f = np.float32
    chunk = lambda v: v.reshape(-1, P).T
    path, need = np.zeros((INNER, 2 * P), f), np.zeros((P, 2), f)
    for node in range(NODES):
        col = node if node < INNER else P + node - INNER
        v = node
        while v > 0:
            up = (v - 1) // 2
            path[up, col] = 1.0 if v == 2 * up + 2 else -1.0
            need[col % P, col // P] += v == 2 * up + 2
            v = up
    ffn_b = np.zeros((P, 2 * TREES), f)
    for r in range(TREES):
        ffn_b[:INNER, 2 * r] = d["L1_ffn_b_in"][r * NODES:r * NODES + INNER]
        ffn_b[:, 2 * r + 1] = d["L1_ffn_b_in"][r * NODES + INNER:(r + 1) * NODES]
    block = lambda v: v.reshape(CB, P, -1).transpose(1, 0, 2)
    chan = np.concatenate([block(d["L1_attn_conv_w"].reshape(DI, DCONV)), block(d["L1_attn_conv_b"]),
                           block(d["L1_attn_b_dt"]), block(d["L1_attn_D_param"])], axis=2)
    before = np.tril(np.ones((EG, EG), f), -1)
    return {
        "X": d["L0_attn_X"], "Wq": d["L0_attn_Wq"], "Wk": d["L0_attn_Wk"], "Wv": d["L0_attn_Wv"], "Wpost": d["L0_attn_Wpost"],
        "gateT": d["L0_ffn_gate_w"].T, "gate_bias": d["L0_ffn_gate_bias"], "w_gate": d["L0_ffn_w_gate"], "w_up": d["L0_ffn_w_up"],
        "w_down": d["L0_ffn_w_down"],
        "ln_gb": np.stack([chunk(d["L1_attn_ln_g"]), chunk(d["L1_attn_ln_b"])], axis=1),
        "WinT": d["L1_attn_W_in"].T, "WxT": d["L1_attn_W_x"].T, "WdtT": d["L1_attn_W_dt"].T, "WoutT": d["L1_attn_W_out"].T,
        "chan": chan, "A_log": block(d["L1_attn_A_log"]), "alpha": d["L1_attn_alpha"],
        "ffn_WinT": d["L1_ffn_W_in"].T, "ffn_b": ffn_b, "ffn_WoutT": d["L1_ffn_W_out"].T,
        "path": path, "need": need, "tri": np.triu(np.ones((P, P), f), 1), "glt": before.reshape(-1),
        "slot_base": (np.arange(EXPERTS) * CAP + 1).astype(f),
    }


def kernel(**inputs):
    import concourse.bacc as bacc
    from concourse.bass_utils import run_bass_kernel_spmd

    nc = bacc.Bacc("TRN2", target_bir_lowering=False, num_devices=1)
    arrays = {f"in_{n}": np.ascontiguousarray(a) for n, a in host_layout({k: np.asarray(v) for k, v in inputs.items()}).items()}
    aps = {n[3:]: nc.dram_tensor(n, a.shape, mybir.dt.from_np(a.dtype), kind="ExternalInput").ap() for n, a in arrays.items()}
    out = nc.dram_tensor("out_x", [NB, SEQ, DM], mybir.dt.float32, kind="ExternalOutput").ap()
    build_program(nc, out=out, **aps)
    result = run_bass_kernel_spmd(nc, [arrays], core_ids=[0])
    return result.results[0]["out_x"]
```

```python
import concourse.bass as bass
from concourse import mybir
from contextlib import ExitStack
import numpy as np

NB, SEQ, DM = 8, 512, 256
P = 128
TILES = SEQ // P
NT = NB * TILES
KC = DM // P
HEADS, GROUPS, HD = 16, 4, 64
HPG = HEADS // GROUPS
EXPERTS, EG, TOPG, TOPK, EI, CAP = 64, 8, 4, 8, 128, 256
EPG = EXPERTS // EG
SLOTS = EXPERTS * CAP
ROUTE_SCALE = 2.5
DI, DS, DTR, DCONV = 512, 16, 64, 4
CB = DI // P
TREES, DEPTH = 8, 7
NODES = 2 ** (DEPTH + 1) - 1
INNER = 2 ** DEPTH - 1
HALF_STATES = DS // 2
EPS = 1e-5
RING_Q = 3
RING_S, LAG_C, LAG_S = 4, 1, 3
RING_W = 4
TREES_PER_PROJECTION, ATTENTION_PER_SCAN = 1.8, 1.05
RING_ROWS = 4
BIG = 3.0e38
GONE = 65536.0


def build_program(nc, X, Wq, Wk, Wv, Wpost, gateT, gate_bias, w_gate, w_up, w_down, ln_gb, WinT, WxT, WdtT,
                  WoutT, chan, A_log, alpha, ffn_WinT, ffn_b, ffn_WoutT, path, need, tri, glt, slot_base, out):
    fp32, f32r, bf16 = mybir.dt.float32, mybir.dt.float32r, mybir.dt.bfloat16
    i32 = mybir.dt.int32
    ALU, ACT, AX = mybir.AluOpType, mybir.ActivationFunctionType, mybir.AxisListType

    ctx = ExitStack()
    queues = {n: [] for n in ("pe", "act", "dve", "pool", "sp")}
    sems, counts = {}, {}

    def semaphore(name):
        if name not in sems:
            sems[name] = ctx.enter_context(nc.semaphore(name))
            counts[name] = 0
        return sems[name]

    def do(engine, emit, after=(), signal=None, by=1):
        target = semaphore(signal) if signal else None
        queues[engine].append((emit, [a for a in after if a is not None], target, by))
        if signal:
            counts[signal] += by
            return (signal, counts[signal])
        return None

    def pe(emit, after=(), signal=None):
        return do("pe", emit, after, signal)

    def act(emit, after=(), signal=None):
        return do("act", emit, after, signal)

    def dve(emit, after=(), signal=None):
        return do("dve", emit, after, signal)

    def pool(emit, after=(), signal=None):
        return do("pool", emit, after, signal)

    def load(dst, src, signal, after=(), queue="sp"):
        return do(queue, lambda e: e.dma_start(dst, src), after, signal, 16)

    def run_queue(name, engine):
        reached = {}
        for emit, after, target, by in queues[name]:
            for sem, value in after:
                if reached.get(sem, 0) < value:
                    engine.wait_ge(sems[sem], value)
                    reached[sem] = value
            ins = emit(engine)
            if target is not None:
                ins.then_inc(target, by)

    def known(token):
        assert token is not None, "its producer must be queued first"
        return token

    def sb(name, shape, dt=fp32):
        return ctx.enter_context(nc.sbuf_tensor(name, shape, dt))

    xbuf = nc.dram_tensor("xbuf", [SLOTS, DM], fp32, kind="Internal").ap()
    ybuf = nc.dram_tensor("ybuf", [SLOTS, DM], fp32, kind="Internal").ap()
    bc_dram = nc.dram_tensor("bc_dram", [NB, 2 * DS, SEQ], fp32, kind="Internal").ap()

    ident = sb("ident", [P, P])
    tri_sb, ones_sb = sb("tri_sb", [P, P], bf16), sb("ones_sb", [P, P], bf16)
    path_sb = sb("path_sb", [P, 2 * P], bf16)
    need_sb = sb("need_sb", [P, 2])
    ffn_b_sb = sb("ffn_b_sb", [P, 2 * TREES])
    ln_gb_sb = sb("ln_gb_sb", [P, 2, KC])
    chan_sb = sb("chan_sb", [P, CB, DCONV + 3])
    A_sb = sb("A_sb", [P, CB, DS])
    alpha_sb = sb("alpha_sb", [P, 1])
    mhalf = sb("mhalf", [P, 1])
    Wq_sb = sb("Wq_sb", [P, KC, HEADS * HD])
    Wk_sb = sb("Wk_sb", [P, KC, GROUPS * 2 * HD])
    Wv_sb = sb("Wv_sb", [P, KC, GROUPS * HD])
    Wpost_sb = sb("Wpost_sb", [P, HEADS // 2, DM])
    WinT_sb = sb("WinT_sb", [P, KC, 2 * DI])
    WxT_sb = sb("WxT_sb", [P, CB, DTR + 2 * DS])
    WdtT_sb = sb("WdtT_sb", [DTR, DI])
    WoutT_sb = sb("WoutT_sb", [P, CB, DM])
    stats0 = sb("stats0", [P, NT, 2])
    slot_idx = sb("slot_idx", [P, NT, TOPK], i32)
    slot_w = sb("slot_w", [P, NT, TOPK])
    xa = sb("xa", [P, TILES, DM])
    xaT = sb("xaT", [P, KC, SEQ])
    Kst = sb("Kst", [P, 2, 2, SEQ], f32r)
    Qst = sb("Qst", [P, RING_Q, SEQ], f32r)
    V_sb = sb("V_sb", [P, TILES, GROUPS * HD])
    Pr = sb("Pr", [P, 3, SEQ])
    PT = sb("PT", [P, 3, TILES, P])
    AT = sb("AT", [P, HEADS // 2, SEQ])
    negmax, rowsum, rowinv = sb("negmax", [P, 4]), sb("rowsum", [P, 4]), sb("rowinv", [P, 4])
    s_sb = sb("s_sb", [P, 2, TILES, DM])
    rows_sb = sb("rows_sb", [P, RING_ROWS, DM])
    acc_sb = sb("acc_sb", [P, DM])
    gate_sb = sb("gate_sb", [P, DM])
    x1 = sb("x1", [P, 2, TILES, DM])
    xn1 = sb("xn1", [P, TILES, DM])
    bst, bag = sb("bst", [P, TILES, 6]), sb("bag", [P, TILES, 2])
    rst = sb("rst", [P, TILES])
    g1 = sb("g1", [P, 2, TILES, DM])
    wr_in = [v.rearrange("p (b c) -> p b c", c=P) for v in (V_sb[:, 0, :], V_sb[:, 1, :], xaT[:, 0, 0:DM], xaT[:, 0, DM:SEQ])]
    wr_out = [V_sb[:, 2, :], V_sb[:, 3, :], xaT[:, 1, 0:DM], xaT[:, 1, DM:SEQ]]
    arena = sb("arena", [P, 18944])
    view = {}
    at = [0]

    def part(name, *dims, base=None):
        n = int(np.prod(dims))
        if base is not None:
            at[0] = base
        v = arena[:, at[0]:at[0] + n]
        if len(dims) == 2:
            v = v.rearrange("p (a b) -> p a b", b=dims[1])
        elif len(dims) == 3:
            v = v.rearrange("p (a b c) -> p a b c", b=dims[1], c=dims[2])
        at[0] += n
        view[name] = v
        assert at[0] <= 18944, (name, at[0])
        return v

    hT = part("hT", KC, SEQ, base=0)
    dt_sb, u_sb, y_sb = part("dt", CB, SEQ), part("u", CB, SEQ), part("y", CB, SEQ)
    res_sb = part("res", SEQ)
    BC = part("BC", HALF_STATES, 2, SEQ)
    dA, st_sb = part("dA", 2, SEQ), part("st", RING_S, SEQ)
    xs = BC.rearrange("p a b s -> p (a b) s")[:, 0:CB, :]
    xd = BC.rearrange("p a b s -> p (a b) s")[:, CB, :]
    sp_a = dA[:, :, :]
    xn_all = part("xn_all", NT, DM, base=0)
    RT = [part(f"route{i}", NT, EXPERTS) for i in range(5)]
    xe = part("xe", 2, 2, DM * 1, base=NT * DM)
    xeT = part("xeT", 2, KC, CAP)
    we = part("we", 2, 3, 2 * P)
    sg = part("sg", 2, CAP)
    he = part("he", 2, CAP)
    ye = part("ye", 2, 2, DM)
    route0_end = NT * DM + 5 * NT * EXPERTS
    gw_sb = arena[:, route0_end:route0_end + KC * EXPERTS].rearrange("p (a b) -> p a b", b=EXPERTS)
    bias_sb = arena[:, route0_end + 128:route0_end + 192]
    base_sb = arena[:, route0_end + 192:route0_end + 256]
    glt_sb = arena[:, route0_end + 256:route0_end + 320].rearrange("p (a b) -> p a b", b=EG)
    assert route0_end + 320 <= 18944
    act_sb = Pr
    masked = PT.rearrange("p a b c -> p a (b c)")
    dec_sb = sb("dec_sb", [P, 2, SEQ], bf16)
    xT1 = AT[:, 0:KC, :]
    oT = AT[:, KC:2 * KC, :]
    zt = AT[:, 4:6, :].rearrange("p a (b c) -> p (a b) c", c=DM)

    bank = [ctx.enter_context(nc.psum_tensor(f"bank{i}", [P, SEQ], fp32)) for i in range(8)]
    MA, MB, MY = 5, 6, 7
    bank_free = [None] * 8

    def broadcast(src, n):
        return bass.AP(src.tensor, src.offset, [[0, P], [1, n]])

    w_first = load(gw_sb, gateT.rearrange("(c p) e -> p c e", p=P), "w_first")
    for dst, src in ((bias_sb, broadcast(gate_bias, EXPERTS)), (base_sb, broadcast(slot_base, EXPERTS)),
                     (glt_sb.rearrange("p a b -> p (a b)"), broadcast(glt, EG * EG))):
        w_first = load(dst, src, "w_first")
    stage = AT.rearrange("p a b -> p (a b)")
    w_small = load(stage[:, 0:P], tri, "w_small")
    for dst, src in ((stage[0:INNER, P:3 * P], path), (need_sb[:, :], need), (ffn_b_sb[:, :], ffn_b),
                     (ln_gb_sb[:, :, :], ln_gb), (chan_sb[:, :, :], chan), (A_sb[:, :, :], A_log),
                     (alpha_sb[:, :], broadcast(alpha, 1))):
        w_small = load(dst, src, "w_small")
    w_att = None
    for c in range(KC):
        for half in range(2):
            dst = Wk_sb[:, c, :].rearrange("p (g t d) -> p g t d", t=2, d=HD)[:, :, half, :]
            w_att = load(dst, Wk[c * P:(c + 1) * P, :].rearrange("p (g d) -> p g d", d=HD), "w_att", queue="act")
    for dst, src in ((Wq_sb, Wq), (Wv_sb, Wv), (Wpost_sb, Wpost)):
        w_att = load(dst[:, :, :], src.rearrange("(c p) n -> p c n", p=P), "w_att", queue="act")

    k0 = pool(lambda e: e.memset(ident[:, :], 0.0), signal="pool_const")
    ident_ok = pool(lambda e: e.affine_select(out=ident[:, :], in_=ident[:, :], compare_op=ALU.not_equal, fill=1.0, base=0,
                                              pattern=[[-1, P]], channel_multiplier=1), [k0], "pool_const")
    k1 = pool(lambda e: e.memset(ones_sb[:, :], 1.0), signal="pool_const")
    const_ok = pool(lambda e: e.memset(mhalf[:, :], -0.5), signal="pool_const")
    tri_ok = dve(lambda e: e.tensor_copy(tri_sb[:, :], stage[:, 0:P]), [w_small], "dve_const")
    path_ok = dve(lambda e: e.tensor_copy(path_sb[0:INNER, :], stage[0:INNER, P:3 * P]), [w_small], "dve_const")
    a0 = act(lambda e: e.activation(A_sb[:, :, :], A_sb[:, :, :], ACT.Exp), [w_small], "act_const")
    A_ok = dve(lambda e: e.tensor_scalar(A_sb[:, :, :], A_sb[:, :, :], -1.0, None, ALU.mult), [a0], "dve_const")
    zero_ok = dve(lambda e: e.memset(RT[4][:, :, :], 0.0), signal="dve_const")
    zrows = RT[4].rearrange("p a b -> p (a b)")
    x_loaded = [load(xn_all[:, b * TILES:(b + 1) * TILES, :], X[b].rearrange("(t p) d -> p t d", p=P), f"x_in{b}") for b in range(NB)]
    ROWS_Z = NT * EXPERTS // DM
    for i in range(SLOTS // (P * ROWS_Z)):
        zeroed = load(xbuf[i * P * ROWS_Z:(i + 1) * P * ROWS_Z, :].rearrange("(p r) d -> p (r d)", p=P), zrows, "zeroed", [zero_ok])

    def statistics(src, mean_of, inv_of, after, tag, last=[None]):
        t = None
        for i in range(TILES):
            t = dve(lambda e, i=i: e.bn_stats(bst[:, i, :], src[:, i, :]), list(after) + [last[0]], "dve_stats")
        for i in range(TILES):
            t = dve(lambda e, i=i: e.bn_aggr(bag[:, i, :], bst[:, i, :]), [t], "dve_stats")
        t = dve(lambda e: e.tensor_scalar(rst[:, :], bag[:, :, 1], EPS, None, ALU.add), [t], "dve_stats")
        m = dve(lambda e: e.tensor_copy(mean_of, bag[:, :, 0]), [t], "dve_stats")
        r = pool(lambda e: e.tensor_tensor(inv_of, rst[:, :], mhalf[:, 0:1].broadcast_to([P, TILES]), ALU.pow), [t, const_ok], "pool_rsqrt")
        last[0] = r
        return [m, r]

    def normalise(dst, src, mean_of, inv_of, after):
        for i in range(TILES):
            t = dve(lambda e, i=i: e.tensor_scalar(dst[:, i, :], src[:, i, :], mean_of[:, i:i + 1], inv_of[:, i:i + 1],
                                                   ALU.subtract, ALU.mult), after, "dve_norm")
        return t

    def transposed(src, after, banks):
        out_t = []
        for c in range(KC):
            for i in range(TILES):
                t = pe(lambda e, c=c, i=i: e.transpose(bank[banks[c]][:, i * P:(i + 1) * P], src[:, i, c * P:(c + 1) * P], ident[:, :]),
                       list(after) + [bank_free[banks[c]], ident_ok], "pe_transposed")
            out_t.append(t)
        return out_t

    scores, sfc = RT[0], RT[1]
    x_done = [None]
    xT_done = [None, None]
    xn_ready = []
    for b in range(NB):
        xin = xn_all[:, b * TILES:(b + 1) * TILES, :]
        mean_v, inv_v = stats0[:, b * TILES:(b + 1) * TILES, 0], stats0[:, b * TILES:(b + 1) * TILES, 1]
        st = statistics(xin, mean_v, inv_v, [x_loaded[b]], "x")
        nrm = normalise(xin, xin, mean_v, inv_v, st)
        xn_ready.append(nrm)
        tr = transposed(xin, [nrm], (0 + 2 * (b % 2), 1 + 2 * (b % 2)))
        for c in range(KC):
            bk = c + 2 * (b % 2)
            cp = act(lambda e, c=c, bk=bk: e.copy(xaT[:, c, :], bank[bk][:, :]), [tr[c], xT_done[0]], "act_xT")
            bank_free[bk] = cp
        for i in range(TILES):
            for c in range(KC):
                t = pe(lambda e, i=i, c=c, b=b: e.matmul(bank[4 + b % 2][:, i * EXPERTS:(i + 1) * EXPERTS], xaT[:, c, i * P:(i + 1) * P],
                                                    gw_sb[:, c, :], start=(c == 0), stop=(c == KC - 1)),
                       [cp, w_first, bank_free[4 + b % 2]], "pe_logits")
        xT_done[0] = t
        sc_ok = act(lambda e, b=b: e.activation(scores[:, b * TILES:(b + 1) * TILES, :].rearrange("p a b -> p (a b)"),
                                                bank[4 + b % 2][:, 0:TILES * EXPERTS], ACT.Sigmoid), [t], "act_scores")
        bank_free[4 + b % 2] = sc_ok

    def wide(src, dims):
        return bass.AP(src.tensor, src.offset, [list(src.ap[0])] + [list(d) for d in dims])

    small = g1.rearrange("p a b c -> p (a b c)")[:, 0:6 * NT * EG].rearrange("p (a b) -> p a b", b=NT * EG)
    m1, m2, n1, gsum, gpen = (small[:, i, :] for i in range(5))
    G8 = "p a (g k) -> p (a g) k"
    R1, R2, R3 = RT[2], RT[3], RT[4]
    ch = [None]

    def step(emit, after=()):
        ch[0] = dve(emit, [ch[0]] + list(after), "dve_route")
        return ch[0]

    def routing():
        sfc4 = sfc.rearrange(G8, k=EPG)
        rs = sfc4.ap[0]
        es = 1
        step(lambda e: e.tensor_tensor(sfc[:, :, :], scores[:, :, :], wide(bias_sb, [[0, NT], [1, EXPERTS]]), ALU.add), [sc_ok, w_first])
        step(lambda e: e.tensor_reduce(m1, sfc4, AX.X, ALU.max))
        step(lambda e: e.tensor_tensor(R1.rearrange(G8, k=EPG), sfc4, wide(m1, [[1, NT * EG], [0, EPG]]), ALU.is_equal))
        step(lambda e: e.tensor_reduce(n1, R1.rearrange(G8, k=EPG), AX.X, ALU.add))
        step(lambda e: e.scalar_tensor_tensor(R1[:, :, :], R1[:, :, :], -BIG, sfc[:, :, :], ALU.mult, ALU.add))
        step(lambda e: e.tensor_reduce(m2, R1.rearrange(G8, k=EPG), AX.X, ALU.max))
        step(lambda e: e.tensor_scalar(n1, n1, 2.0, -BIG, ALU.is_lt, ALU.mult))
        step(lambda e: e.tensor_tensor(n1, n1, m1, ALU.add))
        step(lambda e: e.tensor_tensor(m2, m2, n1, ALU.max))
        step(lambda e: e.tensor_tensor(gsum, m1, m2, ALU.add))
        yield 2.0
        gj = wide(gsum, [[EG, NT], [0, EG], [1, EG]])
        gi = wide(gsum, [[EG, NT], [1, EG], [0, EG]])
        r4 = "p a (i j) -> p a i j"
        step(lambda e: e.tensor_tensor(R1.rearrange(r4, j=EG), gj, gi, ALU.is_equal))
        step(lambda e: e.tensor_tensor(R1[:, :, :], R1[:, :, :], wide(glt_sb, [[0, NT], [1, EG * EG]]), ALU.mult))
        step(lambda e: e.tensor_tensor(R2.rearrange(r4, j=EG), gj, gi, ALU.is_gt))
        step(lambda e: e.tensor_tensor(R1[:, :, :], R1[:, :, :], R2[:, :, :], ALU.add))
        step(lambda e: e.tensor_reduce(gpen, R1.rearrange("p a (i j) -> p (a i) j", j=EG), AX.X, ALU.add))
        step(lambda e: e.tensor_scalar(gpen, gpen, float(TOPG), -BIG, ALU.is_ge, ALU.mult))
        step(lambda e: e.tensor_tensor(sfc4, sfc4, wide(gpen, [[1, NT * EG], [0, EPG]]), ALU.add))
        yield 2.0
        K8 = small[:, 5, :].rearrange("p (a b) -> p a b", b=TOPK)
        for t in range(NT):
            step(lambda e, t=t: e.max(K8[:, t, :], sfc[:, t, :]))
        for t in range(NT):
            step(lambda e, t=t: e.match_replace(R1[:, t, :], K8[:, t, :], sfc[:, t, :], -3.4e38))
        sel_b = R3.rearrange("p a b -> p (a b)")[:, 0:NT * EXPERTS // 2].bitcast(bf16)
        sel3 = sel_b.rearrange("p (a b) -> p a b", b=EXPERTS)
        yield 2.0
        sel_ok = step(lambda e: e.tensor_tensor(sel3, R1[:, :, :], sfc[:, :, :], ALU.not_equal), [zeroed])
        step(lambda e: e.tensor_tensor(scores[:, :, :], scores[:, :, :], sel3, ALU.mult))
        den = small[:, 0, 0:NT]
        step(lambda e: e.tensor_reduce(den, scores[:, :, :], AX.X, ALU.add))
        step(lambda e: e.tensor_scalar(den, den, 1e-20, None, ALU.add))
        step(lambda e: e.reciprocal(den, den))
        step(lambda e: e.tensor_scalar(den, den, ROUTE_SCALE, None, ALU.mult))
        step(lambda e: e.tensor_tensor(scores[:, :, :], scores[:, :, :], wide(den, [[1, NT], [0, EXPERTS]]), ALU.mult))
        yield 2.0
        QT = SEQ // EXPERTS
        tot = sfc.rearrange("p a b -> p (a b)").rearrange("p (b a) -> p a b", a=NT)
        for q in range(NT // QT):
            for j, (w, ok) in enumerate(((tri_sb, tri_ok), (ones_sb, const_ok))):
                t = pe(lambda e, j=j, w=w, q=q: e.matmul(bank[6 + j][:, :], w[:, :], sel_b[:, q * SEQ:(q + 1) * SEQ], start=True, stop=True),
                       [sel_ok, ok, bank_free[6 + j]], "pe_positions")
                dst = (R1 if j == 0 else tot)[:, q * QT:(q + 1) * QT, :]
                bank_free[6 + j] = step(lambda e, j=j, dst=dst: e.tensor_copy(dst, bank[6 + j].rearrange("p (a b) -> p a b", b=EXPERTS)), [t])
        keep = R2.rearrange("p a b -> p (a b)")
        step(lambda e: e.memset(keep, 1.0))
        step(lambda e: e.memset(keep.rearrange("p (b a) -> p b a", a=NT)[:, :, 0:1], 0.0))
        run = RT[3]
        flat = "p a b -> p (a b)"
        pre = small_scan
        step(lambda e: e.tensor_tensor_scan(pre[:, :], keep, sfc.rearrange(flat), 0.0, ALU.mult, ALU.add))
        step(lambda e: e.tensor_tensor(pre[:, :], pre[:, :], sfc.rearrange(flat), ALU.subtract))
        step(lambda e: e.tensor_tensor(R1[:, :, :], R1[:, :, :], pre.rearrange("p (b a) -> p a b", a=NT), ALU.add))
        step(lambda e: e.scalar_tensor_tensor(R2[:, :, :], R1[:, :, :], float(CAP), sel3, ALU.is_lt, ALU.mult))
        step(lambda e: e.tensor_tensor(scores[:, :, :], scores[:, :, :], R2[:, :, :], ALU.mult))
        step(lambda e: e.tensor_tensor(R1[:, :, :], R1[:, :, :], wide(base_sb, [[0, NT], [1, EXPERTS]]), ALU.add))
        step(lambda e: e.tensor_tensor(R1[:, :, :], R1[:, :, :], R2[:, :, :], ALU.mult))
        for t in range(NT):
            step(lambda e, t=t: e.max(K8[:, t, :], R1[:, t, :]))
        yield 2.0
        idx = small[:, 0, :].rearrange("p (a b) -> p a b", b=TOPK)
        step(lambda e: e.tensor_scalar(idx, K8, 0.0, GONE, ALU.is_equal, ALU.mult))
        step(lambda e: e.scalar_tensor_tensor(idx, K8, -1.0, idx, ALU.add, ALU.add))
        idx_ok[0] = step(lambda e: e.tensor_copy(slot_idx[:, :, :], idx))
        yield 2.0
        for k in range(TOPK):
            step(lambda e, k=k: e.tensor_tensor(R2[:, :, :], R1[:, :, :], wide(K8[:, :, k:k + 1], [[TOPK, NT], [0, EXPERTS]]), ALU.is_equal))
            step(lambda e: e.tensor_tensor(R2[:, :, :], R2[:, :, :], scores[:, :, :], ALU.mult))
            w_ok[0] = step(lambda e, k=k: e.tensor_reduce(slot_w[:, :, k], R2[:, :, :], AX.X, ALU.add))
            yield 2.0

    small_scan = s_sb.rearrange("p a b c -> p (a b c)")[:, 0:NT * EXPERTS]
    idx_ok, w_ok = [None], [None]

    def scatter():
        for t in range(NT):
            for k in range(TOPK):
                scattered[0] = do("pool", lambda e, t=t, k=k: e.indirect_dma_start(
                    xbuf, bass.IndirectOffsetOnAxis(ap=slot_idx[:, t, k:k + 1], axis=0), xn_all[:, t, :], None,
                    bounds_check=SLOTS - 1, oob_is_err=False), [idx_ok[0], xn_ready[t // TILES], zeroed], "scattered", 16)
                if k % 4 == 3:
                    yield 2.0

    scattered = [None]

    s_ready, s_free = [None] * NB, [None] * 2
    att_free = [None]

    def attention(b):
        xl = load(xa[:, :, :], X[b].rearrange("(t p) d -> p t d", p=P), "x_att", [att_free[0], att_x[0]])
        mean_v, inv_v = stats0[:, b * TILES:(b + 1) * TILES, 0], stats0[:, b * TILES:(b + 1) * TILES, 1]
        nrm = normalise(xa, xa, mean_v, inv_v, [xl, xn_ready[b]])
        tr = transposed(xa, [nrm], (2, 3))
        for c in range(KC):
            xT = act(lambda e, c=c: e.copy(xaT[:, c, :], bank[2 + c][:, :]), [tr[c], xT_done[0], xT_done[1]], "act_xT")
            bank_free[2 + c] = xT
        yield 2.0
        for i in range(TILES):
            bk = 2 + i // 2
            for c in range(KC):
                t = pe(lambda e, i=i, c=c, bk=bk: e.matmul(bank[bk][:, (i % 2) * DM:(i % 2 + 1) * DM], xaT[:, c, i * P:(i + 1) * P],
                                                           Wv_sb[:, c, :], start=(c == 0), stop=(c == KC - 1)),
                       [xT, w_att, bank_free[bk]], "pe_proj")
            if i % 2:
                v_ok = act(lambda e, i=i, bk=bk: e.copy(V_sb[:, i - 1:i + 1, :].rearrange("p a b -> p (a b)"), bank[bk][:, :]),
                           [t, V_free[0]], "act_v")
                bank_free[bk] = v_ok
            yield 2.0
        q_ready, k_ready = {}, {}

        def project_k(g):
            bk = MB
            for c in range(KC):
                t = pe(lambda e, c=c: e.matmul(bank[bk][:, :], Wk_sb[:, c, g * P:(g + 1) * P], xaT[:, c, :], start=(c == 0), stop=(c == KC - 1)),
                       [xT, bank_free[bk]], "pe_proj")
            hi = act(lambda e: e.activation(Kst[:, g % 2, 0, :], bank[bk][:, :], ACT.Copy, scale=HD ** -0.5), [t, K_free[g % 2]], "act_k")
            lo = dve(lambda e: e.scalar_tensor_tensor(Kst[:, g % 2, 1, :], bank[bk][:, :], HD ** -0.5, Kst[:, g % 2, 0, :].bitcast(fp32),
                                                      ALU.mult, ALU.subtract), [hi, K_free[g % 2]], "dve_k")
            bank_free[bk] = lo
            k_ready[g] = lo

        def project_q(pair):
            bk = MA
            for c in range(KC):
                t = pe(lambda e, c=c: e.matmul(bank[bk][:, :], Wq_sb[:, c, pair * P:(pair + 1) * P], xaT[:, c, :], start=(c == 0), stop=(c == KC - 1)),
                       [xT, bank_free[bk]], "pe_proj")
            for j in range(2):
                slot = (2 * pair + j) % RING_Q
                own, other = slice(j * HD, (j + 1) * HD), slice((1 - j) * HD, (2 - j) * HD)
                hi = act(lambda e, slot=slot, own=own: e.copy(Qst[own, slot, :], bank[bk][own, :]), [t, Q_free[slot]], "act_q")
                lo = dve(lambda e, slot=slot, own=own, other=other: e.tensor_tensor(
                    Qst[other, slot, :], bank[bk][own, :], Qst[own, slot, :].bitcast(fp32), ALU.subtract), [hi], "dve_q")
                q_ready[2 * pair + j] = lo
            bank_free[bk] = lo

        steps = [(h, i) for h in range(HEADS) for i in range(TILES)]
        p_ready, pt_ready = {}, {}
        av_last = {}
        project_k(0)
        yield 2.0
        project_q(0)
        yield 2.0
        LAG_T, LAG_AV = 2, 4
        for n in range(len(steps) + LAG_AV):
            if n < len(steps):
                h, i = steps[n]
                if i == 0 and h % 2 == 1 and h + 1 < HEADS:
                    if (h + 1) % HPG == 0:
                        project_k((h + 1) // HPG)
                    project_q((h + 1) // 2)
                g, slot, bk, r = h // HPG, h % RING_Q, n % 2, n % 3
                for part_ in range(2):
                    t = pe(lambda e, i=i, slot=slot, g=g, bk=bk, part_=part_: e.matmul(
                        bank[bk][:, :], Qst[:, slot, i * P:(i + 1) * P], Kst[:, g % 2, part_, :], start=(part_ == 0), stop=(part_ == 1)),
                        [q_ready[h], k_ready[g], bank_free[bk]], "pe_scores")
                if i == TILES - 1:
                    Q_free[slot] = t
                    if h % HPG == HPG - 1:
                        K_free[g % 2] = t
                q4 = n % 4
                mx = dve(lambda e, bk=bk, q4=q4: e.tensor_reduce(negmax[:, q4:q4 + 1], bank[bk][:, :], AX.X, ALU.max, negate=True), [t, stat_free[q4]], "dve_rowmax")
                ex = act(lambda e, bk=bk, q4=q4, r=r: e.activation(Pr[:, r, :], bank[bk][:, :], ACT.Exp, bias=negmax[:, q4:q4 + 1],
                                                                   accum_out=rowsum[:, q4:q4 + 1]), [mx, P_free[r], att_free[0]], "act_softmax")
                bank_free[bk] = ex
                rc = dve(lambda e, q4=q4: e.reciprocal(rowinv[:, q4:q4 + 1], rowsum[:, q4:q4 + 1]), [ex], "dve_softmax")
                nm = dve(lambda e, q4=q4, r=r: e.tensor_scalar(Pr[:, r, :], Pr[:, r, :], rowinv[:, q4:q4 + 1], None, ALU.mult), [rc], "dve_softmax")
                stat_free[q4] = nm
                p_ready[n] = nm
            m = n - LAG_T
            if 0 <= m < len(steps):
                r, bk = m % 3, 2 + m % 2
                for c in range(TILES):
                    t = pe(lambda e, r=r, bk=bk, c=c: e.transpose(bank[bk][:, c * P:(c + 1) * P], Pr[:, r, c * P:(c + 1) * P], ident[:, :]),
                           [p_ready[m], bank_free[bk], ident_ok], "pe_probT")
                P_free[r] = t
                pt_ready[m] = act(lambda e, r=r, bk=bk: e.copy(PT[:, r, :, :].rearrange("p a b -> p (a b)"), bank[bk][:, :]), [t, PT_free[r]], "act_probT")
                bank_free[bk] = pt_ready[m]
            m = n - LAG_AV
            if m >= 0:
                h, i = steps[m]
                r, g, j = m % 3, h // HPG, h % 2
                for c in range(TILES):
                    t = pe(lambda e, r=r, g=g, j=j, c=c, i=i: e.matmul(bank[4][j * HD:(j + 1) * HD, i * P:(i + 1) * P], V_sb[:, c, g * HD:(g + 1) * HD],
                                                                  PT[:, r, c, :], start=(c == 0), stop=(c == TILES - 1)),
                           [pt_ready[m], v_ok, bank_free[4]], "pe_av")
                PT_free[r] = t
                if j == 1 and i == TILES - 1:
                    a_ok = act(lambda e, h=h: e.copy(AT[:, h // 2, :], bank[4][:, :]), [t, AT_free[0], att_free[0]], "act_av")
                    bank_free[4] = a_ok
            yield 2.0
        V_free[0] = t
        xT_done[1] = t
        sl = b % 2
        for i in range(TILES):
            bk = 2 + i % 2
            for p in range(HEADS // 2):
                t = pe(lambda e, i=i, p=p, bk=bk: e.matmul(bank[bk][:, 0:DM], AT[:, p, i * P:(i + 1) * P], Wpost_sb[:, p, :],
                                                           start=(p == 0), stop=(p == HEADS // 2 - 1)), [a_ok, bank_free[bk]], "pe_post")
            sok = dve(lambda e, i=i, bk=bk: e.tensor_tensor(s_sb[:, sl, i, :], bank[bk][:, 0:DM], xa[:, i, :], ALU.add),
                      [t, s_free[sl], w_ok[0]], "dve_s")
            bank_free[bk] = sok
            yield 2.0
        AT_free[0] = t
        att_x[0] = sok
        s_ready[b] = sok

    att_x, V_free, AT_free = [None], [None], [None]
    Q_free, K_free, P_free, PT_free, stat_free = [None] * RING_Q, [None] * 2, [None] * 3, [None] * 3, [None] * 4

    ex_free = {}

    def experts():
        y_done = None
        F = lambda k: ex_free.get(k)
        for e_ in range(EXPERTS):
            r = e_ % 2
            BK = ((0, 1, 2), (5, 6, 7))[r]
            xl = load(xe[:, r, :, :], xbuf[e_ * CAP:(e_ + 1) * CAP, :].rearrange("(c p) d -> p c d", p=P), f"xe{r}", [scattered[0], w_ok[0], F(("xe", r))])
            wg = we[:, r, 0, :].rearrange("p (c i) -> p c i", c=KC)
            wu = we[:, r, 1, :].rearrange("p (c i) -> p c i", c=KC)
            wd = we[:, r, 2, :]
            for dst, src in ((wg, w_gate[e_].rearrange("(c p) i -> p c i", p=P)), (wu, w_up[e_].rearrange("(c p) i -> p c i", p=P)),
                             (wd, w_down[e_])):
                wl = load(dst, src, f"we{r}", [w_ok[0], F(("we", r))])
            for c in range(KC):
                for s in range(2):
                    t = pe(lambda e, BK=BK, c=c, s=s, r=r: e.transpose(bank[BK[0]][:, c * CAP + s * P:c * CAP + (s + 1) * P], xe[:, r, s, c * P:(c + 1) * P], ident[:, :]),
                           [xl, bank_free[BK[0]]], "pe_expert")
            ex_free[("xe", r)] = t
            xt = dve(lambda e, BK=BK, r=r: e.tensor_copy(xeT[:, r, :, :].rearrange("p a b -> p (a b)"), bank[BK[0]][:, :]), [t, F(("xeT", r))], "dve_expert")
            bank_free[BK[0]] = xt
            for j, w in enumerate((wg, wu)):
                for c in range(KC):
                    t = pe(lambda e, BK=BK, c=c, j=j, w=w, r=r: e.matmul(bank[BK[1]][:, j * CAP:(j + 1) * CAP], w[:, c, :], xeT[:, r, c, :],
                                                                  start=(c == 0), stop=(c == KC - 1)), [xt, wl, bank_free[BK[1]]], "pe_expert")
            ex_free[("xeT", r)] = t
            sl = act(lambda e, BK=BK, r=r: e.activation(sg[:, r, :], bank[BK[1]][:, 0:CAP], ACT.Silu), [t, F(("sg", r))], "act_expert")
            hh = dve(lambda e, BK=BK, r=r: e.tensor_tensor(he[:, r, :], bank[BK[1]][:, CAP:2 * CAP], sg[:, r, :], ALU.mult), [sl, F(("he", r))], "dve_expert")
            bank_free[BK[1]] = hh
            ex_free[("sg", r)] = hh
            yield 2.0
            for s in range(2):
                t = pe(lambda e, BK=BK, s=s, r=r, wd=wd: e.matmul(bank[BK[2]][:, s * DM:(s + 1) * DM], he[:, r, s * P:(s + 1) * P], wd, start=True, stop=True),
                       [hh, bank_free[BK[2]]], "pe_expert")
            ex_free[("he", r)] = ex_free[("we", r)] = t
            yk = act(lambda e, BK=BK, r=r: e.copy(ye[:, r, :, :].rearrange("p a b -> p (a b)"), bank[BK[2]][:, :]), [t, F(("ye", r))], "act_expert")
            bank_free[BK[2]] = yk
            ex_free[("ye", r)] = load(ybuf[e_ * CAP:(e_ + 1) * CAP, :].rearrange("(c p) d -> p c d", p=P), ye[:, r, :, :], f"y_out{r}", [yk], queue="act")
            yield 2.0
        y_stored[:] = [ex_free[("ye", 0)], ex_free[("ye", 1)]]

    y_stored = [None, None]
    x1_ready, xn1_ready, z_args = [None] * NB, [None] * NB, [None] * NB
    batch_free = [None] * 2
    row_free = [None] * RING_ROWS
    xc_free = [None]

    def combine(b):
        sl = b % 2
        z = dve(lambda e: e.memset(rows_sb[:, :, :], 0.0), [], "dve_combine") if b == 0 else None
        xl = load(x1[:, sl, :, :], X[b].rearrange("(t p) d -> p t d", p=P), f"x_comb{sl}", [batch_free[sl]])
        for i in range(TILES):
            t_ = b * TILES + i
            got = {}

            def gather(k, t_=t_, got=got):
                r = k % RING_ROWS
                got[k] = do("pool", lambda e: e.indirect_dma_start(
                    rows_sb[:, r, :], None, ybuf, bass.IndirectOffsetOnAxis(ap=slot_idx[:, t_, k:k + 1], axis=0),
                    bounds_check=SLOTS - 1, oob_is_err=False), y_stored + [row_free[r], z], f"gather{r}", 16)

            for k in range(RING_ROWS):
                gather(k)
            yield 2.0
            for k in range(TOPK):
                r = k % RING_ROWS
                if k == 0:
                    t = dve(lambda e, t_=t_, r=r, k=k: e.tensor_scalar(acc_sb[:, :], rows_sb[:, r, :], slot_w[:, t_, k:k + 1], None, ALU.mult),
                            [got[k], w_ok[0], xc_free[0]], "dve_combine")
                else:
                    t = dve(lambda e, t_=t_, r=r, k=k: e.scalar_tensor_tensor(acc_sb[:, :], rows_sb[:, r, :], slot_w[:, t_, k:k + 1], acc_sb[:, :],
                                                                         ALU.mult, ALU.add), [got[k], t], "dve_combine")
                row_free[r] = t
                if k + RING_ROWS < TOPK:
                    gather(k + RING_ROWS)
                    yield 2.0
            gk = act(lambda e: e.activation(gate_sb[:, :], acc_sb[:, :], ACT.Silu), [t], "act_combine")
            xc_free[0] = gk
            t = dve(lambda e, i=i: e.tensor_tensor(gate_sb[:, :], gate_sb[:, :], s_sb[:, sl, i, :], ALU.mult), [gk, s_ready[b]], "dve_combine")
            t = dve(lambda e, i=i: e.tensor_tensor(x1[:, sl, i, :], x1[:, sl, i, :], gate_sb[:, :], ALU.add), [t, xl], "dve_combine")
            xc_free[0] = t
            yield 2.0
        s_free[sl] = t
        x1_ready[b] = t
        st = statistics(x1[:, sl], lnm[:, sl, 0, :], lnm[:, sl, 1, :], [t], "x1")
        xn1_ready[b] = normalise(xn1, x1[:, sl], lnm[:, sl, 0, :], lnm[:, sl, 1, :], st + xn1_free)
        yield 2.0

    lnm = sb("lnm", [P, 2, 4, TILES])
    g1_ready = [None] * NB
    xn1_free = [None, None]
    wr_free = [None] * RING_W
    dec_free, msk_free, actb_free = [None] * 2, [None] * 3, [None] * 3

    def trees(b):
        sl = b % 2
        tr = transposed(xn1, [xn1_ready[b]], (2, 3))
        xn1_free[0] = tr[KC - 1]
        for c in range(KC):
            xT = act(lambda e, c=c: e.copy(xT1[:, c, :], bank[2 + c][:, :]), [tr[c], AT_free[0]], "act_tree")
            bank_free[2 + c] = xT
        yield 2.0
        n_units = 2 * TREES

        def size(w):
            half = w % 2
            return INNER if half == 0 else P, (w // 2) * NODES + half * INNER

        def fetch(w):
            m, lo = size(w)
            k = w % RING_W
            busy = [wr_free[k], V_free[0], xT_done[0], xT_done[1]]
            load(wr_in[k][:, :, 0:m], ffn_WinT[:, lo:lo + m].rearrange("(c p) n -> p c n", p=P), f"wr{k}", busy)
            fetched[w] = load(wr_out[k][0:m, :], ffn_WoutT[lo:lo + m, :], f"wr{k}", busy)

        def logits(w):
            m, lo = size(w)
            r, k, a3 = w // 2, w % 2, w % 3
            for c in range(KC):
                t = pe(lambda e, c=c, k=k, m=m, w=w: e.matmul(bank[k][0:m, :], wr_in[w % RING_W][:, c, 0:m], xT1[:, c, :], start=(c == 0), stop=(c == KC - 1)),
                       [xT, fetched[w], bank_free[k]], "pe_tree")
            a = act(lambda e, w=w, k=k, m=m, a3=a3: e.activation(act_sb[0:m, a3, :], bank[k][0:m, :], ACT.Silu, bias=ffn_b_sb[0:m, w:w + 1]),
                    [t, actb_free[a3], P_free[a3]], "act_tree")
            bank_free[k] = a
            acted[w] = a
            if w % 2 == 0:
                decided[r] = dve(lambda e, w=w, k=k, r=r: e.tensor_scalar(dec_sb[0:INNER, r % 2, :], bank[k][0:INNER, :], ffn_b_sb[0:INNER, w:w + 1], 0.0,
                                                                          ALU.add, ALU.is_gt), [a, dec_free[r % 2]], "dve_tree")
                bank_free[k] = decided[r]

        def mask(w):
            m, lo = size(w)
            r, half, a3 = w // 2, w % 2, w % 3
            t = pe(lambda e, r=r, half=half, m=m: e.matmul(bank[2][0:m, :], path_sb[0:INNER, half * P:half * P + m], dec_sb[0:INNER, r % 2, :],
                                                           start=True, stop=True), [decided[r], bank_free[2], path_ok], "pe_tree")
            if half == 1:
                dec_free[r % 2] = t
            mk = dve(lambda e, a3=a3, half=half, m=m: e.scalar_tensor_tensor(masked[0:m, a3, :], bank[2][0:m, :], need_sb[0:m, half:half + 1],
                                                                           act_sb[0:m, a3, :], ALU.is_ge, ALU.mult),
                     [t, acted[w], msk_free[a3], PT_free[a3]], "dve_tree")
            bank_free[2] = actb_free[a3] = mk
            mask_ready[w] = mk

        def project(w):
            m, lo = size(w)
            k, a3 = w % RING_W, w % 3
            for c in range(KC):
                t = pe(lambda e, w=w, c=c, m=m, k=k, a3=a3: e.matmul(bank[3 + c][:, :], wr_out[k][0:m, c * P:(c + 1) * P], masked[0:m, a3, :],
                                                                start=(w == 0), stop=(w == n_units - 1)), [mask_ready[w], bank_free[3 + c]], "pe_tree")
            msk_free[a3] = wr_free[k] = t
            return t

        fetched, acted, decided, mask_ready = {}, {}, {}, {}
        for w in range(RING_W - 2):
            fetch(w)
        for w in range(n_units + 2):
            if w < n_units:
                logits(w)
            if 0 <= w - 1 < n_units:
                mask(w - 1)
            if w >= 2:
                t = project(w - 2)
            if w + RING_W - 2 < n_units:
                fetch(w + RING_W - 2)
            yield 3.8
        for c in range(KC):
            o = act(lambda e, c=c: e.copy(oT[:, c, :], bank[3 + c][:, :]), [t, AT_free[0]], "act_tree")
            bank_free[3 + c] = o
        yield 2.0
        for i in range(TILES):
            bk = i // 2
            for c in range(KC):
                t = pe(lambda e, i=i, c=c, bk=bk: e.transpose(bank[bk][:, (i % 2) * DM + c * P:(i % 2) * DM + (c + 1) * P], oT[:, c, i * P:(i + 1) * P], ident[:, :]),
                       [o, bank_free[bk]], "pe_tree")
            if i % 2:
                gk = act(lambda e, i=i, bk=bk: e.activation(g1[:, sl, i - 1:i + 1, :].rearrange("p a b -> p (a b)"), bank[bk][:, :], ACT.Silu),
                         [t, batch_free[sl]], "act_tree")
                bank_free[bk] = gk
        AT_free[0] = t
        for k in range(3):
            P_free[k], PT_free[k] = actb_free[k], msk_free[k]
        V_free[0] = xT_done[0] = msk_free[(n_units - 1) % 3]
        g1_ready[b] = gk
        yield 2.0

    arena_free = [None]
    mz_free = [None]

    def mamba(b):
        sl = b % 2
        first = arena_free[0] if arena_free[0] else [scattered[0], w_ok[0]] + y_stored
        zz = hT.rearrange("p a (b c) -> p (a b) c", c=DM)
        st = statistics(xn1, lnm[:, sl, 2, :], lnm[:, sl, 3, :], [xn1_ready[b]], "xn1")
        z_sb = BC.rearrange("p a b s -> p (a b s)")[:, 0:TILES * DM].rearrange("p (t d) -> p t d", d=DM)
        nrm = normalise(z_sb, xn1, lnm[:, sl, 2, :], lnm[:, sl, 3, :], st + first)
        xn1_free[1] = nrm
        tr = transposed(z_sb, [nrm], (MA, MB))
        for c in range(KC):
            h_ok = act(lambda e, c=c: e.activation(hT[:, c, :], bank[MA + c][:, :], ACT.Identity, scale=ln_gb_sb[:, 0, c:c + 1], bias=ln_gb_sb[:, 1, c:c + 1]),
                       [tr[c]] + first, "act_ssm")
            bank_free[MA + c] = h_ok
        yield 2.0
        for cb in range(CB):
            bk = (MA, MB)[cb % 2]
            for c in range(KC):
                t = pe(lambda e, c=c, cb=cb, bk=bk: e.matmul(bank[bk][:, :], WinT_sb[:, c, cb * P:(cb + 1) * P], hT[:, c, :], start=(c == 0), stop=(c == KC - 1)),
                       [h_ok, w_ssm, bank_free[bk]], "pe_ssm")
            d = dve(lambda e, cb=cb, bk=bk: e.tensor_scalar(y_sb[:, cb, :], bank[bk][:, :], chan_sb[:, cb, DCONV - 1:DCONV], chan_sb[:, cb, DCONV:DCONV + 1],
                                                            ALU.mult, ALU.add), [t] + first, "dve_ssm")
            for j in range(1, DCONV):
                d = dve(lambda e, cb=cb, bk=bk, j=j: e.scalar_tensor_tensor(y_sb[:, cb, j:], bank[bk][:, 0:SEQ - j], chan_sb[:, cb, DCONV - 1 - j:DCONV - j],
                                                                            y_sb[:, cb, j:], ALU.mult, ALU.add), [d], "dve_ssm")
            bank_free[bk] = d
            xs_ok = act(lambda e, cb=cb: e.activation(xs[:, cb, :], y_sb[:, cb, :], ACT.Silu), [d, tr[1]], "act_ssm")
            yield 2.0
        for cb in range(CB):
            t = pe(lambda e, cb=cb: e.matmul(bank[MA][0:DTR + 2 * DS, :], WxT_sb[:, cb, :], xs[:, cb, :], start=(cb == 0), stop=(cb == CB - 1)),
                   [xs_ok, bank_free[MA]], "pe_ssm")
        xd_ok = act(lambda e: e.copy(xd[0:DTR + 2 * DS, :], bank[MA][0:DTR + 2 * DS, :]), [t, tr[1]], "act_ssm")
        bank_free[MA] = xd_ok
        bc_out = load(bc_dram[b], xd[DTR:DTR + 2 * DS, :], "bc_out", [xd_ok])
        bc_stores[:] = [bc_out]
        yield 2.0
        dt_read = None
        for cb in range(CB):
            bk = (MA, MB)[cb % 2]
            t = pe(lambda e, cb=cb, bk=bk: e.matmul(bank[bk][:, :], WdtT_sb[:, cb * P:(cb + 1) * P], xd[0:DTR, :], start=True, stop=True),
                   [xd_ok, bank_free[bk]], "pe_ssm")
            bdt = chan_sb[:, cb, DCONV + 1:DCONV + 2]
            a = act(lambda e, bk=bk, bdt=bdt: e.activation(sp_a[:, 0, :], bank[bk][:, :], ACT.Abs, bias=bdt), [t, dt_read] + first, "act_ssm")
            a = act(lambda e: e.activation(sp_a[:, 0, :], sp_a[:, 0, :], ACT.Exp, scale=-1.0), [a], "act_ssm")
            a = act(lambda e: e.activation(sp_a[:, 0, :], sp_a[:, 0, :], ACT.Ln, bias=1.0), [a], "act_ssm")
            d = dve(lambda e, cb=cb, bk=bk, bdt=bdt: e.tensor_scalar(dt_sb[:, cb, :], bank[bk][:, :], bdt, 0.0, ALU.add, ALU.max), [a] + first, "dve_ssm")
            bank_free[bk] = d
            dt_read = d = dve(lambda e, cb=cb: e.tensor_tensor(dt_sb[:, cb, :], dt_sb[:, cb, :], sp_a[:, 0, :], ALU.add), [d], "dve_ssm")
            u_ok = dve(lambda e, cb=cb: e.tensor_tensor(u_sb[:, cb, :], dt_sb[:, cb, :], xs[:, cb, :], ALU.mult), [d], "dve_ssm")
            y_ok = dve(lambda e, cb=cb: e.tensor_scalar(y_sb[:, cb, :], xs[:, cb, :], chan_sb[:, cb, DCONV + 2:DCONV + 3], None, ALU.mult), [xs_ok], "dve_ssm")
            yield 2.0
        last_bc = []
        yield "scan"
        bc_free = [[u_ok, y_ok, t, bc_out]] * HALF_STATES
        dA_free, st_free = [dt_read, dt_read], [None] * RING_S
        for rnd in range(2):
            bc_ok = []
            for n in range(HALF_STATES):
                src = bass.AP(bc_dram.tensor, bc_dram[b, rnd * HALF_STATES + n].offset, [[0, P], [DS * SEQ, 2], [1, SEQ]])
                bc_ok.append(load(BC[:, n, :, :], src, f"bc{n}", bc_free[n]))
            bc_free = [[]] * HALF_STATES
            todo = [(cb, n) for cb in range(CB) for n in range(HALF_STATES)]
            scanned, weighted, inputs_read = {}, {}, {}
            for k in range(len(todo) + LAG_S):
                if k < len(todo):
                    cb, n = todo[k]
                    r, w = k % 2, k % RING_S
                    s = rnd * HALF_STATES + n
                    ea = act(lambda e, cb=cb, s=s, r=r: e.activation(dA[:, r, :], dt_sb[:, cb, :], ACT.Exp, scale=A_sb[:, cb, s:s + 1]),
                             [dt_read, A_ok, dA_free[r]], "act_decay")
                    eb = pool(lambda e, cb=cb, n=n, w=w: e.tensor_tensor(st_sb[:, w, :], u_sb[:, cb, :], BC[:, n, 0, :], ALU.mult),
                              [u_ok, bc_ok[n], st_free[w]] + (first if k < RING_S else []), "pool_input")
                    sc = dve(lambda e, r=r, w=w: e.tensor_tensor_scan(st_sb[:, w, :], dA[:, r, :], st_sb[:, w, :], 0.0, ALU.mult, ALU.add), [ea, eb], "dve_scan")
                    dA_free[r] = sc
                    scanned[k] = sc
                    inputs_read[n] = eb
                m = k - LAG_C
                if 0 <= m < len(todo):
                    cb, n = todo[m]
                    w = m % RING_S
                    on_pool = n % 2 == 0
                    pr = (pool if on_pool else dve)(lambda e, w=w, n=n: e.tensor_tensor(st_sb[:, w, :], st_sb[:, w, :], BC[:, n, 1, :], ALU.mult),
                                                    [scanned[m], bc_ok[n]], "pool_output" if on_pool else "dve_output")
                    weighted[m] = pr
                    if cb == CB - 1:
                        bc_free[n] = [pr, inputs_read[n]]
                        last_bc += [pr, inputs_read[n]]
                m = k - LAG_S
                if m >= 0:
                    cb, n = todo[m]
                    w = m % RING_S
                    t = pe(lambda e, w=w, n=n: e.matmul(bank[MY][:, :], ident[:, :], st_sb[:, w, :], start=(n == 0), stop=(n == HALF_STATES - 1)),
                           [weighted[m], bank_free[MY]], "pe_states")
                    st_free[w] = t
                    if n == HALF_STATES - 1:
                        y_ok = dve(lambda e, cb=cb: e.tensor_tensor(y_sb[:, cb, :], bank[MY][:, :], y_sb[:, cb, :], ALU.add), [t, y_ok], "dve_y")
                        bank_free[MY] = y_ok
                yield 1.9
        for cb in range(CB):
            bk = (MA, MB)[cb % 2]
            for c in range(KC):
                t = pe(lambda e, c=c, cb=cb, bk=bk: e.matmul(bank[bk][:, :], WinT_sb[:, c, DI + cb * P:DI + (cb + 1) * P], hT[:, c, :], start=(c == 0), stop=(c == KC - 1)),
                       [bank_free[bk]], "pe_ssm")
            a = act(lambda e, bk=bk: e.activation(res_sb[:, :], bank[bk][:, :], ACT.Silu), [t, mz_free[0]] + first, "act_ssm")
            bank_free[bk] = a
            y_ok = mz_free[0] = dve(lambda e, cb=cb: e.tensor_tensor(y_sb[:, cb, :], y_sb[:, cb, :], res_sb[:, :], ALU.mult), [a, y_ok], "dve_y")
            yield 2.0
        d = y_ok
        for i in range(TILES):
            bk = (MA, MB)[i % 2]
            for cb in range(CB):
                t = pe(lambda e, i=i, cb=cb, bk=bk: e.matmul(bank[bk][:, 0:DM], y_sb[:, cb, i * P:(i + 1) * P], WoutT_sb[:, cb, :], start=(cb == 0), stop=(cb == CB - 1)),
                       [y_ok, bank_free[bk]], "pe_ssm")
            fin = res_sb[:, (i % 2) * DM:(i % 2 + 1) * DM]
            d0 = dve(lambda e, i=i, fin=fin: e.tensor_scalar(fin, x1[:, sl, i, :], lnm[:, sl, 0, i:i + 1], lnm[:, sl, 1, i:i + 1],
                                                        ALU.subtract, ALU.mult), [y_ok, d], "dve_y")
            d = dve(lambda e, i=i, bk=bk, fin=fin: e.scalar_tensor_tensor(fin, bank[bk][:, 0:DM], alpha_sb[:, 0:1], fin, ALU.mult, ALU.add), [t, d0, w_small], "dve_y")
            bank_free[bk] = d
            d = dve(lambda e, i=i, fin=fin: e.tensor_tensor(fin, fin, g1[:, sl, i, :], ALU.mult), [d, known(g1_ready[b])], "dve_y")
            d = dve(lambda e, i=i, fin=fin: e.tensor_tensor(x1[:, sl, i, :], x1[:, sl, i, :], fin, ALU.add), [d], "dve_y")
            yield 2.0
        stored = load(out[b].rearrange("(t p) d -> p t d", p=P), x1[:, sl, :, :], f"stored{sl}", [d])
        batch_free[sl] = stored
        final[sl] = stored
        arena_free[0] = [d, t, y_ok] + last_bc[-4:]
        yield 2.0

    final, bc_stores = [None, None], []

    def run(g):
        for _ in g:
            pass

    def together(a, b, share):
        credit = 0.0
        for cost in b:
            if cost == "scan":
                return
            credit += share * cost
            while credit > 0:
                cost = next(a, None)
                if cost is None:
                    break
                credit -= cost

    def chain(*gens):
        for g in gens:
            yield from g

    w_ssm = None
    for dst, src in ((WinT_sb, WinT), (WxT_sb, WxT), (WoutT_sb, WoutT)):
        w_ssm = load(dst[:, :, :], src.rearrange("(c p) n -> p c n", p=P), "w_ssm", queue="act")
    w_ssm = load(WdtT_sb[:, :], WdtT, "w_ssm", queue="act")
    AT_free[0] = path_ok
    ahead = chain(attention(0), attention(1))
    together(ahead, routing(), 3.0)
    run(scatter())
    run(ahead)
    run(experts())
    run(combine(0))
    for b in range(NB):
        layer, tree = mamba(b), trees(b)
        together(tree, layer, TREES_PER_PROJECTION)
        run(tree)
        beside = chain(*([combine(b + 1)] if b + 1 < NB else []), *([attention(b + 2)] if b + 2 < NB else []))
        together(beside, layer, ATTENTION_PER_SCAN)
        run(beside)
        run(layer)

    block = ctx.enter_context(nc.Block())

    @block.sync
    def _(e):
        run_queue("sp", e)
        for sem, value in final + bc_stores:
            e.wait_ge(sems[sem], value)

    @block.scalar
    def _(e):
        run_queue("act", e)

    @block.vector
    def _(e):
        run_queue("dve", e)

    @block.gpsimd
    def _(e):
        run_queue("pool", e)

    @block.tensor
    def _(e):
        run_queue("pe", e)

    ctx.close()


def host_layout(d):
    f = np.float32
    chunk = lambda v: v.reshape(-1, P).T
    path, need = np.zeros((INNER, 2 * P), f), np.zeros((P, 2), f)
    for node in range(NODES):
        col = node if node < INNER else P + node - INNER
        v = node
        while v > 0:
            up = (v - 1) // 2
            path[up, col] = 1.0 if v == 2 * up + 2 else -1.0
            need[col % P, col // P] += v == 2 * up + 2
            v = up
    ffn_b = np.zeros((P, 2 * TREES), f)
    for r in range(TREES):
        ffn_b[:INNER, 2 * r] = d["L1_ffn_b_in"][r * NODES:r * NODES + INNER]
        ffn_b[:, 2 * r + 1] = d["L1_ffn_b_in"][r * NODES + INNER:(r + 1) * NODES]
    block = lambda v: v.reshape(CB, P, -1).transpose(1, 0, 2)
    chan = np.concatenate([block(d["L1_attn_conv_w"].reshape(DI, DCONV)), block(d["L1_attn_conv_b"]),
                           block(d["L1_attn_b_dt"]), block(d["L1_attn_D_param"])], axis=2)
    before = np.tril(np.ones((EG, EG), f), -1)
    return {
        "X": d["L0_attn_X"], "Wq": d["L0_attn_Wq"], "Wk": d["L0_attn_Wk"], "Wv": d["L0_attn_Wv"], "Wpost": d["L0_attn_Wpost"],
        "gateT": d["L0_ffn_gate_w"].T, "gate_bias": d["L0_ffn_gate_bias"], "w_gate": d["L0_ffn_w_gate"], "w_up": d["L0_ffn_w_up"],
        "w_down": d["L0_ffn_w_down"],
        "ln_gb": np.stack([chunk(d["L1_attn_ln_g"]), chunk(d["L1_attn_ln_b"])], axis=1),
        "WinT": d["L1_attn_W_in"].T, "WxT": d["L1_attn_W_x"].T, "WdtT": d["L1_attn_W_dt"].T, "WoutT": d["L1_attn_W_out"].T,
        "chan": chan, "A_log": block(d["L1_attn_A_log"]), "alpha": d["L1_attn_alpha"],
        "ffn_WinT": d["L1_ffn_W_in"].T, "ffn_b": ffn_b, "ffn_WoutT": d["L1_ffn_W_out"].T,
        "path": path, "need": need, "tri": np.triu(np.ones((P, P), f), 1), "glt": before.reshape(-1),
        "slot_base": (np.arange(EXPERTS) * CAP + 1).astype(f),
    }


def kernel(**inputs):
    import concourse.bacc as bacc
    from concourse.bass_utils import run_bass_kernel_spmd

    nc = bacc.Bacc("TRN2", target_bir_lowering=False, num_devices=1)
    arrays = {f"in_{n}": np.ascontiguousarray(a) for n, a in host_layout({k: np.asarray(v) for k, v in inputs.items()}).items()}
    aps = {n[3:]: nc.dram_tensor(n, a.shape, mybir.dt.from_np(a.dtype), kind="ExternalInput").ap() for n, a in arrays.items()}
    out = nc.dram_tensor("out_x", [NB, SEQ, DM], mybir.dt.float32, kind="ExternalOutput").ap()
    build_program(nc, out=out, **aps)
    result = run_bass_kernel_spmd(nc, [arrays], core_ids=[0])
    return result.results[0]["out_x"]
```

```python
import concourse.bass as bass
from concourse import mybir
from contextlib import ExitStack
import numpy as np

NB, SEQ, DM = 8, 512, 256
P = 128
TILES = SEQ // P
NT = NB * TILES
KC = DM // P
HEADS, GROUPS, HD = 16, 4, 64
HPG = HEADS // GROUPS
EXPERTS, EG, TOPG, TOPK, CAP = 64, 8, 4, 8, 256
EPG = EXPERTS // EG
SLOTS = EXPERTS * CAP
ROUTE_SCALE = 2.5
DI, DS, DTR, DCONV = 512, 16, 64, 4
CB = DI // P
TREES, DEPTH = 8, 7
NODES = 2 ** (DEPTH + 1) - 1
INNER = 2 ** DEPTH - 1
HALF_STATES = DS // 2
EPS = 1e-5
ROUTE_TILES = SEQ // EXPERTS
RING_Q, RING_P, RING_STAT = 3, 3, 4
LAG_MAX, LAG_EXP, LAG_NORM, LAG_T, LAG_AV = 1, 2, 3, 4, 6
NORM_TURN = 4
RING_E, LAG_WIDEN, LAG_NARROW = 5, 1, 2
RING_ROWS, LAG_ROWS = 4, 2
RING_DA, RING_S = 3, 8
LAG_SCAN, LAG_C, LAG_ADD, LAG_S = 2, 3, 4, 5
ARENA = 20992
FIRST_AHEAD, ATTENTION_PER_ROUTING = 1, 0.6
SECOND_AHEAD, ATTENTION_PER_EXPERTS, WEIGHTS_PER_EXPERTS, ATTENTION_PER_COMBINE = 45, 0.25, 0.6, 0.6
COMBINE_PER_OTHERS, COMBINE_PER_TREES, OTHERS_PER_LAYER = 0.22, 0.6, 1.95
BIG = 3.0e38
GONE = 65536.0


def build_program(nc, X, Wq, Wk, Wv, Wpost, gateT, gate_bias, w_gate, w_up, w_down, ln_gb, WinT, WxT, WdtT,
                  WoutT, chan, A_log, alpha, ffn_WinT, ffn_b, ffn_WoutT, path, need, tri, glt, slot_base, out):
    fp32, f32r, bf16 = mybir.dt.float32, mybir.dt.float32r, mybir.dt.bfloat16
    i32 = mybir.dt.int32
    ALU, ACT, AX = mybir.AluOpType, mybir.ActivationFunctionType, mybir.AxisListType

    ctx = ExitStack()
    queues = {n: [] for n in ("pe", "act", "dve", "pool", "sp")}
    sems, counts = {}, {}

    def semaphore(name):
        if name not in sems:
            sems[name] = ctx.enter_context(nc.semaphore(name))
            counts[name] = 0
        return sems[name]

    def do(engine, emit, after=(), signal=None, by=1):
        target = semaphore(signal) if signal else None
        queues[engine].append((emit, [a for a in after if a is not None], target, by))
        if signal:
            counts[signal] += by
            return (signal, counts[signal])
        return None

    def pe(emit, after=(), signal=None):
        return do("pe", emit, after, signal)

    def act(emit, after=(), signal=None):
        return do("act", emit, after, signal)

    def dve(emit, after=(), signal=None):
        return do("dve", emit, after, signal)

    def pool(emit, after=(), signal=None):
        return do("pool", emit, after, signal)

    def load(dst, src, signal, after=(), queue="sp"):
        return do(queue, lambda e: e.dma_start(dst, src), after, signal, 16)

    def run_queue(name, engine):
        reached = {}
        for emit, after, target, by in queues[name]:
            for sem, value in after:
                if reached.get(sem, 0) < value:
                    engine.wait_ge(sems[sem], value)
                    reached[sem] = value
            ins = emit(engine)
            if target is not None:
                ins.then_inc(target, by)

    def known(token):
        assert token is not None, "its producer must be queued first"
        return token

    def sb(name, shape, dt=fp32):
        return ctx.enter_context(nc.sbuf_tensor(name, shape, dt))

    xbuf = nc.dram_tensor("xbuf", [SLOTS, DM], fp32, kind="Internal").ap()
    ybuf = nc.dram_tensor("ybuf", [SLOTS, DM], fp32, kind="Internal").ap()
    bc_dram = nc.dram_tensor("bc_dram", [NB, 2 * DS, SEQ], fp32, kind="Internal").ap()

    ident = sb("ident", [P, P])
    tri_sb, ones_sb = sb("tri_sb", [P, P], bf16), sb("ones_sb", [P, P], bf16)
    path_sb = sb("path_sb", [P, 2 * P], bf16)
    need_sb = sb("need_sb", [P, 2])
    ffn_b_sb = sb("ffn_b_sb", [P, 2 * TREES])
    ln_gb_sb = sb("ln_gb_sb", [P, 2, KC])
    chan_sb = sb("chan_sb", [P, CB, DCONV + 3])
    A_sb = sb("A_sb", [P, CB, DS])
    alpha_sb = sb("alpha_sb", [P, 1])
    mhalf = sb("mhalf", [P, 1])
    Wq_sb = sb("Wq_sb", [P, KC, HEADS * HD])
    Wk_sb = sb("Wk_sb", [P, KC, GROUPS * 2 * HD])
    Wv_sb = sb("Wv_sb", [P, KC, GROUPS * HD])
    Wpost_sb = sb("Wpost_sb", [P, HEADS // 2, DM])
    WinT_sb = sb("WinT_sb", [P, KC, 2 * DI])
    WxT_sb = sb("WxT_sb", [P, CB, DTR + 2 * DS])
    WdtT_sb = sb("WdtT_sb", [DTR, DI])
    WoutT_sb = sb("WoutT_sb", [P, CB, DM])
    stats0 = sb("stats0", [P, NT, 2])
    slot_idx = sb("slot_idx", [P, NT, TOPK], i32)
    slot_w = sb("slot_w", [P, NT, TOPK])
    s_sb = sb("s_sb", [P, 2, TILES, DM])
    xaT = sb("xaT", [P, KC, SEQ])
    Kst = sb("Kst", [P, 2, 2, SEQ], f32r)
    Qst = sb("Qst", [P, RING_Q, SEQ], f32r)
    V_sb = sb("V_sb", [P, TILES, GROUPS * HD])
    Pr = sb("Pr", [P, RING_P, SEQ])
    PT = sb("PT", [P, RING_P, TILES, P])
    AT = sb("AT", [P, HEADS // 2, SEQ])
    negmax, rowsum, rowinv = (sb(n, [P, RING_STAT]) for n in ("negmax", "rowsum", "rowinv"))
    rows_sb = sb("rows_sb", [P, RING_ROWS, DM])
    acc_sb = sb("acc_sb", [P, DM])
    x1 = sb("x1", [P, 2, TILES, DM])
    xn1 = sb("xn1", [P, TILES, DM])
    bst, bag = sb("bst", [P, TILES, 6]), sb("bag", [P, TILES, 2])
    rst = sb("rst", [P, TILES])
    g1 = sb("g1", [P, 2, TILES, DM])
    tree_in = [v.rearrange("p (b c) -> p b c", c=P) for v in (V_sb[:, 0, :], V_sb[:, 1, :], xaT[:, 0, 0:DM], xaT[:, 0, DM:SEQ])]
    tree_out = [V_sb[:, 2, :], V_sb[:, 3, :], xaT[:, 1, 0:DM], xaT[:, 1, DM:SEQ]]
    arena = sb("arena", [P, ARENA])
    at = [0]

    def part(name, *dims, base=None):
        n = int(np.prod(dims))
        if base is not None:
            at[0] = base
        v = arena[:, at[0]:at[0] + n]
        if len(dims) == 2:
            v = v.rearrange("p (a b) -> p a b", b=dims[1])
        elif len(dims) == 3:
            v = v.rearrange("p (a b c) -> p a b c", b=dims[1], c=dims[2])
        at[0] += n
        assert at[0] <= ARENA, (name, at[0])
        return v

    hT = part("hT", KC, SEQ, base=0)
    dt_sb, u_sb, y_sb = part("dt", CB, SEQ), part("u", CB, SEQ), part("y", CB, SEQ)
    BC = part("BC", HALF_STATES, 2, SEQ)
    dA, st_sb = part("dA", RING_DA, SEQ), part("st", RING_S, SEQ)
    xs = BC.rearrange("p a b s -> p (a b) s")[:, 0:CB, :]
    xd = BC.rearrange("p a b s -> p (a b) s")[:, CB, :]
    slots_bc = BC.rearrange("p a b s -> p (a b) s")
    soft = slots_bc[:, CB + 1:2 * CB + 1, :]
    res_sb, fin_sb = slots_bc[:, 0:CB, :], slots_bc[:, CB:CB + 2, :].rearrange("p a (b c) -> p (a b) c", c=DM)
    xn_all = part("xn_all", NT, DM, base=0)
    RT = [part(f"route{i}", NT, EXPERTS) for i in range(5)]
    xe = part("xe", RING_E, 2, DM, base=0)
    xeT = part("xeT", 2, KC, CAP)
    we = part("we", RING_E, 3, 2 * P)
    sg = part("sg", 2, CAP)
    assert at[0] <= NT * DM
    he = part("he", 2, CAP, base=NT * DM + NT * EXPERTS)
    ye = part("ye", 2, 2, DM)
    route0_end = NT * DM + 5 * NT * EXPERTS
    gw_sb = arena[:, route0_end:route0_end + KC * EXPERTS].rearrange("p (a b) -> p a b", b=EXPERTS)
    bias_sb = arena[:, route0_end + 128:route0_end + 192]
    base_sb = arena[:, route0_end + 192:route0_end + 256]
    glt_sb = arena[:, route0_end + 256:route0_end + 320].rearrange("p (a b) -> p a b", b=EG)
    zrows = arena[:, route0_end + 320:route0_end + 320 + NT * EXPERTS]
    assert route0_end + 320 + NT * EXPERTS <= ARENA
    act_sb = AT[:, 4:8, :]
    masked = [Pr[:, 0, :], Pr[:, 1, :], Pr[:, 2, :], PT[:, 0, :, :].rearrange("p b c -> p (b c)")]
    dec_sb = PT[:, 1, :, :].rearrange("p b c -> p (b c)").bitcast(bf16).rearrange("p (a b) -> p a b", b=SEQ)
    xT1 = AT[:, 0:KC, :]
    oT = AT[:, KC:2 * KC, :]

    bank = [ctx.enter_context(nc.psum_tensor(f"bank{i}", [P, SEQ], fp32)) for i in range(8)]
    PROBT, AV, PROJ = 3, 4, 5
    MA, MB = 6, 7
    MY = MB
    bank_free = [None] * 8

    def broadcast(src, n):
        return bass.AP(src.tensor, src.offset, [[0, P], [1, n]])

    def load_x(b):
        return load(xn_all[:, b * TILES:(b + 1) * TILES, :], X[b].rearrange("(t p) d -> p t d", p=P), f"x_in{b}")

    x_loaded = [load_x(0)]
    w_first = load(gw_sb, gateT.rearrange("(c p) e -> p c e", p=P), "w_first")
    for dst, src in ((bias_sb, broadcast(gate_bias, EXPERTS)), (base_sb, broadcast(slot_base, EXPERTS)),
                     (glt_sb.rearrange("p a b -> p (a b)"), broadcast(glt, EG * EG))):
        w_first = load(dst, src, "w_first")
    stage = AT.rearrange("p a b -> p (a b)")
    w_small = load(stage[:, 0:P], tri, "w_small")
    for dst, src in ((stage[0:INNER, P:3 * P], path), (need_sb[:, :], need), (ffn_b_sb[:, :], ffn_b),
                     (ln_gb_sb[:, :, :], ln_gb), (chan_sb[:, :, :], chan), (A_sb[:, :, :], A_log),
                     (alpha_sb[:, :], broadcast(alpha, 1))):
        w_small = load(dst, src, "w_small")
    x_loaded += [load_x(b) for b in range(1, NB)]
    w_att = None
    for c in range(KC):
        for half in range(2):
            dst = Wk_sb[:, c, :].rearrange("p (g t d) -> p g t d", t=2, d=HD)[:, :, half, :]
            w_att = load(dst, Wk[c * P:(c + 1) * P, :].rearrange("p (g d) -> p g d", d=HD), "w_att", queue="act")
    for dst, src in ((Wq_sb, Wq), (Wv_sb, Wv), (Wpost_sb, Wpost)):
        w_att = load(dst[:, :, :], src.rearrange("(c p) n -> p c n", p=P), "w_att", queue="act")

    blank_ok = pool(lambda e: e.memset(ident[:, :], 0.0), signal="pool_const")
    ident_ok = pool(lambda e: e.affine_select(out=ident[:, :], in_=ident[:, :], compare_op=ALU.not_equal, fill=1.0, base=0,
                                              pattern=[[-1, P]], channel_multiplier=1), [blank_ok], "pool_const")
    pool(lambda e: e.memset(ones_sb[:, :], 1.0), signal="pool_const")
    const_ok = pool(lambda e: e.memset(mhalf[:, :], -0.5), signal="pool_const")
    zero_ok = dve(lambda e: e.memset(zrows, 0.0), signal="dve_const")
    ROWS_Z = NT * EXPERTS // DM
    for i in range(SLOTS // (P * ROWS_Z)):
        zeroed = load(xbuf[i * P * ROWS_Z:(i + 1) * P * ROWS_Z, :].rearrange("(p r) d -> p (r d)", p=P), zrows, "zeroed", [zero_ok])

    def statistics(src, mean_of, inv_of, after, last=[None]):
        t = None
        for i in range(TILES):
            t = dve(lambda e, i=i: e.bn_stats(bst[:, i, :], src[:, i, :]), list(after) + [last[0]], "dve_stats")
        for i in range(TILES):
            t = dve(lambda e, i=i: e.bn_aggr(bag[:, i, :], bst[:, i, :]), [t], "dve_stats")
        t = dve(lambda e: e.tensor_scalar(rst[:, :], bag[:, :, 1], EPS, None, ALU.add), [t], "dve_stats")
        m = dve(lambda e: e.tensor_copy(mean_of, bag[:, :, 0]), [t], "dve_stats")
        r = pool(lambda e: e.tensor_tensor(inv_of, rst[:, :], mhalf[:, 0:1].broadcast_to([P, TILES]), ALU.pow), [t, const_ok], "pool_rsqrt")
        last[0] = r
        return [m, r]

    def normalise(dst, src, mean_of, inv_of, after):
        for i in range(TILES):
            t = dve(lambda e, i=i: e.tensor_scalar(dst[:, i, :], src[:, i, :], mean_of[:, i:i + 1], inv_of[:, i:i + 1],
                                                   ALU.subtract, ALU.mult), after, "dve_norm")
        return t

    def transposed(src, after, banks):
        out_t = []
        for c in range(KC):
            for i in range(TILES):
                t = pe(lambda e, c=c, i=i: e.transpose(bank[banks[c]][:, i * P:(i + 1) * P], src[:, i, c * P:(c + 1) * P], ident[:, :]),
                       list(after) + [bank_free[banks[c]], ident_ok], "pe_transposed")
            out_t.append(t)
        return out_t

    scores = RT[0]
    logits_done = [None, None]
    xn_ready, scored_x = [], []
    for b in range(NB):
        xin = xn_all[:, b * TILES:(b + 1) * TILES, :]
        mean_v, inv_v = stats0[:, b * TILES:(b + 1) * TILES, 0], stats0[:, b * TILES:(b + 1) * TILES, 1]
        st = statistics(xin, mean_v, inv_v, [x_loaded[b]])
        nrm = normalise(xin, xin, mean_v, inv_v, st)
        xn_ready.append(nrm)
        tr = transposed(xin, [nrm], (0 + 2 * (b % 2), 1 + 2 * (b % 2)))
        xT = (xaT, AT[:, KC:2 * KC, :])[b % 2]
        for c in range(KC):
            bk = c + 2 * (b % 2)
            cp = act(lambda e, c=c, bk=bk, xT=xT: e.copy(xT[:, c, :], bank[bk][:, :]), [tr[c], logits_done[b % 2]], "act_xT")
            bank_free[bk] = cp
        for i in range(TILES):
            for c in range(KC):
                t = pe(lambda e, i=i, c=c, b=b, xT=xT: e.matmul(bank[4 + b % 2][:, i * EXPERTS:(i + 1) * EXPERTS], xT[:, c, i * P:(i + 1) * P],
                                                                gw_sb[:, c, :], start=(c == 0), stop=(c == KC - 1)),
                       [cp, w_first, bank_free[4 + b % 2]], "pe_logits")
        logits_done[b % 2] = t
        scored_x.append(act(lambda e, b=b: e.activation(scores[:, b * TILES:(b + 1) * TILES, :].rearrange("p a b -> p (a b)"),
                                                bank[4 + b % 2][:, 0:TILES * EXPERTS], ACT.Sigmoid), [t], "act_scores"))
        bank_free[4 + b % 2] = scored_x[b]

    tri_ok = dve(lambda e: e.tensor_copy(tri_sb[:, :], stage[:, 0:P]), [w_small], "dve_const")
    path_ok = dve(lambda e: e.tensor_copy(path_sb[0:INNER, :], stage[0:INNER, P:3 * P]), [w_small], "dve_const")

    def wide(src, dims):
        return bass.AP(src.tensor, src.offset, [list(src.ap[0])] + [list(d) for d in dims])

    ROWS = ROUTE_TILES * EG
    small = g1.rearrange("p a b c -> p (a b c)")
    assert NT * EG * 6 + (NT // ROUTE_TILES + 1) * EXPERTS <= 2 * TILES * DM
    carry_at = NT * EG * 6
    chain_ok = [None]

    def step(emit, after=()):
        chain_ok[0] = dve(emit, [chain_ok[0]] + list(after), "dve_route")
        return chain_ok[0]

    def routing(part_):
        t0, t1 = part_ * ROUTE_TILES, (part_ + 1) * ROUTE_TILES
        T = ROUTE_TILES
        scores, sfc, R1, R2, R3 = (v[:, t0:t1, :] for v in RT)
        flat = "p a b -> p (a b)"
        narrow = [small[:, (part_ * 6 + i) * ROWS:(part_ * 6 + i + 1) * ROWS] for i in range(6)]
        m1, m2, n1, gsum, gpen = narrow[:5]
        K8 = narrow[5].rearrange("p (a b) -> p a b", b=TOPK)
        carry = [small[:, carry_at + (part_ + i) * EXPERTS:carry_at + (part_ + i + 1) * EXPERTS] for i in range(2)]
        G8 = "p a (g k) -> p (a g) k"
        sfc4 = sfc.rearrange(G8, k=EPG)
        step(lambda e: e.tensor_tensor(sfc, scores, wide(bias_sb, [[0, T], [1, EXPERTS]]), ALU.add), [scored_x[(t1 - 1) // TILES], w_first])
        step(lambda e: e.tensor_reduce(m1, sfc4, AX.X, ALU.max))
        step(lambda e: e.tensor_tensor(R1.rearrange(G8, k=EPG), sfc4, wide(m1, [[1, ROWS], [0, EPG]]), ALU.is_equal))
        step(lambda e: e.tensor_reduce(n1, R1.rearrange(G8, k=EPG), AX.X, ALU.add))
        yield 2.2
        step(lambda e: e.scalar_tensor_tensor(R1, R1, -BIG, sfc, ALU.mult, ALU.add))
        step(lambda e: e.tensor_reduce(m2, R1.rearrange(G8, k=EPG), AX.X, ALU.max))
        step(lambda e: e.tensor_scalar(n1, n1, 2.0, -BIG, ALU.is_lt, ALU.mult))
        step(lambda e: e.tensor_tensor(n1, n1, m1, ALU.add))
        step(lambda e: e.tensor_tensor(m2, m2, n1, ALU.max))
        step(lambda e: e.tensor_tensor(gsum, m1, m2, ALU.add))
        yield 2.2
        gj = wide(gsum, [[EG, T], [0, EG], [1, EG]])
        gi = wide(gsum, [[EG, T], [1, EG], [0, EG]])
        r4 = "p a (i j) -> p a i j"
        step(lambda e: e.tensor_tensor(R1.rearrange(r4, j=EG), gj, gi, ALU.is_equal))
        step(lambda e: e.tensor_tensor(R1, R1, wide(glt_sb, [[0, T], [1, EG * EG]]), ALU.mult))
        step(lambda e: e.tensor_tensor(R2.rearrange(r4, j=EG), gj, gi, ALU.is_gt))
        step(lambda e: e.tensor_tensor(R1, R1, R2, ALU.add))
        yield 2.2
        step(lambda e: e.tensor_reduce(gpen, R1.rearrange("p a (i j) -> p (a i) j", j=EG), AX.X, ALU.add))
        step(lambda e: e.tensor_scalar(gpen, gpen, float(TOPG), -BIG, ALU.is_ge, ALU.mult))
        step(lambda e: e.tensor_tensor(sfc4, sfc4, wide(gpen, [[1, ROWS], [0, EPG]]), ALU.add))
        yield 2.2
        for t in range(T):
            step(lambda e, t=t: e.max(K8[:, t, :], sfc[:, t, :]))
        for t in range(T):
            step(lambda e, t=t: e.match_replace(R1[:, t, :], K8[:, t, :], sfc[:, t, :], -3.4e38))
        sel_b = R3.rearrange(flat)[:, 0:T * EXPERTS // 2].bitcast(bf16)
        sel3 = sel_b.rearrange("p (a b) -> p a b", b=EXPERTS)
        sel_ok = step(lambda e: e.tensor_tensor(sel3, R1, sfc, ALU.not_equal))
        yield 2.2
        tot = sfc.rearrange(flat).rearrange("p (b a) -> p a b", a=T)
        for j, (w, ok) in enumerate(((tri_sb, tri_ok), (ones_sb, const_ok))):
            t = pe(lambda e, j=j, w=w: e.matmul(bank[6 + j][:, :], w[:, :], sel_b, start=True, stop=True),
                   [sel_ok, ok, bank_free[6 + j]], "pe_positions")
            dst = (R1 if j == 0 else tot)
            bank_free[6 + j] = step(lambda e, j=j, dst=dst: e.tensor_copy(dst, bank[6 + j].rearrange("p (a b) -> p a b", b=EXPERTS)), [t])
        keep = R2.rearrange(flat)
        pre = x1.rearrange("p a b c -> p (a b c)")[:, part_ * T * EXPERTS:(part_ + 1) * T * EXPERTS]
        by_tile = pre.rearrange("p (b a) -> p a b", a=T)
        step(lambda e: e.memset(keep, 1.0))
        step(lambda e: e.memset(keep.rearrange("p (b a) -> p b a", a=T)[:, :, 0:1], 0.0))
        if part_ == 0:
            step(lambda e: e.memset(carry[0], 0.0))
        step(lambda e: e.tensor_tensor_scan(pre, keep, sfc.rearrange(flat), 0.0, ALU.mult, ALU.add))
        step(lambda e: e.tensor_tensor(carry[1], carry[0], by_tile[:, T - 1, :], ALU.add))
        step(lambda e: e.tensor_tensor(pre, pre, sfc.rearrange(flat), ALU.subtract))
        yield 2.2
        step(lambda e: e.tensor_tensor(R1, R1, by_tile, ALU.add))
        step(lambda e: e.tensor_tensor(R1, R1, wide(carry[0], [[0, T], [1, EXPERTS]]), ALU.add))
        step(lambda e: e.scalar_tensor_tensor(R2, R1, float(CAP), sel3, ALU.is_lt, ALU.mult))
        step(lambda e: e.tensor_tensor(R1, R1, wide(base_sb, [[0, T], [1, EXPERTS]]), ALU.add))
        step(lambda e: e.tensor_tensor(R1, R1, R2, ALU.mult))
        for t in range(T):
            step(lambda e, t=t: e.max(K8[:, t, :], R1[:, t, :]))
        yield 2.2
        idx = m1.rearrange("p (a b) -> p a b", b=TOPK)
        step(lambda e: e.tensor_scalar(idx, K8, 0.0, GONE, ALU.is_equal, ALU.mult))
        step(lambda e: e.scalar_tensor_tensor(idx, K8, -1.0, idx, ALU.add, ALU.add))
        idx_ok[part_] = step(lambda e: e.tensor_copy(slot_idx[:, t0:t1, :], idx))
        yield 2.2

    def weights(part_):
        t0, t1 = part_ * ROUTE_TILES, (part_ + 1) * ROUTE_TILES
        T = ROUTE_TILES
        scores, sfc, R1, R2, R3 = (v[:, t0:t1, :] for v in RT)
        den = small[:, part_ * 6 * ROWS:part_ * 6 * ROWS + T]
        K8 = small[:, (part_ * 6 + 5) * ROWS:(part_ * 6 + 6) * ROWS].rearrange("p (a b) -> p a b", b=TOPK)
        sel3 = R3.rearrange("p a b -> p (a b)")[:, 0:T * EXPERTS // 2].bitcast(bf16).rearrange("p (a b) -> p a b", b=EXPERTS)
        step(lambda e: e.tensor_tensor(scores, scores, sel3, ALU.mult))
        step(lambda e: e.tensor_reduce(den, scores, AX.X, ALU.add))
        step(lambda e: e.tensor_scalar(den, den, 1e-20, None, ALU.add))
        step(lambda e: e.reciprocal(den, den))
        step(lambda e: e.tensor_scalar(den, den, ROUTE_SCALE, None, ALU.mult))
        step(lambda e: e.tensor_tensor(scores, scores, wide(den, [[1, T], [0, EXPERTS]]), ALU.mult))
        step(lambda e: e.tensor_tensor(scores, scores, R2, ALU.mult))
        yield 2.2
        for k in range(TOPK):
            step(lambda e, k=k: e.tensor_tensor(R2, R1, wide(K8[:, :, k:k + 1], [[TOPK, T], [0, EXPERTS]]), ALU.is_equal))
            step(lambda e: e.tensor_tensor(R2, R2, scores, ALU.mult))
            w_ok[0] = step(lambda e, k=k: e.tensor_reduce(slot_w[:, t0:t1, k], R2, AX.X, ALU.add))
            yield 1.7

    idx_ok, w_ok = {}, [None]

    def scatter(part_):
        for t in range(part_ * ROUTE_TILES, (part_ + 1) * ROUTE_TILES):
            for k in range(TOPK):
                scattered[0] = do("pool", lambda e, t=t, k=k: e.indirect_dma_start(
                    xbuf, bass.IndirectOffsetOnAxis(ap=slot_idx[:, t, k:k + 1], axis=0), xn_all[:, t, :], None,
                    bounds_check=SLOTS - 1, oob_is_err=False), [idx_ok[part_], xn_ready[t // TILES], zeroed], "scattered", 16)

    scattered = [None]

    xT_done = [t, None]
    s_ready, s_free = [None] * NB, [None] * 2
    att_free = [t]

    def attention(b):
        sl = b % 2
        xa = s_sb[:, sl]
        xl = load(xa, X[b].rearrange("(t p) d -> p t d", p=P), f"x_att{sl}", [s_free[sl] if b < 2 else known(s_free[sl])])
        mean_v, inv_v = stats0[:, b * TILES:(b + 1) * TILES, 0], stats0[:, b * TILES:(b + 1) * TILES, 1]
        nrm = normalise(xa, xa, mean_v, inv_v, [xl, xn_ready[b]])
        tr = transposed(xa, [nrm], (2, 3))
        for c in range(KC):
            xT = act(lambda e, c=c: e.copy(xaT[:, c, :], bank[2 + c][:, :]), [tr[c], xT_done[0], xT_done[1]], "act_xT")
            bank_free[2 + c] = xT
        yield 2.0
        for i in range(TILES):
            bk = 2 + i // 2
            for c in range(KC):
                t = pe(lambda e, i=i, c=c, bk=bk: e.matmul(bank[bk][:, (i % 2) * DM:(i % 2 + 1) * DM], xaT[:, c, i * P:(i + 1) * P],
                                                           Wv_sb[:, c, :], start=(c == 0), stop=(c == KC - 1)),
                       [xT, w_att, bank_free[bk]], "pe_proj")
            if i % 2:
                v_ok = act(lambda e, i=i, bk=bk: e.copy(V_sb[:, i - 1:i + 1, :].rearrange("p a b -> p (a b)"), bank[bk][:, :]),
                           [t, V_free[0]], "act_v")
                bank_free[bk] = v_ok
            yield 2.0
        q_ready, k_ready = {}, {}

        def product_k(g):
            for c in range(KC):
                t = pe(lambda e, c=c: e.matmul(bank[PROJ][:, :], Wk_sb[:, c, g * P:(g + 1) * P], xaT[:, c, :], start=(c == 0), stop=(c == KC - 1)),
                       [xT, bank_free[PROJ]], "pe_proj")
            product[0] = t

        def high_k(g):
            product[0] = act(lambda e: e.activation(Kst[:, g % 2, 0, :], bank[PROJ][:, :], ACT.Copy, scale=HD ** -0.5), [product[0], K_free[g % 2]], "act_k")

        def low_k(g):
            k_ready[g] = bank_free[PROJ] = dve(lambda e: e.scalar_tensor_tensor(
                Kst[:, g % 2, 1, :], bank[PROJ][:, :], HD ** -0.5, Kst[:, g % 2, 0, :].bitcast(fp32), ALU.mult, ALU.subtract), [product[0]], "dve_k")

        def product_q(pair):
            for c in range(KC):
                t = pe(lambda e, c=c: e.matmul(bank[PROJ][:, :], Wq_sb[:, c, pair * P:(pair + 1) * P], xaT[:, c, :], start=(c == 0), stop=(c == KC - 1)),
                       [xT, bank_free[PROJ]], "pe_proj")
            product[0] = t

        def halves(pair):
            for j in range(2):
                yield 2 * pair + j, (2 * pair + j) % RING_Q, slice(j * HD, (j + 1) * HD), slice((1 - j) * HD, (2 - j) * HD)

        def high_q(pair):
            for h, slot, own, other in halves(pair):
                hi = act(lambda e, slot=slot, own=own: e.copy(Qst[own, slot, :], bank[PROJ][own, :]), [product[0], Q_free[slot]], "act_q")
            product[0] = hi

        def low_q(pair):
            for h, slot, own, other in halves(pair):
                q_ready[h] = bank_free[PROJ] = dve(lambda e, slot=slot, own=own, other=other: e.tensor_tensor(
                    Qst[other, slot, :], bank[PROJ][own, :], Qst[own, slot, :].bitcast(fp32), ALU.subtract), [product[0]], "dve_q")

        product = [None]
        plan = {}
        for h in range(0, HEADS - 2, 2):
            pair, at_step = h // 2 + 1, h * TILES
            if (h + 2) % HPG == 0:
                for j, make in enumerate((product_k, high_k, low_k)):
                    plan[at_step + j] = (make, (h + 2) // HPG)
            for j, make in ((3, product_q), (4, high_q), (5, low_q)):
                plan[at_step + j] = (make, pair)
        steps = [(h, i) for h in range(HEADS) for i in range(TILES)]
        p_ready, pt_ready = {}, {}
        av_last = {}
        for make in (product_k, high_k, low_k, product_q, high_q, low_q):
            make(0)
            yield 1.5
        scored, maxed, exps = {}, {}, {}
        for n in range(len(steps) + LAG_AV):
            if n < len(steps):
                h, i = steps[n]
                g, slot, bk = h // HPG, h % RING_Q, n % 3
                for part_ in range(2):
                    t = pe(lambda e, i=i, slot=slot, g=g, bk=bk, part_=part_: e.matmul(
                        bank[bk][:, :], Qst[:, slot, i * P:(i + 1) * P], Kst[:, g % 2, part_, :], start=(part_ == 0), stop=(part_ == 1)),
                        [q_ready[h], k_ready[g], bank_free[bk]], "pe_scores")
                if i == TILES - 1:
                    Q_free[slot] = t
                    if h % HPG == HPG - 1:
                        K_free[g % 2] = t
                scored[n] = t
                if n in plan:
                    make, which = plan[n]
                    make(which)
            m = n - LAG_MAX
            if 0 <= m < len(steps):
                maxed[m] = dve(lambda e, bk=m % 3, q4=m % RING_STAT: e.tensor_reduce(negmax[:, q4:q4 + 1], bank[bk][:, :], AX.X, ALU.max, negate=True),
                               [scored[m], stat_free[m % RING_STAT]], "dve_rowmax")
            m = n - LAG_EXP
            if 0 <= m < len(steps):
                exps[m] = bank_free[m % 3] = act(lambda e, bk=m % 3, q4=m % RING_STAT, r=m % RING_P: e.activation(
                    Pr[:, r, :], bank[bk][:, :], ACT.Exp, bias=negmax[:, q4:q4 + 1], accum_out=rowsum[:, q4:q4 + 1]),
                    [maxed[m], P_free[m % RING_P], att_free[0]], "act_softmax")
            m = n - LAG_NORM
            if 0 <= m < len(steps):
                rc = dve(lambda e, q4=m % RING_STAT: e.reciprocal(rowinv[:, q4:q4 + 1], rowsum[:, q4:q4 + 1]), [exps[m]], "dve_softmax")
                if m % NORM_TURN:
                    p_ready[m] = stat_free[m % RING_STAT] = dve(lambda e, q4=m % RING_STAT, r=m % RING_P: e.tensor_scalar(
                        Pr[:, r, :], Pr[:, r, :], rowinv[:, q4:q4 + 1], None, ALU.mult), [rc], "dve_softmax")
                else:
                    p_ready[m] = stat_free[m % RING_STAT] = act(lambda e, q4=m % RING_STAT, r=m % RING_P: e.activation(
                        Pr[:, r, :], Pr[:, r, :], ACT.Identity, scale=rowinv[:, q4:q4 + 1]), [rc], "act_norm")
            m = n - LAG_T
            if 0 <= m < len(steps):
                r, bk = m % RING_P, PROBT
                for c in range(TILES):
                    t = pe(lambda e, r=r, bk=bk, c=c: e.transpose(bank[bk][:, c * P:(c + 1) * P], Pr[:, r, c * P:(c + 1) * P], ident[:, :]),
                           [p_ready[m], bank_free[bk], ident_ok], "pe_probT")
                P_free[r] = t
                pt_ready[m] = act(lambda e, r=r, bk=bk: e.copy(PT[:, r, :, :].rearrange("p a b -> p (a b)"), bank[bk][:, :]), [t, PT_free[r]], "act_probT")
                bank_free[bk] = pt_ready[m]
            m = n - LAG_AV
            if m >= 0:
                h, i = steps[m]
                r, g, j = m % RING_P, h // HPG, h % 2
                for c in range(TILES):
                    t = pe(lambda e, r=r, g=g, j=j, c=c, i=i: e.matmul(bank[AV][j * HD:(j + 1) * HD, i * P:(i + 1) * P], V_sb[:, c, g * HD:(g + 1) * HD],
                                                                  PT[:, r, c, :], start=(c == 0), stop=(c == TILES - 1)),
                           [pt_ready[m], v_ok, bank_free[AV]], "pe_av")
                PT_free[r] = t
                if j == 1 and i == TILES - 1:
                    a_ok = act(lambda e, h=h: e.copy(AT[:, h // 2, :], bank[AV][:, :]), [t, AT_free[0], att_free[0]], "act_av")
                    bank_free[AV] = a_ok
            yield 2.0
        V_free[0] = t
        xT_done[1] = t
        for i in range(TILES):
            bk = 2 + i % 2
            for p in range(HEADS // 2):
                t = pe(lambda e, i=i, p=p, bk=bk: e.matmul(bank[bk][:, 0:DM], AT[:, p, i * P:(i + 1) * P], Wpost_sb[:, p, :],
                                                           start=(p == 0), stop=(p == HEADS // 2 - 1)), [a_ok, bank_free[bk]], "pe_post")
            yield 3.5
            sok = dve(lambda e, i=i, bk=bk: e.tensor_tensor(xa[:, i, :], bank[bk][:, 0:DM], xa[:, i, :], ALU.add), [t], "dve_s")
            bank_free[bk] = sok
        AT_free[0] = t
        s_ready[b] = sok

    V_free, AT_free = [None], [None]
    Q_free, K_free, P_free, PT_free, stat_free = [None] * RING_Q, [None] * 2, [None] * RING_P, [None] * RING_P, [None] * RING_STAT

    ex_free = {}

    def experts():
        F = lambda k: ex_free.get(k)
        loaded, turned, hidden = {}, {}, {}
        start = [scattered[0]]

        def fetch(n):
            r = n % RING_E
            xl = load(xe[:, r, :, :], xbuf[n * CAP:(n + 1) * CAP, :].rearrange("(c p) d -> p c d", p=P), f"xe{r}", start + [F(("xe", r))])
            for j, src in enumerate((w_gate[n], w_up[n])):
                load(we[:, r, j, :].rearrange("p (c i) -> p c i", c=KC), src.rearrange("(c p) i -> p c i", p=P), f"we{r}", start + [F(("we", r))])
            loaded[n] = [xl, load(we[:, r, 2, :], w_down[n], f"we{r}", start + [F(("we", r))])]

        def turn(n):
            r, k, EX = n % RING_E, n % 2, MA
            for c in range(KC):
                for s in range(2):
                    t = pe(lambda e, c=c, s=s: e.transpose(bank[EX][:, c * CAP + s * P:c * CAP + (s + 1) * P], xe[:, r, s, c * P:(c + 1) * P], ident[:, :]),
                           [loaded[n][0], bank_free[EX]], "pe_expert")
            ex_free[("xe", r)] = t
            turned[n] = bank_free[EX] = dve(lambda e: e.tensor_copy(xeT[:, k, :, :].rearrange("p a b -> p (a b)"), bank[EX][:, :]),
                                            [t, F(("xeT", k))], "dve_expert")

        def widen(n):
            r, k = n % RING_E, n % 2
            bk = MB
            for j in range(2):
                w = we[:, r, j, :].rearrange("p (c i) -> p c i", c=KC)
                for c in range(KC):
                    t = pe(lambda e, c=c, j=j, w=w: e.matmul(bank[bk][:, j * CAP:(j + 1) * CAP], w[:, c, :], xeT[:, k, c, :],
                                                             start=(c == 0), stop=(c == KC - 1)), [turned[n], loaded[n][1], bank_free[bk]], "pe_expert")
            ex_free[("xeT", k)] = t
            gated = act(lambda e: e.activation(sg[:, k, :], bank[bk][:, 0:CAP], ACT.Silu), [t, F(("sg", k))], "act_expert")
            hidden[n] = bank_free[bk] = ex_free[("sg", k)] = dve(lambda e: e.tensor_tensor(he[:, k, :], bank[bk][:, CAP:2 * CAP], sg[:, k, :], ALU.mult),
                                                                 [gated, F(("he", k))], "dve_expert")

        def narrow(n):
            r, k, EX = n % RING_E, n % 2, MA
            for s in range(2):
                t = pe(lambda e, s=s: e.matmul(bank[EX][:, s * DM:(s + 1) * DM], he[:, k, s * P:(s + 1) * P], we[:, r, 2, :], start=True, stop=True),
                       [hidden[n], bank_free[EX]], "pe_expert")
            ex_free[("he", k)] = ex_free[("we", r)] = t
            yk = bank_free[EX] = act(lambda e: e.copy(ye[:, k, :, :].rearrange("p a b -> p (a b)"), bank[EX][:, :]), [t, F(("ye", k))], "act_expert")
            ex_free[("ye", k)] = load(ybuf[n * CAP:(n + 1) * CAP, :].rearrange("(c p) d -> p c d", p=P), ye[:, k, :, :], f"y_out{k}", [yk], queue="act")

        for n in range(RING_E):
            fetch(n)
        for n in range(EXPERTS + LAG_NARROW):
            if n < EXPERTS:
                turn(n)
            if LAG_WIDEN <= n < EXPERTS + LAG_WIDEN:
                widen(n - LAG_WIDEN)
            if n >= LAG_NARROW:
                narrow(n - LAG_NARROW)
            if LAG_NARROW <= n < EXPERTS + LAG_NARROW - RING_E:
                fetch(n + RING_E - LAG_NARROW)
            yield 3.0
        y_stored[:] = [ex_free[("ye", 0)], ex_free[("ye", 1)]]

    y_stored = [None, None]
    xn1_ready = [None] * NB
    batch_free = [None] * 2
    row_free = [None] * RING_ROWS
    acc_free = [None]

    def combine(b):
        sl = b % 2
        z = dve(lambda e: e.memset(rows_sb[:, :, :], 0.0), [], "dve_combine") if b == 0 else None
        xl = load(x1[:, sl, :, :], X[b].rearrange("(t p) d -> p t d", p=P), f"x_comb{sl}", [batch_free[sl], w_ok[0]])
        parts = [(i, k) for i in range(TILES) for k in range(TOPK)]
        got = {}
        for n in range(len(parts) + LAG_ROWS):
            m = n - LAG_ROWS
            if m >= 0:
                i, k = parts[m]
                r, weight = m % RING_ROWS, slot_w[:, b * TILES + i, k:k + 1]
                if k == 0:
                    t = dve(lambda e, r=r, weight=weight: e.tensor_scalar(acc_sb[:, :], rows_sb[:, r, :], weight, None, ALU.mult),
                            [got[m], w_ok[0], acc_free[0]], "dve_combine")
                else:
                    t = dve(lambda e, r=r, weight=weight: e.scalar_tensor_tensor(acc_sb[:, :], rows_sb[:, r, :], weight, acc_sb[:, :], ALU.mult, ALU.add),
                            [got[m], t], "dve_combine")
                row_free[r] = t
            if n < len(parts):
                i, k = parts[n]
                r = n % RING_ROWS
                got[n] = do("pool", lambda e, r=r, index=slot_idx[:, b * TILES + i, k:k + 1]: e.indirect_dma_start(
                    rows_sb[:, r, :], None, ybuf, bass.IndirectOffsetOnAxis(ap=index, axis=0),
                    bounds_check=SLOTS - 1, oob_is_err=False), y_stored + [row_free[r], z], f"gather{r}", 16)
            yield 1.5
            if m >= 0 and parts[m][1] == TOPK - 1:
                i = parts[m][0]
                gk = act(lambda e: e.activation(acc_sb[:, :], acc_sb[:, :], ACT.Silu), [t], "act_combine")
                t = dve(lambda e, i=i: e.tensor_tensor(acc_sb[:, :], acc_sb[:, :], s_sb[:, sl, i, :], ALU.mult), [gk, s_ready[b]], "dve_combine")
                t = acc_free[0] = dve(lambda e, i=i: e.tensor_tensor(x1[:, sl, i, :], x1[:, sl, i, :], acc_sb[:, :], ALU.add), [t, xl], "dve_combine")
        s_free[sl] = t
        st = statistics(x1[:, sl], lnm[:, sl, 0, :], lnm[:, sl, 1, :], [t])
        yield 2.0
        xn1_ready[b] = normalise(xn1, x1[:, sl], lnm[:, sl, 0, :], lnm[:, sl, 1, :], st + xn1_free)
        yield 2.0

    lnm = sb("lnm", [P, 2, 4, TILES])
    g1_ready = [None] * NB
    xn1_free = [None, None]
    tree_w_free = {(kind, r): None for kind in ("in", "out") for r in range(2)}
    dec_free, masked_free, act_free = [None] * 2, [None] * 4, [None] * 4

    def trees(b):
        sl = b % 2
        tr = transposed(xn1, [xn1_ready[b]], (2, 3))
        xn1_free[0] = tr[KC - 1]
        for c in range(KC):
            xT = act(lambda e, c=c: e.copy(xT1[:, c, :], bank[2 + c][:, :]), [tr[c], AT_free[0]], "act_tree")
            bank_free[2 + c] = xT
        yield 2.0
        width = (INNER, P)

        def fetch(kind, r):
            for half, m in enumerate(width):
                k, lo = 2 * (r % 2) + half, r * NODES + half * INNER
                busy = [tree_w_free[kind, r % 2], V_free[0], xT_done[0], xT_done[1]]
                if kind == "in":
                    fetched[kind, r] = load(tree_in[k][:, :, 0:m], ffn_WinT[:, lo:lo + m].rearrange("(c p) n -> p c n", p=P), f"tree_in{r % 2}", busy)
                else:
                    fetched[kind, r] = load(tree_out[k][0:m, :], ffn_WoutT[lo:lo + m, :], f"tree_out{r % 2}", busy)

        def logits(r, half):
            k, m = 2 * (r % 2) + half, width[half]
            for c in range(KC):
                t = pe(lambda e, c=c: e.matmul(bank[half][0:m, :], tree_in[k][:, c, 0:m], xT1[:, c, :], start=(c == 0), stop=(c == KC - 1)),
                       [xT, fetched["in", r], bank_free[half]], "pe_tree")
            product[half] = tree_w_free["in", r % 2] = t

        def activate(r):
            for half, m in enumerate(width):
                k = 2 * (r % 2) + half
                acted[r, half] = bank_free[half] = act(lambda e, half=half, k=k, m=m: e.activation(
                    act_sb[0:m, k, :], bank[half][0:m, :], ACT.Silu, bias=ffn_b_sb[0:m, 2 * r + half:2 * r + half + 1]),
                    [product[half], act_free[k], AT_free[0]], "act_tree")
            decided[r] = bank_free[0] = dve(lambda e: e.tensor_scalar(dec_sb[0:INNER, r % 2, :], bank[0][0:INNER, :], ffn_b_sb[0:INNER, 2 * r:2 * r + 1], 0.0,
                                                                      ALU.add, ALU.is_gt), [acted[r, 0], dec_free[r % 2]] + PT_free, "dve_tree")

        def mask(r, half):
            k, m = 2 * (r % 2) + half, width[half]
            t = dec_free[r % 2] = pe(lambda e: e.matmul(bank[2][0:m, :], path_sb[0:INNER, half * P:half * P + m], dec_sb[0:INNER, r % 2, :],
                                                        start=True, stop=True), [decided[r], bank_free[2], path_ok], "pe_tree")
            masked_ok[r, half] = bank_free[2] = act_free[k] = dve(lambda e: e.scalar_tensor_tensor(
                masked[k][0:m, :], bank[2][0:m, :], need_sb[0:m, half:half + 1], act_sb[0:m, k, :], ALU.is_ge, ALU.mult),
                [t, acted[r, half], masked_free[k]] + P_free + PT_free, "dve_tree")

        def project(r):
            for half, m in enumerate(width):
                k = 2 * (r % 2) + half
                for c in range(KC):
                    t = pe(lambda e, c=c, k=k, m=m, half=half: e.matmul(
                        bank[3 + c][:, :], tree_out[k][0:m, c * P:(c + 1) * P], masked[k][0:m, :], start=(r == 0 and half == 0),
                        stop=(r == TREES - 1 and half == 1)), [masked_ok[r, half], fetched["out", r], bank_free[3 + c]], "pe_tree")
                masked_free[k] = t
            tree_w_free["out", r % 2] = t
            return t

        fetched, product, acted, decided, masked_ok = {}, {}, {}, {}, {}
        for r in range(2):
            fetch("in", r)
            fetch("out", r)
        for r in range(TREES + 1):
            if r >= 1:
                mask(r - 1, 0)
            if r < TREES:
                logits(r, 0)
            if r >= 1:
                mask(r - 1, 1)
            if r < TREES:
                logits(r, 1)
                activate(r)
                if r + 2 < TREES:
                    fetch("in", r + 2)
            yield 3.8
            if r >= 1:
                t = project(r - 1)
                if r + 1 < TREES:
                    fetch("out", r + 1)
            yield 3.8
        for c in range(KC):
            o = act(lambda e, c=c: e.copy(oT[:, c, :], bank[3 + c][:, :]), [t, AT_free[0]], "act_tree")
            bank_free[3 + c] = o
        yield 2.0
        for i in range(TILES):
            bk = i // 2
            for c in range(KC):
                t = pe(lambda e, i=i, c=c, bk=bk: e.transpose(bank[bk][:, (i % 2) * DM + c * P:(i % 2) * DM + (c + 1) * P], oT[:, c, i * P:(i + 1) * P], ident[:, :]),
                       [o, bank_free[bk]], "pe_tree")
            if i % 2:
                gk = act(lambda e, i=i, bk=bk: e.activation(g1[:, sl, i - 1:i + 1, :].rearrange("p a b -> p (a b)"), bank[bk][:, :], ACT.Silu),
                         [t, batch_free[sl]], "act_tree")
                bank_free[bk] = gk
        AT_free[0] = t
        P_free[:], PT_free[:] = [masked_free[3]] * len(P_free), [masked_free[3]] * len(PT_free)
        V_free[0] = xT_done[0] = masked_free[3]
        g1_ready[b] = gk
        yield 2.0

    arena_free = [None]

    def mamba(b):
        sl = b % 2
        tensor_idle = b >= NB - 2
        first = arena_free[0] if arena_free[0] else [scattered[0], w_ok[0]] + y_stored
        st = statistics(xn1, lnm[:, sl, 2, :], lnm[:, sl, 3, :], [xn1_ready[b]])
        yield 2.0
        z_sb = BC.rearrange("p a b s -> p (a b s)")[:, 0:TILES * DM].rearrange("p (t d) -> p t d", d=DM)
        nrm = normalise(z_sb, xn1, lnm[:, sl, 2, :], lnm[:, sl, 3, :], st + first)
        xn1_free[1] = nrm
        yield 2.0
        tr = transposed(z_sb, [nrm], (MA, MB))
        for c in range(KC):
            h_ok = act(lambda e, c=c: e.activation(hT[:, c, :], bank[MA + c][:, :], ACT.Identity, scale=ln_gb_sb[:, 0, c:c + 1], bias=ln_gb_sb[:, 1, c:c + 1]),
                       [tr[c]] + first, "act_ssm")
            bank_free[MA + c] = h_ok
        yield 3.0
        for cb in range(CB):
            bk = (MA, MB)[cb % 2]
            for c in range(KC):
                t = pe(lambda e, c=c, cb=cb, bk=bk: e.matmul(bank[bk][:, :], WinT_sb[:, c, cb * P:(cb + 1) * P], hT[:, c, :], start=(c == 0), stop=(c == KC - 1)),
                       [h_ok, w_ssm, bank_free[bk]], "pe_ssm")
            d = dve(lambda e, cb=cb, bk=bk: e.tensor_scalar(y_sb[:, cb, :], bank[bk][:, :], chan_sb[:, cb, DCONV - 1:DCONV], chan_sb[:, cb, DCONV:DCONV + 1],
                                                            ALU.mult, ALU.add), [t] + first, "dve_ssm")
            for j in range(1, DCONV):
                d = dve(lambda e, cb=cb, bk=bk, j=j: e.scalar_tensor_tensor(y_sb[:, cb, j:], bank[bk][:, 0:SEQ - j], chan_sb[:, cb, DCONV - 1 - j:DCONV - j],
                                                                            y_sb[:, cb, j:], ALU.mult, ALU.add), [d], "dve_ssm")
            bank_free[bk] = d
            yield 2.0
        for cb in range(CB):
            xs_ok = act(lambda e, cb=cb: e.activation(xs[:, cb, :], y_sb[:, cb, :], ACT.Silu), [d, tr[1]], "act_ssm")
        yield 4.0
        for cb in range(CB):
            t = pe(lambda e, cb=cb: e.matmul(bank[MA][0:DTR + 2 * DS, :], WxT_sb[:, cb, :], xs[:, cb, :], start=(cb == 0), stop=(cb == CB - 1)),
                   [xs_ok, bank_free[MA]], "pe_ssm")
        xd_ok = act(lambda e: e.copy(xd[0:DTR + 2 * DS, :], bank[MA][0:DTR + 2 * DS, :]), [t, tr[1]], "act_ssm")
        bank_free[MA] = xd_ok
        bc_out = load(bc_dram[b], xd[DTR:DTR + 2 * DS, :], "bc_out", [xd_ok])
        bc_stores[:] = [bc_out]
        yield 3.0
        for cb in range(CB):
            bk = (MA, MB)[cb % 2]
            t = pe(lambda e, cb=cb, bk=bk: e.matmul(bank[bk][:, :], WdtT_sb[:, cb * P:(cb + 1) * P], xd[0:DTR, :], start=True, stop=True),
                   [xd_ok, bank_free[bk]], "pe_ssm")
            bdt = chan_sb[:, cb, DCONV + 1:DCONV + 2]
            a = act(lambda e, cb=cb, bk=bk, bdt=bdt: e.activation(soft[:, cb, :], bank[bk][:, :], ACT.Abs, bias=bdt), [t, tr[1]], "act_ssm")
            d = dve(lambda e, cb=cb, bk=bk, bdt=bdt: e.tensor_scalar(dt_sb[:, cb, :], bank[bk][:, :], bdt, 0.0, ALU.add, ALU.max), [a] + first, "dve_ssm")
            bank_free[bk] = d
            y_ok = dve(lambda e, cb=cb: e.tensor_scalar(y_sb[:, cb, :], xs[:, cb, :], chan_sb[:, cb, DCONV + 2:DCONV + 3], None, ALU.mult), [xs_ok], "dve_ssm")
            yield 1.0
        whole = lambda v: v.rearrange("p a b -> p (a b)")
        a = act(lambda e: e.activation(whole(soft), whole(soft), ACT.Exp, scale=-1.0), [a], "act_ssm")
        a = act(lambda e: e.activation(whole(soft), whole(soft), ACT.Ln, bias=1.0), [a], "act_ssm")
        yield 4.0
        dt_read = dve(lambda e: e.tensor_tensor(whole(dt_sb), whole(dt_sb), whole(soft), ALU.add), [d, a], "dve_ssm")
        u_ok = dve(lambda e: e.tensor_tensor(whole(u_sb), whole(dt_sb), whole(xs), ALU.mult), [dt_read], "dve_ssm")
        yield 2.0
        last_bc = []
        bc_free = [[u_ok, y_ok, t, bc_out]] * HALF_STATES
        dA_free, st_free = [dt_read] * RING_DA, [None] * RING_S
        steps = [(rnd, cb, n) for rnd in range(2) for cb in range(CB) for n in range(HALF_STATES)]
        bc_ok, inputs, decays, scanned, weighted, added = [None] * HALF_STATES, {}, {}, {}, {}, {}
        for k in range(len(steps) + LAG_S):
            if k < len(steps):
                rnd, cb, n = steps[k]
                r, w, s = k % RING_DA, k % RING_S, rnd * HALF_STATES + n
                if cb == 0:
                    src = bass.AP(bc_dram.tensor, bc_dram[b, s].offset, [[0, P], [DS * SEQ, 2], [1, SEQ]])
                    bc_ok[n] = load(BC[:, n, :, :], src, f"bc{n}", bc_free[n])
                decays[k] = act(lambda e, cb=cb, s=s, r=r: e.activation(dA[:, r, :], dt_sb[:, cb, :], ACT.Exp, scale=A_sb[:, cb, s:s + 1]),
                                [dt_read, A_ok, dA_free[r]], "act_decay")
                inputs[k] = pool(lambda e, cb=cb, n=n, w=w: e.tensor_tensor(st_sb[:, w, :], u_sb[:, cb, :], BC[:, n, 0, :], ALU.mult),
                                 [u_ok, bc_ok[n], st_free[w]] + (first if k < RING_S else []), "pool_input")
            m = k - LAG_SCAN
            if 0 <= m < len(steps):
                r, w = m % RING_DA, m % RING_S
                scanned[m] = dA_free[r] = dve(lambda e, r=r, w=w: e.tensor_tensor_scan(st_sb[:, w, :], dA[:, r, :], st_sb[:, w, :], 0.0, ALU.mult, ALU.add),
                                              [decays[m], inputs[m]], "dve_scan")
            m = k - LAG_C
            if 0 <= m < len(steps):
                rnd, cb, n = steps[m]
                w, on_pool = m % RING_S, n % 2 == 0 and not tensor_idle
                weighted[m] = (pool if on_pool else dve)(lambda e, w=w, n=n: e.tensor_tensor(st_sb[:, w, :], st_sb[:, w, :], BC[:, n, 1, :], ALU.mult),
                                                         [scanned[m], bc_ok[n]], "pool_output" if on_pool else "dve_output")
                if cb == CB - 1:
                    bc_free[n] = [weighted[m], inputs[m]]
                    if rnd == 1:
                        last_bc += bc_free[n]
            m = k - LAG_ADD
            if 0 <= m < len(steps) and m % 2 and not tensor_idle:
                w, v = m % RING_S, (m - 1) % RING_S
                added[m] = st_free[w] = dve(lambda e, v=v, w=w: e.tensor_tensor(st_sb[:, v, :], st_sb[:, v, :], st_sb[:, w, :], ALU.add),
                                            [weighted[m - 1], weighted[m]], "dve_pair")
            m = k - LAG_S
            if m >= 0 and (m % 2 or tensor_idle):
                rnd, cb, n = steps[m]
                v = (m if tensor_idle else m - 1) % RING_S
                t = st_free[v] = pe(lambda e, v=v, n=n: e.matmul(bank[MY][:, :], ident[:, :], st_sb[:, v, :], start=(n == (not tensor_idle)), stop=(n == HALF_STATES - 1)),
                                    [weighted[m] if tensor_idle else added[m], bank_free[MY]], "pe_states")
                if n == HALF_STATES - 1:
                    y_ok = dve(lambda e, cb=cb: e.tensor_tensor(y_sb[:, cb, :], bank[MY][:, :], y_sb[:, cb, :], ALU.add), [t, y_ok], "dve_y")
                    bank_free[MY] = y_ok
            yield 1.9
        for pair in range(CB // 2):
            for cb in (2 * pair, 2 * pair + 1):
                bk = (MA, MB)[cb % 2]
                for c in range(KC):
                    t = pe(lambda e, c=c, cb=cb, bk=bk: e.matmul(bank[bk][:, :], WinT_sb[:, c, DI + cb * P:DI + (cb + 1) * P], hT[:, c, :],
                                                                start=(c == 0), stop=(c == KC - 1)), [bank_free[bk]], "pe_ssm")
                bank_free[bk] = t
            yield 2.0
            for cb in (2 * pair, 2 * pair + 1):
                bk = (MA, MB)[cb % 2]
                a = bank_free[bk] = act(lambda e, cb=cb, bk=bk: e.activation(res_sb[:, cb, :], bank[bk][:, :], ACT.Silu), [t] + last_bc, "act_ssm")
        yield 2.0
        y_ok = d = dve(lambda e: e.tensor_tensor(whole(y_sb), whole(y_sb), whole(res_sb), ALU.mult), [a, y_ok], "dve_y")
        yield 3.0
        for i in range(TILES):
            bk = (MA, MB)[i % 2]
            for cb in range(CB):
                t = pe(lambda e, i=i, cb=cb, bk=bk: e.matmul(bank[bk][:, 0:DM], y_sb[:, cb, i * P:(i + 1) * P], WoutT_sb[:, cb, :], start=(cb == 0), stop=(cb == CB - 1)),
                       [y_ok, bank_free[bk]], "pe_ssm")
            fin = fin_sb[:, i, :]
            d = dve(lambda e, i=i, fin=fin: e.tensor_scalar(fin, x1[:, sl, i, :], lnm[:, sl, 0, i:i + 1], lnm[:, sl, 1, i:i + 1],
                                                            ALU.subtract, ALU.mult), last_bc, "dve_y")
            d = dve(lambda e, i=i, bk=bk, fin=fin: e.scalar_tensor_tensor(fin, bank[bk][:, 0:DM], alpha_sb[:, 0:1], fin, ALU.mult, ALU.add), [t, d, w_small], "dve_y")
            bank_free[bk] = d
            d = dve(lambda e, i=i, fin=fin: e.tensor_tensor(fin, fin, g1[:, sl, i, :], ALU.mult), [d, known(g1_ready[b])], "dve_y")
            d = dve(lambda e, i=i, fin=fin: e.tensor_tensor(x1[:, sl, i, :], x1[:, sl, i, :], fin, ALU.add), [d], "dve_y")
            yield 2.0
        stored = load(out[b].rearrange("(t p) d -> p t d", p=P), x1[:, sl, :, :], f"stored{sl}", [d])
        batch_free[sl] = stored
        final[sl] = stored
        arena_free[0] = [d, t, y_ok] + last_bc
        yield 2.0

    final, bc_stores = [None, None], []

    def run(g):
        for _ in g:
            pass

    def together(leader, *others):
        owed = [0.0] * len(others)
        for cost in leader:
            for j, (steps, share) in enumerate(others):
                owed[j] += share * cost
                while owed[j] > 0:
                    took = next(steps, None)
                    if took is None:
                        break
                    owed[j] -= took

    def alongside(a, b, share):
        owed = 0.0
        for cost in a:
            yield cost
            owed += share * cost
            while owed > 0:
                took = next(b, None)
                if took is None:
                    break
                owed -= took
                yield took
        yield from b

    def chain(*gens):
        for g in gens:
            yield from g

    def nothing():
        return iter(())

    w_ssm = None
    for dst, src in ((WinT_sb, WinT), (WxT_sb, WxT), (WoutT_sb, WoutT)):
        w_ssm = load(dst[:, :, :], src.rearrange("(c p) n -> p c n", p=P), "w_ssm", queue="act")
    w_ssm = load(WdtT_sb[:, :], WdtT, "w_ssm", queue="act")
    AT_free[0] = path_ok
    first = attention(0)
    for _ in range(FIRST_AHEAD):
        next(first)
    for part_ in range(NT // ROUTE_TILES):
        together(routing(part_), (first, ATTENTION_PER_ROUTING))
        scatter(part_)
    a0 = act(lambda e: e.activation(A_sb[:, :, :], A_sb[:, :, :], ACT.Exp), [w_small], "act_const")
    A_ok = dve(lambda e: e.tensor_scalar(A_sb[:, :, :], A_sb[:, :, :], -1.0, None, ALU.mult), [a0], "dve_const")
    run(first)
    second = attention(1)
    for _ in range(SECOND_AHEAD):
        next(second)
    slot_weights = chain(*(weights(part_) for part_ in range(NT // ROUTE_TILES)))
    together(experts(), (second, ATTENTION_PER_EXPERTS), (slot_weights, WEIGHTS_PER_EXPERTS))
    run(slot_weights)
    together(combine(0), (second, ATTENTION_PER_COMBINE))
    run(second)
    for b in range(NB):
        layer, tree = mamba(b), trees(b)
        following = combine(b + 1) if b + 1 < NB else nothing()
        next(tree)
        next(layer)
        next(layer)
        later = attention(b + 2) if b + 2 < NB else nothing()
        others = alongside(chain(tree, later), following, COMBINE_PER_OTHERS if b + 2 < NB else COMBINE_PER_TREES)
        together(layer, (others, OTHERS_PER_LAYER))
        run(others)

    block = ctx.enter_context(nc.Block())

    @block.sync
    def _(e):
        run_queue("sp", e)
        for sem, value in final + bc_stores:
            e.wait_ge(sems[sem], value)

    @block.scalar
    def _(e):
        run_queue("act", e)

    @block.vector
    def _(e):
        run_queue("dve", e)

    @block.gpsimd
    def _(e):
        run_queue("pool", e)

    @block.tensor
    def _(e):
        run_queue("pe", e)

    ctx.close()


def host_layout(d):
    f = np.float32
    chunk = lambda v: v.reshape(-1, P).T
    path, need = np.zeros((INNER, 2 * P), f), np.zeros((P, 2), f)
    for node in range(NODES):
        col = node if node < INNER else P + node - INNER
        v = node
        while v > 0:
            up = (v - 1) // 2
            path[up, col] = 1.0 if v == 2 * up + 2 else -1.0
            need[col % P, col // P] += v == 2 * up + 2
            v = up
    ffn_b = np.zeros((P, 2 * TREES), f)
    for r in range(TREES):
        ffn_b[:INNER, 2 * r] = d["L1_ffn_b_in"][r * NODES:r * NODES + INNER]
        ffn_b[:, 2 * r + 1] = d["L1_ffn_b_in"][r * NODES + INNER:(r + 1) * NODES]
    block = lambda v: v.reshape(CB, P, -1).transpose(1, 0, 2)
    chan = np.concatenate([block(d["L1_attn_conv_w"].reshape(DI, DCONV)), block(d["L1_attn_conv_b"]),
                           block(d["L1_attn_b_dt"]), block(d["L1_attn_D_param"])], axis=2)
    before = np.tril(np.ones((EG, EG), f), -1)
    return {
        "X": d["L0_attn_X"], "Wq": d["L0_attn_Wq"], "Wk": d["L0_attn_Wk"], "Wv": d["L0_attn_Wv"], "Wpost": d["L0_attn_Wpost"],
        "gateT": d["L0_ffn_gate_w"].T, "gate_bias": d["L0_ffn_gate_bias"], "w_gate": d["L0_ffn_w_gate"], "w_up": d["L0_ffn_w_up"],
        "w_down": d["L0_ffn_w_down"],
        "ln_gb": np.stack([chunk(d["L1_attn_ln_g"]), chunk(d["L1_attn_ln_b"])], axis=1),
        "WinT": d["L1_attn_W_in"].T, "WxT": d["L1_attn_W_x"].T, "WdtT": d["L1_attn_W_dt"].T, "WoutT": d["L1_attn_W_out"].T,
        "chan": chan, "A_log": block(d["L1_attn_A_log"]), "alpha": d["L1_attn_alpha"],
        "ffn_WinT": d["L1_ffn_W_in"].T, "ffn_b": ffn_b, "ffn_WoutT": d["L1_ffn_W_out"].T,
        "path": path, "need": need, "tri": np.triu(np.ones((P, P), f), 1), "glt": before.reshape(-1),
        "slot_base": (np.arange(EXPERTS) * CAP + 1).astype(f),
    }


def kernel(**inputs):
    import concourse.bacc as bacc
    from concourse.bass_utils import run_bass_kernel_spmd

    nc = bacc.Bacc("TRN2", target_bir_lowering=False, num_devices=1)
    arrays = {f"in_{n}": np.ascontiguousarray(a) for n, a in host_layout({k: np.asarray(v) for k, v in inputs.items()}).items()}
    aps = {n[3:]: nc.dram_tensor(n, a.shape, mybir.dt.from_np(a.dtype), kind="ExternalInput").ap() for n, a in arrays.items()}
    out = nc.dram_tensor("out_x", [NB, SEQ, DM], mybir.dt.float32, kind="ExternalOutput").ap()
    build_program(nc, out=out, **aps)
    result = run_bass_kernel_spmd(nc, [arrays], core_ids=[0])
    return result.results[0]["out_x"]
```
